# Optimizing a Trainium2 kernel written in Bass

```python
import numpy as np
import jax
import jax.numpy as jnp

def _softmax(x, axis=-1):
    return jax.nn.softmax(x, axis=axis)

def _gelu(x):
    return jax.nn.gelu(x, approximate=True)

def _silu(x):
    return jax.nn.silu(x)

def _sigmoid(x):
    return jax.nn.sigmoid(x)

def _layernorm(x, axis=-1, eps=1e-05):
    m = jnp.mean(x, axis=axis, keepdims=True)
    v = jnp.var(x, axis=axis, keepdims=True)
    return (x - m) / jnp.sqrt(v + eps)

def _scatter_add(tgt, idx, src, axis=0):
    return tgt.at[idx].add(src)

def _segment_sum(src, seg, n):
    return jax.ops.segment_sum(src, seg, n)
kernel_name = 'mk_decoder_preln_d2_seqx_r4_7573a1'

def setup_inputs(seed: int=0):
    np.random.seed(seed)
    _w = jnp.asarray

    def _rec_inputs():
        import jax
        import jax.numpy as jnp
        _rk = jax.random.key(seed)
        x = 7.22e-05 + 1 * jax.random.normal(jax.random.fold_in(_rk, 1), (32, 128, 256), jnp.float32)
        _lenS = 128 - jax.random.randint(jax.random.fold_in(_rk, 7), (32,), 0, max(1, 128 // 4) + 1, jnp.int32)
        _lenS2 = 128 - jax.random.randint(jax.random.fold_in(_rk, 8), (32,), 0, max(1, 128 // 4) + 1, jnp.int32)
        _ctx_1024P = jax.random.normal(jax.random.fold_in(_rk, 11), (32, 16, 256), jnp.float32)
        _ctx_1024c = jax.random.dirichlet(jax.random.fold_in(_rk, 511), 0.3 * jnp.ones((16,), jnp.float32), (32, 128))
        _ctx_1024t = jnp.einsum('bsk,bkd->bsd', _ctx_1024c, _ctx_1024P)
        _ctx_1024t = _ctx_1024t * jax.lax.rsqrt(jnp.mean(jnp.square(_ctx_1024t)) + 1e-12) * 0.953939
        ctx_1024 = 4.13588e-05 + 0.999923 * (_ctx_1024t + 0.3 * jax.random.normal(jax.random.fold_in(_rk, 611), (32, 128, 256), jnp.float32))
        return (x, ctx_1024)
    x, ctx_1024 = _rec_inputs()

    def _L0_attn_setup():
        import jax, jax.numpy as jnp
        import numpy as np
        D_MODEL, D_STATE, D_CONV = (256, 16, 4)
        B_, L_ = (4, 512)
        LN_EPS = 1e-05

        def _silu(v):
            return v * jax.nn.sigmoid(v)

        def _mamba_fwd(x, in_proj_w, in_proj_b, conv_w, conv_b, bc_w, bc_b, dt_w, dt_b, A_log, D, out_w, out_b, ln_g, ln_b):
            b, l, d = x.shape
            x_proj = x @ in_proj_w.T + in_proj_b
            x_ssm, x_gate = jnp.split(x_proj, 2, axis=-1)
            xc = lax.conv_general_dilated(x_ssm.transpose(0, 2, 1), conv_w, window_strides=(1,), padding=[(D_CONV - 1, 0)], feature_group_count=d, dimension_numbers=('NCH', 'OIH', 'NCH'))
            x_conv = _silu((xc + conv_b[None, :, None]).transpose(0, 2, 1))
            BC = x_conv @ bc_w.T + bc_b
            Bm, Cm = jnp.split(BC, 2, axis=-1)
            dt = jax.nn.softplus(x_conv @ dt_w.T + dt_b)
            A = -jnp.exp(A_log)

            def step(h, inp):
                xt, dtt, Bt, Ct = inp
                dA = jnp.exp(dtt[:, :, None] * A)
                dB = dtt[:, :, None] * Bt[:, None, :]
                h = h * dA + dB * xt[:, :, None]
                y = jnp.einsum('bdn,bn->bd', h, Ct) + xt * D
                return (h, y)
            h0 = jnp.zeros((b, d, D_STATE), x.dtype)
            xs = (x_conv.transpose(1, 0, 2), dt.transpose(1, 0, 2), Bm.transpose(1, 0, 2), Cm.transpose(1, 0, 2))
            _, ys = lax.scan(step, h0, xs)
            y = ys.transpose(1, 0, 2)
            y = y * _silu(x_gate)
            out = y @ out_w.T + out_b
            z = out + x
            mu = jnp.mean(z, axis=-1, keepdims=True)
            var = jnp.var(z, axis=-1, keepdims=True)
            return (z - mu) * jax.lax.rsqrt(var + LN_EPS) * ln_g + ln_b
        from jax import lax
        key = jax.random.key(seed)
        ks = jax.random.split(key, 16)
        s = 0.02
        return {'x': jax.random.normal(ks[0], (B_, L_, D_MODEL), jnp.float32), 'in_proj_w': jax.random.normal(ks[1], (2 * D_MODEL, D_MODEL), jnp.float32) * s, 'in_proj_b': jnp.zeros((2 * D_MODEL,), jnp.float32), 'conv_w': jax.random.normal(ks[2], (D_MODEL, 1, D_CONV), jnp.float32) * s, 'conv_b': jnp.zeros((D_MODEL,), jnp.float32), 'bc_w': jax.random.normal(ks[3], (2 * D_STATE, D_MODEL), jnp.float32) * s, 'bc_b': jnp.zeros((2 * D_STATE,), jnp.float32), 'dt_w': jax.random.normal(ks[4], (D_MODEL, D_MODEL), jnp.float32) * s, 'dt_b': jnp.zeros((D_MODEL,), jnp.float32), 'A_log': jax.random.normal(ks[5], (D_MODEL, D_STATE), jnp.float32), 'D': jnp.ones((D_MODEL,), jnp.float32), 'out_w': jax.random.normal(ks[6], (D_MODEL, D_MODEL), jnp.float32) * s, 'out_b': jnp.zeros((D_MODEL,), jnp.float32), 'ln_g': jnp.ones((D_MODEL,), jnp.float32), 'ln_b': jnp.zeros((D_MODEL,), jnp.float32)}
    _L0_attn_all = _L0_attn_setup()
    _L0_attn_in = {k: v for k, v in _L0_attn_all.items() if k in ('in_proj_w', 'in_proj_b', 'conv_w', 'conv_b', 'bc_w', 'bc_b', 'dt_w', 'dt_b', 'A_log', 'D', 'out_w', 'out_b', 'ln_g', 'ln_b')}
    del _L0_attn_all

    def _L0_xattn_setup():
        import jax, jax.numpy as jnp
        import numpy as np
        BETA = 256
        NUM_HEADS = 16
        NORM = (BETA // NUM_HEADS) ** (-0.5)
        key = jax.random.key(seed)
        ks = jax.random.split(key, 6)
        B, N = (4, 512)
        D_in_q = D_in_k = D_in_v = 256
        D_out_k = D_out_v = 256
        q = jax.random.normal(ks[0], (B, N, D_in_q), dtype=jnp.float32)
        k = jax.random.normal(ks[1], (B, N, D_in_k), dtype=jnp.float32)
        v = jax.random.normal(ks[2], (B, N, D_in_v), dtype=jnp.float32)
        Wq = jax.random.normal(ks[3], (D_out_k, D_in_q), dtype=jnp.float32) * D_in_q ** (-0.5)
        Wk = jax.random.normal(ks[4], (D_out_k, D_in_k), dtype=jnp.float32) * D_in_k ** (-0.5)
        Wv = jax.random.normal(ks[5], (D_out_v, D_in_v), dtype=jnp.float32) * D_in_v ** (-0.5)
        return {'q': q, 'k': k, 'v': v, 'Wq': Wq, 'Wk': Wk, 'Wv': Wv}
    _L0_xattn_all = _L0_xattn_setup()
    _L0_xattn_in = {k: v for k, v in _L0_xattn_all.items() if k in ('Wq', 'Wk', 'Wv')}
    del _L0_xattn_all

    def _L0_ffn_setup():
        import jax, jax.numpy as jnp
        import numpy as np
        D_MODEL = 256
        N_HEADS = 16
        D_HEAD = D_MODEL // N_HEADS
        N_EXPERTS = 8
        TOP_K = 2
        D_FF = 512
        EPS = 1e-06

        def rmsnorm(x, w):
            return x * jax.lax.rsqrt(jnp.mean(x * x, axis=-1, keepdims=True) + EPS) * w

        def swiglu(x, w_gate, w_up, w_down):
            return jax.nn.silu(x @ w_gate) * (x @ w_up) @ w_down
        key = jax.random.key(seed)
        ks = jax.random.split(key, 16)
        s = 0.02
        B, S = (2, 512)
        return {'X': jax.random.normal(ks[0], (B, S, D_MODEL), dtype=jnp.float32), 'norm1_w': jnp.ones((D_MODEL,), jnp.float32), 'norm2_w': jnp.ones((D_MODEL,), jnp.float32), 'wq': jax.random.normal(ks[1], (D_MODEL, D_MODEL), jnp.float32) * s, 'wk': jax.random.normal(ks[2], (D_MODEL, D_MODEL), jnp.float32) * s, 'wv': jax.random.normal(ks[3], (D_MODEL, D_MODEL), jnp.float32) * s, 'wo': jax.random.normal(ks[4], (D_MODEL, D_MODEL), jnp.float32) * s, 'router_w': jax.random.normal(ks[5], (D_MODEL, N_EXPERTS), jnp.float32) * s, 'sh_gate': jax.random.normal(ks[6], (D_MODEL, D_FF), jnp.float32) * s, 'sh_up': jax.random.normal(ks[7], (D_MODEL, D_FF), jnp.float32) * s, 'sh_down': jax.random.normal(ks[8], (D_FF, D_MODEL), jnp.float32) * s, 'e_gate': jax.random.normal(ks[9], (N_EXPERTS, D_MODEL, D_FF), jnp.float32) * s, 'e_up': jax.random.normal(ks[10], (N_EXPERTS, D_MODEL, D_FF), jnp.float32) * s, 'e_down': jax.random.normal(ks[11], (N_EXPERTS, D_FF, D_MODEL), jnp.float32) * s}
    _L0_ffn_all = _L0_ffn_setup()
    _L0_ffn_in = {k: v for k, v in _L0_ffn_all.items() if k in ('norm1_w', 'norm2_w', 'wq', 'wk', 'wv', 'wo', 'router_w', 'sh_gate', 'sh_up', 'sh_down', 'e_gate', 'e_up', 'e_down')}
    del _L0_ffn_all

    def _L1_attn_setup():
        import jax, jax.numpy as jnp
        import numpy as np
        B, T, D, H = (64, 128, 256, 256)
        key = jax.random.key(seed)
        k1, k2, k3 = jax.random.split(key, 3)
        scale = 0.02
        return {'x': jax.random.normal(k1, (B, T, D), dtype=jnp.float32), 'Wi': jax.random.normal(k2, (H, D), dtype=jnp.float32) * scale, 'bi': jnp.zeros((H,), dtype=jnp.float32), 'Wh': jax.random.normal(k3, (H, H), dtype=jnp.float32) * scale, 'bh': jnp.zeros((H,), dtype=jnp.float32)}
    _L1_attn_all = _L1_attn_setup()
    _L1_attn_in = {k: v for k, v in _L1_attn_all.items() if k in ('Wi', 'bi', 'Wh', 'bh')}
    del _L1_attn_all

    def _L1_xattn_setup():
        import jax, jax.numpy as jnp
        import numpy as np
        D, H = (256, 16)
        DH = D // H

        def _split_heads(z):
            b, t, _ = z.shape
            return z.reshape(b, t, H, DH).transpose(0, 2, 1, 3)
        key = jax.random.key(seed)
        ks = jax.random.split(key, 11)
        b, t, ta = (2, 512, 375)
        s = 1.0 / np.sqrt(D)
        return {'x': jax.random.normal(ks[0], (b, t, D), dtype=jnp.float32), 'xa': jax.random.normal(ks[1], (b, ta, D), dtype=jnp.float32), 'Wqkv': jax.random.normal(ks[2], (D, 3 * D), dtype=jnp.float32) * s, 'bqkv': jax.random.normal(ks[3], (3 * D,), dtype=jnp.float32) * 0.01, 'Wqkv_aux': jax.random.normal(ks[4], (D, 3 * D), dtype=jnp.float32) * s, 'bqkv_aux': jax.random.normal(ks[5], (3 * D,), dtype=jnp.float32) * 0.01, 'Wo': jax.random.normal(ks[6], (D, D), dtype=jnp.float32) * s, 'bo': jax.random.normal(ks[7], (D,), dtype=jnp.float32) * 0.01, 'g': jnp.zeros((H,), dtype=jnp.float32)}
    _L1_xattn_all = _L1_xattn_setup()
    _L1_xattn_in = {k: v for k, v in _L1_xattn_all.items() if k in ('Wqkv', 'bqkv', 'Wqkv_aux', 'bqkv_aux', 'Wo', 'bo', 'g')}
    del _L1_xattn_all

    def _L1_ffn_setup():
        import jax, jax.numpy as jnp
        import numpy as np
        DIM = 256
        NUM_EXPERTS = 8
        ACTIVE_EXPERTS = 2
        EXPERT_DIM = 512
        key = jax.random.key(seed)
        k1, k2, k3, k4 = jax.random.split(key, 4)
        x = jax.random.normal(k1, (1, 512, DIM), dtype=jnp.float32)
        gate_w = jax.random.normal(k2, (NUM_EXPERTS, DIM), dtype=jnp.float32) * 0.02
        balance_bias = jnp.zeros((NUM_EXPERTS,), dtype=jnp.float32)
        w1 = jax.random.normal(k3, (NUM_EXPERTS, EXPERT_DIM, DIM), dtype=jnp.float32) * 0.02
        w2 = jax.random.normal(k4, (NUM_EXPERTS, DIM, EXPERT_DIM), dtype=jnp.float32) * 0.02
        return {'x': x, 'gate_w': gate_w, 'balance_bias': balance_bias, 'w1': w1, 'w2': w2}
    _L1_ffn_all = _L1_ffn_setup()
    _L1_ffn_in = {k: v for k, v in _L1_ffn_all.items() if k in ('gate_w', 'balance_bias', 'w1', 'w2')}
    del _L1_ffn_all
    return {'x': x, 'ctx_1024': ctx_1024, 'L0_attn_in_proj_w': _L0_attn_in['in_proj_w'], 'L0_attn_in_proj_b': _L0_attn_in['in_proj_b'], 'L0_attn_conv_w': _L0_attn_in['conv_w'], 'L0_attn_conv_b': _L0_attn_in['conv_b'], 'L0_attn_bc_w': _L0_attn_in['bc_w'], 'L0_attn_bc_b': _L0_attn_in['bc_b'], 'L0_attn_dt_w': _L0_attn_in['dt_w'], 'L0_attn_dt_b': _L0_attn_in['dt_b'], 'L0_attn_A_log': _L0_attn_in['A_log'], 'L0_attn_D': _L0_attn_in['D'], 'L0_attn_out_w': _L0_attn_in['out_w'], 'L0_attn_out_b': _L0_attn_in['out_b'], 'L0_attn_ln_g': _L0_attn_in['ln_g'], 'L0_attn_ln_b': _L0_attn_in['ln_b'], 'L0_xattn_Wq': _L0_xattn_in['Wq'], 'L0_xattn_Wk': _L0_xattn_in['Wk'], 'L0_xattn_Wv': _L0_xattn_in['Wv'], 'L0_ffn_norm1_w': _L0_ffn_in['norm1_w'], 'L0_ffn_norm2_w': _L0_ffn_in['norm2_w'], 'L0_ffn_wq': _L0_ffn_in['wq'], 'L0_ffn_wk': _L0_ffn_in['wk'], 'L0_ffn_wv': _L0_ffn_in['wv'], 'L0_ffn_wo': _L0_ffn_in['wo'], 'L0_ffn_router_w': _L0_ffn_in['router_w'], 'L0_ffn_sh_gate': _L0_ffn_in['sh_gate'], 'L0_ffn_sh_up': _L0_ffn_in['sh_up'], 'L0_ffn_sh_down': _L0_ffn_in['sh_down'], 'L0_ffn_e_gate': _L0_ffn_in['e_gate'], 'L0_ffn_e_up': _L0_ffn_in['e_up'], 'L0_ffn_e_down': _L0_ffn_in['e_down'], 'L1_attn_Wi': _L1_attn_in['Wi'], 'L1_attn_bi': _L1_attn_in['bi'], 'L1_attn_Wh': _L1_attn_in['Wh'], 'L1_attn_bh': _L1_attn_in['bh'], 'L1_xattn_Wqkv': _L1_xattn_in['Wqkv'], 'L1_xattn_bqkv': _L1_xattn_in['bqkv'], 'L1_xattn_Wqkv_aux': _L1_xattn_in['Wqkv_aux'], 'L1_xattn_bqkv_aux': _L1_xattn_in['bqkv_aux'], 'L1_xattn_Wo': _L1_xattn_in['Wo'], 'L1_xattn_bo': _L1_xattn_in['bo'], 'L1_xattn_g': _L1_xattn_in['g'], 'L1_ffn_gate_w': _L1_ffn_in['gate_w'], 'L1_ffn_balance_bias': _L1_ffn_in['balance_bias'], 'L1_ffn_w1': _L1_ffn_in['w1'], 'L1_ffn_w2': _L1_ffn_in['w2']}

def reference(x, ctx_1024, L0_attn_in_proj_w, L0_attn_in_proj_b, L0_attn_conv_w, L0_attn_conv_b, L0_attn_bc_w, L0_attn_bc_b, L0_attn_dt_w, L0_attn_dt_b, L0_attn_A_log, L0_attn_D, L0_attn_out_w, L0_attn_out_b, L0_attn_ln_g, L0_attn_ln_b, L0_xattn_Wq, L0_xattn_Wk, L0_xattn_Wv, L0_ffn_norm1_w, L0_ffn_norm2_w, L0_ffn_wq, L0_ffn_wk, L0_ffn_wv, L0_ffn_wo, L0_ffn_router_w, L0_ffn_sh_gate, L0_ffn_sh_up, L0_ffn_sh_down, L0_ffn_e_gate, L0_ffn_e_up, L0_ffn_e_down, L1_attn_Wi, L1_attn_bi, L1_attn_Wh, L1_attn_bh, L1_xattn_Wqkv, L1_xattn_bqkv, L1_xattn_Wqkv_aux, L1_xattn_bqkv_aux, L1_xattn_Wo, L1_xattn_bo, L1_xattn_g, L1_ffn_gate_w, L1_ffn_balance_bias, L1_ffn_w1, L1_ffn_w2):
    import jax
    import jax.numpy as jnp

    def _L0_attn_ref(x, in_proj_w, in_proj_b, conv_w, conv_b, bc_w, bc_b, dt_w, dt_b, A_log, D, out_w, out_b, ln_g, ln_b):
        import jax, jax.numpy as jnp
        import numpy as np
        D_MODEL, D_STATE, D_CONV = (256, 16, 4)
        B_, L_ = (4, 512)
        LN_EPS = 1e-05

        def _silu(v):
            return v * jax.nn.sigmoid(v)

        def _mamba_fwd(x, in_proj_w, in_proj_b, conv_w, conv_b, bc_w, bc_b, dt_w, dt_b, A_log, D, out_w, out_b, ln_g, ln_b):
            b, l, d = x.shape
            x_proj = x @ in_proj_w.T + in_proj_b
            x_ssm, x_gate = jnp.split(x_proj, 2, axis=-1)
            xc = lax.conv_general_dilated(x_ssm.transpose(0, 2, 1), conv_w, window_strides=(1,), padding=[(D_CONV - 1, 0)], feature_group_count=d, dimension_numbers=('NCH', 'OIH', 'NCH'))
            x_conv = _silu((xc + conv_b[None, :, None]).transpose(0, 2, 1))
            BC = x_conv @ bc_w.T + bc_b
            Bm, Cm = jnp.split(BC, 2, axis=-1)
            dt = jax.nn.softplus(x_conv @ dt_w.T + dt_b)
            A = -jnp.exp(A_log)

            def step(h, inp):
                xt, dtt, Bt, Ct = inp
                dA = jnp.exp(dtt[:, :, None] * A)
                dB = dtt[:, :, None] * Bt[:, None, :]
                h = h * dA + dB * xt[:, :, None]
                y = jnp.einsum('bdn,bn->bd', h, Ct) + xt * D
                return (h, y)
            h0 = jnp.zeros((b, d, D_STATE), x.dtype)
            xs = (x_conv.transpose(1, 0, 2), dt.transpose(1, 0, 2), Bm.transpose(1, 0, 2), Cm.transpose(1, 0, 2))
            _, ys = lax.scan(step, h0, xs)
            y = ys.transpose(1, 0, 2)
            y = y * _silu(x_gate)
            out = y @ out_w.T + out_b
            z = out + x
            mu = jnp.mean(z, axis=-1, keepdims=True)
            var = jnp.var(z, axis=-1, keepdims=True)
            return (z - mu) * jax.lax.rsqrt(var + LN_EPS) * ln_g + ln_b
        from jax import lax
        return _mamba_fwd(x, in_proj_w, in_proj_b, conv_w, conv_b, bc_w, bc_b, dt_w, dt_b, A_log, D, out_w, out_b, ln_g, ln_b)

    def _L0_xattn_ref(q, k, v, Wq, Wk, Wv):
        import jax, jax.numpy as jnp
        import numpy as np
        BETA = 256
        NUM_HEADS = 16
        NORM = (BETA // NUM_HEADS) ** (-0.5)
        qp = jax.nn.relu(jnp.einsum('bnd,od->bno', q, Wq))
        kp = jax.nn.relu(jnp.einsum('bnd,od->bno', k, Wk))
        vp = jax.nn.relu(jnp.einsum('bnd,od->bno', v, Wv))
        B, N, D = qp.shape
        dh = D // NUM_HEADS
        qh = qp.reshape(B, N, NUM_HEADS, dh)
        kh = kp.reshape(B, N, NUM_HEADS, dh)
        vh = vp.reshape(B, N, NUM_HEADS, vp.shape[-1] // NUM_HEADS)
        E = NORM * jnp.einsum('bqhd,bkhd->bhqk', qh, kh)
        A = jax.nn.softmax(E, axis=-1)
        out = jnp.einsum('bhqk,bkhd->bqhd', A, vh)
        return out.reshape(B, N, -1)

    def _L0_ffn_ref(X, norm1_w, norm2_w, wq, wk, wv, wo, router_w, sh_gate, sh_up, sh_down, e_gate, e_up, e_down):
        import jax, jax.numpy as jnp
        import numpy as np
        D_MODEL = 256
        N_HEADS = 16
        D_HEAD = D_MODEL // N_HEADS
        N_EXPERTS = 8
        TOP_K = 2
        D_FF = 512
        EPS = 1e-06

        def rmsnorm(x, w):
            return x * jax.lax.rsqrt(jnp.mean(x * x, axis=-1, keepdims=True) + EPS) * w

        def swiglu(x, w_gate, w_up, w_down):
            return jax.nn.silu(x @ w_gate) * (x @ w_up) @ w_down
        B, S, d = X.shape
        scale = 1.0 / jnp.sqrt(jnp.asarray(D_HEAD, X.dtype))
        h = rmsnorm(X, norm1_w)
        q = (h @ wq).reshape(B, S, N_HEADS, D_HEAD)
        k = (h @ wk).reshape(B, S, N_HEADS, D_HEAD)
        v = (h @ wv).reshape(B, S, N_HEADS, D_HEAD)
        scores = jnp.einsum('bshd,bthd->bhst', q, k) * scale
        attn = jax.nn.softmax(scores, axis=-1)
        ctx = jnp.einsum('bhst,bthd->bshd', attn, v).reshape(B, S, d)
        X = X + ctx @ wo
        h2 = rmsnorm(X, norm2_w).reshape(B * S, d)
        logits = h2 @ router_w
        probs = jax.nn.softmax(logits, axis=-1)
        topw, topi = jax.lax.top_k(probs, TOP_K)
        topw = jax.nn.softmax(topw, axis=-1)
        combine = jnp.sum(jax.nn.one_hot(topi, N_EXPERTS, dtype=h2.dtype) * topw[..., None], axis=1)
        shared = swiglu(h2, sh_gate, sh_up, sh_down)
        gate = jnp.einsum('td,edf->etf', h2, e_gate)
        up = jnp.einsum('td,edf->etf', h2, e_up)
        eout = jnp.einsum('etf,efd->etd', jax.nn.silu(gate) * up, e_down)
        spec = jnp.einsum('etd,te->td', eout, combine)
        moe_out = (shared + spec).reshape(B, S, d)
        return X + moe_out

    def _L1_attn_ref(x, Wi, bi, Wh, bh):
        import jax, jax.numpy as jnp
        import numpy as np
        B, T, D, H = (64, 128, 256, 256)
        xi = jnp.einsum('btd,hd->bth', x, Wi) + bi

        def step(h, xt):
            h_new = jnp.tanh(xt + h @ Wh.T + bh)
            return (h_new, h_new)
        h0 = jnp.zeros((x.shape[0], Wh.shape[0]), dtype=x.dtype)
        _, hs = jax.lax.scan(step, h0, jnp.swapaxes(xi, 0, 1))
        return jnp.swapaxes(hs, 0, 1)

    def _L1_xattn_ref(x, xa, Wqkv, bqkv, Wqkv_aux, bqkv_aux, Wo, bo, g):
        import jax, jax.numpy as jnp
        import numpy as np
        D, H = (256, 16)
        DH = D // H

        def _split_heads(z):
            b, t, _ = z.shape
            return z.reshape(b, t, H, DH).transpose(0, 2, 1, 3)
        qkv = x @ Wqkv + bqkv
        qkv_a = xa @ Wqkv_aux + bqkv_aux
        q, k, v = (_split_heads(c) for c in jnp.split(qkv, 3, axis=-1))
        qa, ka, va = (_split_heads(c) for c in jnp.split(qkv_a, 3, axis=-1))
        scale = 1.0 / jnp.sqrt(jnp.float32(DH))
        dots = jnp.einsum('bhqd,bhkd->bhqk', q, k) * scale
        dots_aux = jnp.einsum('bhqd,bhkd->bhqk', q, ka) * scale
        p = jax.nn.softmax(dots, axis=-1)
        pa = jax.nn.softmax(dots_aux, axis=-1)
        h_main = jnp.einsum('bhqk,bhkd->bhqd', p, v)
        h_aux = jnp.einsum('bhqk,bhkd->bhqd', pa, va)
        gate = jax.nn.sigmoid(g).reshape(1, H, 1, 1)
        out = h_main * (1.0 - gate) + h_aux * gate
        b, _, t, _ = out.shape
        out = out.transpose(0, 2, 1, 3).reshape(b, t, H * DH)
        return out @ Wo + bo

    def _L1_ffn_ref(x, gate_w, balance_bias, w1, w2):
        import jax, jax.numpy as jnp
        import numpy as np
        DIM = 256
        NUM_EXPERTS = 8
        ACTIVE_EXPERTS = 2
        EXPERT_DIM = 512
        B, S, D = x.shape
        T = B * S
        xf = x.reshape(T, D)
        gate_logits = jnp.einsum('td,ed->te', xf, gate_w)
        gate_scores = jax.nn.sigmoid(gate_logits + balance_bias)
        topk_scores, topk_idx = jax.lax.top_k(gate_scores, ACTIVE_EXPERTS)
        topk_scores = topk_scores / (topk_scores.sum(axis=-1, keepdims=True) + 1e-06)
        comb = jnp.zeros((T, NUM_EXPERTS), dtype=x.dtype)
        comb = comb.at[jnp.arange(T)[:, None], topk_idx].add(topk_scores)
        h = jax.nn.silu(jnp.einsum('td,ehd->teh', xf, w1))
        expert_out = jnp.einsum('teh,edh->ted', h, w2)
        out = jnp.einsum('te,ted->td', comb, expert_out)
        return out.reshape(B, S, D)
    x = x + _L0_attn_ref(_layernorm(x, axis=-1), L0_attn_in_proj_w, L0_attn_in_proj_b, L0_attn_conv_w, L0_attn_conv_b, L0_attn_bc_w, L0_attn_bc_b, L0_attn_dt_w, L0_attn_dt_b, L0_attn_A_log, L0_attn_D, L0_attn_out_w, L0_attn_out_b, L0_attn_ln_g, L0_attn_ln_b)
    x = x + _L0_xattn_ref(_layernorm(x, axis=-1), ctx_1024, ctx_1024, L0_xattn_Wq, L0_xattn_Wk, L0_xattn_Wv)
    x = x + _L0_ffn_ref(_layernorm(x, axis=-1), L0_ffn_norm1_w, L0_ffn_norm2_w, L0_ffn_wq, L0_ffn_wk, L0_ffn_wv, L0_ffn_wo, L0_ffn_router_w, L0_ffn_sh_gate, L0_ffn_sh_up, L0_ffn_sh_down, L0_ffn_e_gate, L0_ffn_e_up, L0_ffn_e_down)
    x = x + _L1_attn_ref(_layernorm(x, axis=-1), L1_attn_Wi, L1_attn_bi, L1_attn_Wh, L1_attn_bh)
    x = x + _L1_xattn_ref(_layernorm(x, axis=-1), ctx_1024, L1_xattn_Wqkv, L1_xattn_bqkv, L1_xattn_Wqkv_aux, L1_xattn_bqkv_aux, L1_xattn_Wo, L1_xattn_bo, L1_xattn_g)
    x = x + _L1_ffn_ref(_layernorm(x, axis=-1), L1_ffn_gate_w, L1_ffn_balance_bias, L1_ffn_w1, L1_ffn_w2)
    return x

_drawn_inputs = setup_inputs


def setup_inputs(seed=0):
    import zlib

    import numpy as np

    out = dict(_drawn_inputs(seed))
    spreads = {'L0_attn_in_proj_b': (0.0, 0.8),
     'L0_attn_conv_b': (0.0, 0.8),
     'L0_attn_bc_b': (0.0, 0.8),
     'L0_attn_dt_b': (0.0, 0.8),
     'L0_attn_D': (1.0, 0.6),
     'L0_attn_out_b': (0.0, 0.593),
     'L0_attn_ln_g': (1.0, 0.2),
     'L0_attn_ln_b': (0.0, 0.1),
     'L0_ffn_norm1_w': (1.0, 0.6),
     'L0_ffn_norm2_w': (1.0, 0.6),
     'L1_attn_bi': (0.0, 2.0),
     'L1_attn_bh': (0.0, 0.8),
     'L1_xattn_g': (0.0, 2.0),
     'L1_ffn_balance_bias': (0.0, 2.0)}
    factors = {'L0_attn_in_proj_w': 8.0,
     'L0_attn_conv_w': 8.0,
     'L0_attn_bc_w': 8.0,
     'L0_attn_dt_w': 8.0,
     'L0_attn_A_log': 8.0,
     'L0_attn_out_w': 8.0,
     'L0_ffn_wq': 8.0,
     'L0_ffn_wk': 8.0,
     'L0_ffn_wv': 8.0,
     'L0_ffn_wo': 8.0,
     'L0_ffn_router_w': 8.0,
     'L0_ffn_sh_gate': 6.216,
     'L0_ffn_sh_up': 6.147,
     'L0_ffn_sh_down': 6.146,
     'L0_ffn_e_gate': 8.0,
     'L0_ffn_e_up': 8.0,
     'L0_ffn_e_down': 8.0,
     'L1_xattn_bqkv': 64.0,
     'L1_xattn_bqkv_aux': 64.0,
     'L1_xattn_bo': 200.0,
     'L1_ffn_gate_w': 16.159,
     'L1_ffn_w1': 11.492,
     'L1_ffn_w2': 10.692,
     'L1_attn_Wi': 7.61,
     'L1_attn_Wh': 8.0,
     'L1_xattn_Wqkv': 8.0,
     'L1_xattn_Wqkv_aux': 6.663,
     'L1_xattn_Wo': 6.207}
    for name, (base, spread) in spreads.items():
        noise = np.random.default_rng([zlib.crc32(name.encode()), seed]).standard_normal(out[name].shape)
        drawn = base * np.exp(spread * noise) if base else spread * noise
        out[name] = jnp.asarray(drawn.astype(out[name].dtype))
    for name, factor in factors.items():
        out[name] = (out[name] * factor).astype(out[name].dtype)
    return out
```

```python
import numpy as np

import concourse.bass as bass
from concourse import mybir
from contextlib import ExitStack

F32 = mybir.dt.float32
BF16 = mybir.dt.bfloat16
U32 = mybir.dt.uint32
I32 = mybir.dt.int32
ALU = mybir.AluOpType
ACT = mybir.ActivationFunctionType
AX = mybir.AxisListType


def after(eng, sem, count):
    if not isinstance(count, int) or count > 0:
        eng.wait_ge(sem, count)


def weave(main, side):
    due = next(side, None)
    for step in main:
        while due is not None and due <= step:
            due = next(side, None)
    while due is not None:
        due = next(side, None)


def alone(side):
    for _ in side:
        pass


def merged(*sides):
    heads = [next(s, None) for s in sides]
    while any(h is not None for h in heads):
        n = min((h, n) for n, h in enumerate(heads) if h is not None)[1]
        yield heads[n]
        heads[n] = next(sides[n], None)


class Chain:

    def __init__(self, eng, sem, per, turn):
        self.eng, self.sem, self.per, self.turn, self.k = eng, sem, per, turn, 0

    def __call__(self, step):
        self.k += 1
        assert self.k <= self.per
        step.then_inc(self.sem, 1)
        self.eng.wait_ge(self.sem, self.turn * self.per + self.k)

    def turn_over(self):
        assert self.k == self.per, (self.k, self.per)


class Stage:

    def __init__(self, nc, numbers):
        self.nc, self.stack, self.numbers, self.left = nc, ExitStack(), numbers, iter(numbers)

    def take(self, name, shape, dtype=F32):
        return self.stack.enter_context(self.nc.sbuf_tensor(name, shape, dtype))

    def sem(self, name):
        return self.stack.enter_context(self.nc.semaphore(name, num=next(self.left)))

    def end(self):
        self.stack.close()


def flat(a):
    return a.rearrange("p a b -> p (a b)")


EPS, TINY = 1e-5, 1e-30
D, L, KD, NS = 256, 128, 2, 16
GS = 4
GT = GS * L
STAGES, SET = 7, 60


NH, DH = 16, 16
RMS_EPS = 1e-6


def heads(a):
    return a.rearrange("p (h d) -> p h d", h=NH)


def seqs(a):
    return a.rearrange("p (s t) -> p s t", s=GS)


def decoder_kernel(nc, ins, out):
    NG = ins["x"].shape[0] // GS
    ctx = ExitStack()

    def sem(name):
        return ctx.enter_context(nc.semaphore(name))

    def keep(name, shape, dtype=F32):
        return ctx.enter_context(nc.sbuf_tensor(name, shape, dtype))

    X = keep("X", [128, NG, GS, D])
    ident = keep("ident", [128, 128])
    neg_half, eps = keep("neg_half", [128, 16]), keep("eps", [128, 16])
    rms_eps, minus_one = keep("rms_eps", [128, 16]), keep("minus_one", [128, 16])
    PS = ctx.enter_context(nc.psum_tensor("PS", [128, 8, 512], F32))
    x_first, x_rest = [sem("x_first0"), sem("x_first1")], sem("x_rest")
    setup, stored = sem("setup"), sem("stored")
    cleared = sem("cleared")
    passed = [sem(f"passed{n}") for n in range(STAGES)]
    own = passed[-1].num + 1
    sem_set = [range(own, own + SET), range(own + SET, own + 2 * SET)]

    mamba_mem = Stage(nc, sem_set[0])
    m_w_sb = mamba_mem.take("m_w", [128, 2240])
    w_in = m_w_sb[:, 0:1024].rearrange("p (k o) -> p k o", k=KD)
    w_dt = m_w_sb[:, 1024:1536].rearrange("p (k o) -> p k o", k=KD)
    w_out = m_w_sb[:, 1536:2048].rearrange("p (k o) -> p k o", k=KD)
    w_bc = m_w_sb[:, 2048:2240].rearrange("p (k o) -> p k o", k=KD)
    m_v_sb = mamba_mem.take("m_v", [128, 50])
    b_in, cw, cb = m_v_sb[:, 0:4], m_v_sb[:, 4:12], m_v_sb[:, 12:14]
    b_dt, a_log, d_skip = m_v_sb[:, 14:16], m_v_sb[:, 16:48], m_v_sb[:, 48:50]
    b_bc = mamba_mem.take("b_bc", [96, 1])
    m_rows = mamba_mem.take("m_rows", [128, 3, D])
    selector = mamba_mem.take("selector", [96, 2 * NS, 128], BF16)
    decay_rate = mamba_mem.take("decay_rate", [128, KD * NS])
    half_v = mamba_mem.take("half_v", [128, 14])
    hb_in, hcw, hcb = half_v[:, 0:4], half_v[:, 4:12], half_v[:, 12:14]

    RD, RU, RC = 4, 4, 4
    xn = mamba_mem.take("xn", [128, 2, GS, D])
    xnb = mamba_mem.take("xnb", [128, 2, GS, D])
    xnT = mamba_mem.take("xnT", [128, 2, KD, GT])
    xpad = mamba_mem.take("xpad", [128, KD, GS, L + 3])
    half_conv = mamba_mem.take("half_conv", [128, KD, GS, L])
    conv_tanh = mamba_mem.take("conv_tanh", [128, KD * GT])
    xconv = mamba_mem.take("xconv", [128, 2, KD, GT])
    half_gate = mamba_mem.take("half_gate", [128, KD, GT])
    gate_tanh = mamba_mem.take("gate_tanh", [128, KD, GT])
    gate = mamba_mem.take("gate", [128, 2, KD * GT])
    bc96 = mamba_mem.take("bc96", [96, GT])
    bc_rest = mamba_mem.take("bc_rest", [64, GT])
    bc16 = mamba_mem.take("bc16", [96, 2, GT], BF16)
    dt_pre = mamba_mem.take("dt_pre", [128, KD * GT])
    dt_e = mamba_mem.take("dt_e", [128, KD * GT])
    dt_u = mamba_mem.take("dt_u", [128, KD * GT])
    dt_l = mamba_mem.take("dt_l", [128, KD * GT])
    dt_c = mamba_mem.take("dt_c", [128, KD * GT])
    dt = mamba_mem.take("dt", [128, 2, KD, GT])
    dtx = mamba_mem.take("dtx", [128, 2, KD, GT])
    b_rep = mamba_mem.take("b_rep", [128, 2, GT])
    decay = mamba_mem.take("decay", [128, RD, GS, L])
    u_in = mamba_mem.take("u_in", [128, RU, GT])
    state = mamba_mem.take("state", [128, 2, GT])
    scaled = mamba_mem.take("scaled", [128, RC, GT])
    skip_w = mamba_mem.take("skip_w", [128, KD, 128])
    bc_mid = mamba_mem.take("bc_mid", [32, GT])
    y_gated = mamba_mem.take("y_gated", [128, KD, GT])
    z_row = mamba_mem.take("z_row", [128, GS, D])
    z_norm = mamba_mem.take("z_norm", [128, GS, D])
    spare = mamba_mem.take("spare", [128, 1])
    stat = mamba_mem.take("stat", [128, 2, GS, 6])
    mv = mamba_mem.take("mv", [128, 2, GS, 2])
    rst = mamba_mem.take("rst", [128, 2, 4, GS])

    FB, BB, CB, YB = PS[:, 0:2], PS[:, 2:4], PS[:, 4:6], PS[:, 6:8]
    m_loaded, m_prep, m_edge = mamba_mem.sem("m_loaded"), mamba_mem.sem("m_prep"), mamba_mem.sem("m_edge")
    m_half, m_skip = mamba_mem.sem("m_half"), mamba_mem.sem("m_skip")
    m_vec, m_vec3, m_pool = mamba_mem.sem("m_vec"), mamba_mem.sem("m_vec3"), mamba_mem.sem("m_pool")
    m_vec2, m_pool2 = mamba_mem.sem("m_vec2"), mamba_mem.sem("m_pool2")
    m_mv, m_nb, m_xn, m_tr, m_fev1, m_fev2, m_xnb = map(
        mamba_mem.sem, ("m_mv", "m_nb", "m_xn", "m_tr", "m_fev1", "m_fev2", "m_xnb"))
    m_ip, m_ipg, m_gate, m_conv, m_th, m_xc, m_bcp, m_bcs, m_br = map(
        mamba_mem.sem, ("m_ip", "m_ipg", "m_gate", "m_conv", "m_th", "m_xc", "m_bcp", "m_bcs", "m_br"))
    m_dtp, m_e, m_u1, m_ln, m_q, m_dt, m_dtx = map(
        mamba_mem.sem, ("m_dtp", "m_e", "m_u1", "m_ln", "m_q", "m_dt", "m_dtx"))
    m_bb, m_cb, m_brep, m_da, m_u, m_h, m_hc, m_y = map(
        mamba_mem.sem, ("m_bb", "m_cb", "m_brep", "m_da", "m_u", "m_h", "m_hc", "m_y"))
    m_abs, m_yg, m_op, m_z, m_mv2, m_nb2, m_zn, m_zb, m_x = map(
        mamba_mem.sem, ("m_abs", "m_yg", "m_op", "m_z", "m_mv2", "m_nb2", "m_zn", "m_zb", "m_x"))

    NU = KD * NS
    EV1, EV2 = 3, 5

    def rstd_of(pool, turn, which, chain, counted, done):
        after(pool, counted, turn + 1)
        m, r = mv[:, which], rst[:, which]
        chain(nc.gpsimd.tensor_tensor(r[:, 0], m[:, :, 1], eps[:, 0:GS], ALU.add))
        chain(nc.gpsimd.tensor_tensor(r[:, 1], r[:, 0], neg_half[:, 0:GS], ALU.pow))
        chain(nc.gpsimd.tensor_tensor(r[:, 2], m[:, :, 0], r[:, 1], ALU.mult))
        nc.gpsimd.tensor_tensor(r[:, 3], r[:, 2], minus_one[:, 0:GS], ALU.mult).then_inc(done, 1)

    def mamba_setup_scalar(act):
        act.wait_ge(m_loaded, 16 * 5)
        nc.scalar.activation(decay_rate[:], a_log, ACT.Exp).then_inc(m_prep, 1)

    def mamba_setup_vector(dve):
        dve.sem_inc(m_z, 1)
        dve.wait_ge(m_loaded, 16 * 5)
        dve.wait_ge(setup, 17)
        for c in range(KD):
            nc.vector.tensor_scalar(skip_w[:, c], ident[:], d_skip[:, c:c + 1], None, ALU.mult).then_inc(m_skip, 1)
        dve.wait_ge(m_half, 1)
        dve.wait_ge(m_edge, 2)

    def mamba_setup_pool(pool):
        nc.gpsimd.memset(decay[:], 0.0).then_inc(m_edge, 1)
        nc.gpsimd.memset(xpad[:], 0.0).then_inc(m_edge, 1)
        pool.wait_ge(m_loaded, 16 * 5)
        nc.gpsimd.tensor_scalar(half_v[:], m_v_sb[:, 0:14], 0.5, None, ALU.mult).then_inc(m_half, 1)
        pool.wait_ge(m_prep, 1)
        nc.gpsimd.tensor_scalar(decay_rate[:], decay_rate[:], -1.0, None, ALU.mult).then_inc(m_prep, 1)

    def mamba_early_vector(dve, g, p):
        link = Chain(dve, m_vec, 1, g)
        yield 12
        if isinstance(g, int) and g < 2:
            dve.wait_ge(x_first[g], 16)
        else:
            dve.wait_ge(x_rest, 16 * (NG - 2))
        for s in range(GS):
            step = nc.vector.bn_stats(stat[:, 0, s], X[:, g, s])
        link(step)
        after(dve, m_nb, g)
        nc.vector.tensor_copy(spare[:], eps[:, 0:1])
        for s in range(GS):
            step = nc.vector.bn_aggr(mv[:, 0, s], stat[:, 0, s])
        step.then_inc(m_mv, 1)

    def mamba_early_pool(pool, g, p):
        yield 17
        rstd_of(pool, g, 0, Chain(pool, m_pool, 3, g), m_mv, m_nb)

    def mamba_early_scalar(act, g, p):
        yield 19
        after(act, m_nb, g + 1)
        after(act, m_xnb, g - 1)
        for s in range(GS):
            step = nc.scalar.activation(xn[:, p, s], X[:, g, s], ACT.Identity, bias=rst[:, 0, 3, s:s + 1],
                                        scale=rst[:, 0, 1, s:s + 1])
        step.then_inc(m_xn, 1)
        yield 27
        after(act, m_tr, g + 1)
        after(act, m_ipg, 2 * g - 2)
        nc.scalar.activation(flat(xnT[:, p]), flat(FB), ACT.Copy).then_inc(m_fev1, 1)
        yield 31
        for m in range(2):
            after(act, m_ip, 2 * g + m + 1)
            after(act, m_conv, KD * g - KD + m + 1 if not isinstance(g, int) or g else 0)
            nc.scalar.activation(xpad[:, m, :, 3:L + 3], seqs(FB[:, m]), ACT.Identity,
                                 bias=b_in[:, m:m + 1]).then_inc(m_fev1, 1)

    def mamba_early_tensor(pe, g, p):
        yield 22
        after(pe, m_xn, g + 1)
        after(pe, m_fev2, EV2 * g)
        for c in range(KD):
            for s in range(GS):
                step = nc.tensor.transpose(FB[:, c, s * L:s * L + L], xn[:, p, s, c * 128:c * 128 + 128], ident[:])
        step.then_inc(m_tr, 1)
        yield 25
        after(pe, m_fev1, EV1 * g + 1)
        for m in range(2):
            for c in range(KD):
                step = nc.tensor.matmul(FB[:, m], w_in[:, c, m * 128:m * 128 + 128], xnT[:, p, c],
                                        start=c == 0, stop=c == KD - 1)
            step.then_inc(m_ip, 1)

    def mamba_late_vector(dve, g, p):
        link = Chain(dve, m_vec3, 7, g)
        for c in range(KD):
            yield 2 + 2 * c
            after(dve, m_fev1, EV1 * g + 2 + c)
            after(dve, m_th, g)
            link(nc.vector.tensor_scalar(half_conv[:, c], xpad[:, c, :, 0:L], hcw[:, 4 * c:4 * c + 1],
                                         hcb[:, c:c + 1], ALU.mult, ALU.add))
            for j in range(1, 4):
                step = nc.vector.scalar_tensor_tensor(
                    out=half_conv[:, c], in0=xpad[:, c, :, j:j + L], scalar=hcw[:, 4 * c + j:4 * c + j + 1],
                    in1=half_conv[:, c], op0=ALU.mult, op1=ALU.add)
                if j < 3:
                    link(step)
            step.then_inc(m_conv, 1)
        yield 8
        after(dve, m_th, g + 1)
        after(dve, m_conv, KD * g + KD)
        nc.vector.scalar_tensor_tensor(out=flat(xconv[:, p]), in0=conv_tanh[:], scalar=1.0,
                                       in1=half_conv.rearrange("p c s t -> p (c s t)"),
                                       op0=ALU.add, op1=ALU.mult).then_inc(m_xc, 1)
        yield 19
        after(dve, m_e, g + 1)
        nc.vector.tensor_scalar(dt_u[:], dt_e[:], 1.0, None, ALU.add).then_inc(m_u1, 1)
        yield 20
        dve.wait_ge(m_u1, g + 1)
        nc.vector.scalar_tensor_tensor(out=dt_c[:], in0=dt_u[:], scalar=1.0, in1=dt_e[:],
                                       op0=ALU.subtract, op1=ALU.subtract).then_inc(m_q, 1)
        yield 22
        after(dve, m_fev2, EV2 * g + 5)
        link(nc.vector.scalar_tensor_tensor(out=gate[:, p], in0=flat(gate_tanh), scalar=1.0, in1=flat(half_gate),
                                            op0=ALU.add, op1=ALU.mult))
        yield 24
        after(dve, m_ln, g + 1)
        nc.vector.scalar_tensor_tensor(out=dt_l[:], in0=dt_pre[:], scalar=0.0, in1=dt_l[:],
                                       op0=ALU.max, op1=ALU.add).then_inc(m_q, 1)
        link.turn_over()

    def mamba_late_pool(pool, g, p):
        yield 10
        after(pool, m_xn, g + 1)
        after(pool, m_z, g)
        nc.gpsimd.tensor_tensor(xnb[:, p], xn[:, p], m_rows[:, 0:1].broadcast_to([128, GS, D]),
                                ALU.add).then_inc(m_xnb, 1)
        yield 18
        after(pool, m_bcs, 3 * g + 1)
        nc.gpsimd.tensor_tensor(bc_rest[:], bc96[0:64], bc16[0:64, p], ALU.subtract).then_inc(m_br, 1)
        yield 21
        after(pool, m_bcs, 3 * g + 2)
        nc.gpsimd.tensor_tensor(bc_mid[:], bc_rest[0:32], bc16[0:32, p], ALU.subtract).then_inc(m_br, 1)
        yield 28
        after(pool, m_q, 2 * g + 2)
        after(pool, m_h, NU * g - NU)
        nc.gpsimd.tensor_tensor(flat(dt[:, p]), dt_l[:], dt_c[:], ALU.subtract).then_inc(m_dt, 1)
        yield 29
        pool.wait_ge(m_dt, g + 1)
        nc.gpsimd.tensor_tensor(dtx[:, p], dt[:, p], xconv[:, p], ALU.mult).then_inc(m_dtx, 1)

    def mamba_late_scalar(act, g, p):
        yield 11
        after(act, m_conv, KD * g + KD)
        nc.scalar.activation(conv_tanh[:], half_conv.rearrange("p c s t -> p (c s t)"), ACT.Tanh).then_inc(m_th, 1)
        yield 16
        after(act, m_bcp, g + 1)
        after(act, m_br, 2 * g)
        after(act, m_cb, NS * g - NS)
        nc.scalar.activation(bc96[:], PS[0:96, 0], ACT.Identity, bias=b_bc[:])
        nc.scalar.activation(bc16[:, p], PS[0:96, 0], ACT.Identity, bias=b_bc[:]).then_inc(m_bcs, 1)
        act.wait_ge(m_bcs, 3 * g + 1)
        act.sem_inc(m_fev2, 1)
        for m in range(KD):
            yield 16 + 3 * m
            after(act, m_dtp, KD * g + m + 1)
            after(act, m_dt, g)
            nc.scalar.activation(dt_pre[:, m * GT:m * GT + GT], FB[:, 1 - m], ACT.Identity,
                                 bias=b_dt[:, m:m + 1]).then_inc(m_fev2, 1)
        yield 20
        after(act, m_br, 2 * g + 1)
        nc.scalar.activation(bc16[0:64, p], bc_rest[:], ACT.Copy).then_inc(m_bcs, 1)
        yield 21
        act.wait_ge(m_fev2, EV2 * g + 3)
        nc.scalar.activation(dt_e[:], dt_pre[:], ACT.Abs).then_inc(m_abs, 1)
        act.wait_ge(m_abs, g + 1)
        nc.scalar.activation(dt_e[:], dt_e[:], ACT.Exp, scale=-1.0).then_inc(m_e, 1)
        yield 22
        after(act, m_br, 2 * g + 2)
        nc.scalar.activation(bc16[0:32, p], bc_mid[:], ACT.Copy).then_inc(m_bcs, 1)
        for m in range(2):
            yield 24
            after(act, m_ipg, 2 * g + m + 1)
            after(act, m_vec3, 7 * g)
            nc.scalar.activation(half_gate[:, m], FB[:, 1 - m], ACT.Identity, bias=hb_in[:, 2 + m:3 + m], scale=0.5)
            nc.scalar.activation(gate_tanh[:, m], FB[:, 1 - m], ACT.Tanh, bias=hb_in[:, 2 + m:3 + m],
                                 scale=0.5).then_inc(m_fev2, 1)
        yield 25
        after(act, m_u1, g + 1)
        nc.scalar.activation(dt_l[:], dt_u[:], ACT.Ln).then_inc(m_ln, 1)

    def mamba_late_tensor(pe, g, p):
        yield 9
        after(pe, m_xc, g + 1)
        after(pe, m_z, g)
        after(pe, m_fev1, EV1 * g + 3)
        for c in range(KD):
            step = nc.tensor.matmul(PS[0:96, 0], w_bc[:, c], xconv[:, p, c], start=c == 0, stop=c == KD - 1)
        step.then_inc(m_bcp, 1)
        for m in range(KD):
            yield 9 + 3 * m
            after(pe, m_fev2, EV2 * g + m)
            for c in range(KD):
                step = nc.tensor.matmul(FB[:, 1 - m], w_dt[:, c, m * 128:m * 128 + 128], xconv[:, p, c],
                                        start=c == 0, stop=c == KD - 1)
            step.then_inc(m_dtp, 1)
        for m in range(2):
            yield 16 + m
            after(pe, m_fev2, EV2 * g + 2 + m)
            for c in range(KD):
                step = nc.tensor.matmul(FB[:, 1 - m], w_in[:, c, 256 + m * 128:384 + m * 128], xnT[:, p, c],
                                        start=c == 0, stop=c == KD - 1)
            step.then_inc(m_ipg, 1)

    def mamba_scan_tensor(pe, g, p):
        def rep_b(n):
            after(pe, m_brep, NS * g + n - 1)
            nc.tensor.matmul(BB[:, n % 2], selector[:, n], bc16[:, p], start=True, stop=True).then_inc(m_bb, 1)

        def rep_c(n):
            after(pe, m_hc, KD * (NS * g + n - 1))
            nc.tensor.matmul(CB[:, n % 2], selector[:, NS + n], bc16[:, p], start=True, stop=True).then_inc(m_cb, 1)

        after(pe, m_bcs, 3 * g + 3)
        rep_b(0)
        rep_c(0)
        rep_b(1)
        rep_c(1)
        after(pe, m_yg, g)
        for c in range(KD):
            nc.tensor.matmul(YB[:, c], skip_w[:, c], xconv[:, p, c], start=True, stop=False)
        for n in range(NS):
            if n + 2 < NS:
                rep_b(n + 2)
            for c in range(KD):
                unit = NU * g + KD * n + c
                after(pe, m_hc, unit + 1)
                nc.tensor.matmul(YB[:, c], ident[:], scaled[:, (KD * n + c) % RC], start=False,
                                 stop=n == NS - 1).then_inc(m_y, 1)
                if c == KD - 1 and n + 2 < NS:
                    rep_c(n + 2)
                yield KD * n + c

    def mamba_scan_scalar(act, g, p):
        after(act, m_dt, g + 1)
        for n in range(NS):
            after(act, m_bb, NS * g + n + 1)
            after(act, m_u, KD * (NS * g + n - 1))
            nc.scalar.activation(b_rep[:, n % 2], BB[:, n % 2], ACT.Copy).then_inc(m_brep, 1)
            for c in range(KD):
                k = KD * n + c
                after(act, m_h, NU * g + k - RD + 1)
                nc.scalar.activation(decay[:, k % RD, :, 1:L], seqs(dt[:, p, c])[:, :, 1:L], ACT.Exp,
                                     scale=decay_rate[:, c * NS + n:c * NS + n + 1]).then_inc(m_da, 1)
                yield k

    def mamba_scan_pool(pool, g, p):
        after(pool, m_dtx, g + 1)
        for n in range(NS):
            after(pool, m_brep, NS * g + n + 1)
            for c in range(KD):
                k = KD * n + c
                after(pool, m_h, NU * g + k - RU + 1)
                nc.gpsimd.tensor_tensor(u_in[:, k % RU], dtx[:, p, c], b_rep[:, n % 2],
                                        ALU.mult).then_inc(m_u, 1)
                yield k

    def mamba_scan_vector(dve, g, p):
        def scale_by_c(k):
            n = k // KD
            after(dve, m_h, NU * g + k + 1)
            after(dve, m_cb, NS * g + n + 1)
            after(dve, m_y, NU * g + k - RC + 1)
            nc.vector.tensor_tensor(scaled[:, k % RC], state[:, k % 2], CB[:, n % 2], ALU.mult).then_inc(m_hc, 1)

        for k in range(NU):
            after(dve, m_da, NU * g + k + 1)
            after(dve, m_u, NU * g + k + 1)
            after(dve, m_hc, NU * g + k - 1)
            nc.vector.tensor_tensor_scan(state[:, k % 2], decay[:, k % RD].rearrange("p s t -> p (s t)"), u_in[:, k % RU],
                                         0.0, ALU.mult, ALU.add).then_inc(m_h, 1)
            if k:
                scale_by_c(k - 1)
            yield k
        scale_by_c(NU - 1)

    def mamba_back_vector(dve, g, p):
        link = Chain(dve, m_vec2, 1, g)
        yield 1
        after(dve, m_op, g)
        after(dve, m_y, NU * g + NU)
        nc.vector.tensor_tensor(flat(y_gated), flat(YB), gate[:, p], ALU.mult).then_inc(m_yg, 1)
        yield 6
        after(dve, m_op, g + 1)
        after(dve, m_zn, g)
        nc.vector.tensor_tensor(flat(z_row), flat(FB), flat(xnb[:, p]), ALU.add).then_inc(m_z, 1)
        dve.wait_ge(m_z, g + 2)
        for s in range(GS):
            step = nc.vector.bn_stats(stat[:, 1, s], z_row[:, s])
        link(step)
        after(dve, m_nb2, g)
        nc.vector.tensor_copy(spare[:], eps[:, 0:1])
        for s in range(GS):
            step = nc.vector.bn_aggr(mv[:, 1, s], stat[:, 1, s])
        step.then_inc(m_mv2, 1)
        yield 17
        after(dve, m_zb, g + 1)
        nc.vector.tensor_tensor(X[:, g], X[:, g], z_norm[:], ALU.add).then_inc(m_x, 1)

    def mamba_back_tensor(pe, g, p):
        yield 2
        after(pe, m_yg, g + 1)
        after(pe, m_fev1, EV1 * (g + 3) if not isinstance(g, int) else EV1 * min(g + 3, NG))
        after(pe, m_fev2, EV2 * (g + 2) if not isinstance(g, int) else EV2 * min(g + 2, NG))
        after(pe, m_z, g + 1)
        for s in range(GS):
            for c in range(KD):
                step = nc.tensor.matmul(flat(FB)[:, s * D:s * D + D], y_gated[:, c, s * L:s * L + L],
                                        w_out[:, c], start=c == 0, stop=c == KD - 1)
        step.then_inc(m_op, 1)

    def mamba_back_scalar(act, g, p):
        yield 13
        after(act, m_nb2, g + 1)
        after(act, m_x, g)
        for s in range(GS):
            step = nc.scalar.activation(z_norm[:, s], z_row[:, s], ACT.Identity, bias=rst[:, 1, 3, s:s + 1],
                                        scale=rst[:, 1, 1, s:s + 1])
        step.then_inc(m_zn, 1)

    def mamba_back_pool(pool, g, p):
        yield 11
        link = Chain(pool, m_pool2, 4, g)
        rstd_of(pool, g, 1, link, m_mv2, m_nb2)
        yield 15
        after(pool, m_zn, g + 1)
        link(nc.gpsimd.tensor_tensor(z_norm[:], z_norm[:], m_rows[:, 1:2].broadcast_to([128, GS, D]), ALU.mult))
        yield 16
        nc.gpsimd.tensor_tensor(z_norm[:], z_norm[:], m_rows[:, 2:3].broadcast_to([128, GS, D]),
                                ALU.add).then_inc(m_zb, 1)
        link.turn_over()

    def mamba(eng, early, late, scan, back):
        def turn(g, p):
            sides = []
            if not isinstance(g, int) or g > 0:
                sides.append(back(eng, g - 1, 1 - p))
            if not isinstance(g, int) or g + 1 < NG:
                sides.append(late(eng, g + 1, 1 - p))
            if not isinstance(g, int) or g + 2 < NG:
                sides.append(early(eng, g + 2, p))
            weave(scan(eng, g, p), merged(*sides))

        alone(early(eng, 0, 0))
        alone(late(eng, 0, 0))
        alone(early(eng, 1, 1))
        turn(0, 0)
        turn(1, 1)
        with eng.Fori(0, (NG - 4) // 2) as pair:
            turn(2 * pair + 2, 0)
            turn(2 * pair + 3, 1)
        turn(NG - 2, 0)
        turn(NG - 1, 1)
        alone(back(eng, NG - 1, 1))
    mamba_mem.end()

    def attention(tag, turn, sets, relu=False, rms=None, out_w=None):
        A = len(sets)
        UNITS = GS * A * KD
        mem = Stage(nc, sem_set[turn])
        t = lambda name, shape, dtype=F32: mem.take(f"{tag}_{name}", shape, dtype)
        s = lambda name: mem.sem(f"{tag}_{name}")
        wide = {"wq": KD * D}
        for a in range(A):
            wide |= {f"wk{a}": KD * D, f"wv{a}": KD * D}
        if out_w:
            wide["wo"] = KD * D
        w = {name: t(name, [128, n]) for name, n in wide.items()}
        halves = {name: a.rearrange("p (k o) -> p k o", k=KD) for name, a in w.items()}
        vecs = {"mask": [128, 2]}
        if rms:
            vecs["norm"] = [128, KD]
        if not relu and not rms:
            vecs |= {"bq": [128, KD], "bo": [128, D], "gate": [128, NH]}
            for a in range(A):
                vecs |= {f"bk{a}": [128, KD], f"bv{a}": [128, D]}
        biased = "bq" in vecs
        v = {name: t(name, shape) for name, shape in vecs.items()}
        bqm = t("bqm", [128, 2, KD])
        share = t("share", [128, A, NH])
        xn = t("xn", [128, 2, GS, D])
        hn = t("hn", [128, GS, D]) if rms else None
        xT = t("xT", [128, KD, GT])
        cT = t("cT", [128, 2, KD, GT]) if "ctx" in sets else None
        q = t("q", [128, 2, 2, KD, GT])
        kT = t("kT", [128, 2, A, KD, GT])
        va = t("va", [128, 2, A, GS, NH, DH + 1])
        pr = t("pr", [128, 2, 8, L])
        pT = t("pT", [128, 2, 8, L])
        mx = t("mx", [128, 2, 8])
        rec = t("rec", [128, NH])
        part = t("part", [128, NH, DH])
        ctx_rows = t("ctx_rows", [128, 2, GS, D])
        oT = t("oT", [128, KD, GT])
        st, mvs, rs = t("st", [128, GS, 6]), t("mvs", [128, GS, 2]), t("rs", [128, 8, GS])
        spare = t("spare", [128, 1])
        x1 = t("x1", [128, 2, D]) if rms else None
        st2, mvs2, rs2 = t("st2", [128, 2, 6]), t("mvs2", [128, 2, 2]), t("rs2", [128, 2, 2])
        scores_of = lambda i: PS[:, 2 * (i % 2):2 * (i % 2) + 2].rearrange("p b (h k) -> p (b h) k", h=4)
        TR = PS[:, 4:6].rearrange("p b (h q) -> p (b h) q", h=4)
        PV = PS[:, 6, 0:NH * (DH + 1)].rearrange("p (h d) -> p h d", h=NH)
        FB = PS[:, 7]

        loaded, ready, ctx_in, ones_set = s("loaded"), s("ready"), [s("ctx_in0"), s("ctx_in1")], s("ones_set")
        mean, scaled_by, normed, vec, pool_c = s("mean"), s("scaled_by"), s("normed"), s("vec"), s("pool_c")
        full, empty = s("full"), s("empty")
        scored, shifted, maxed, exped, turned, taken, valued, rowed, recip, parted, back_in, x_done = map(s, (
            "scored", "shifted", "maxed", "exped", "turned", "taken", "valued", "rowed", "recip", "parted",
            "back_in", "x_done"))
        x1_in, x1_mean, x1_scale = s("x1_in"), s("x1_mean"), s("x1_scale")
        n_loads = len(wide) + len(vecs)

        front_parts = [("tr", 0), ("tr", 1), ("q", 0), ("q", 1)]
        for a in range(A):
            front_parts += [("k", a, 0), ("k", a, 1), ("v", a, 0), ("v", a, 1)]
        back_parts = [("tb", 0), ("tb", 1), ("o", 0), ("o", 1)] if out_w else []
        NF, NB = len(front_parts), len(back_parts)
        STEPS = 3 * UNITS
        back_at = {j: 2 + 2 * j for j in range(NB)}
        norm_at = 2 + 2 * NB if rms else 2
        first_front = max(norm_at + 2, 2 + 2 * NB)
        pace = (STEPS - 2 - first_front) / NF
        front_at = {j: int(first_front + pace * j) for j in range(NF)}

        def product(kind, g, j):
            if kind == "front":
                if isinstance(g, int) and g < 2:
                    return g * NF + j
                return 2 * NF + (g - 2) * (NF + NB) + NB + j
            if isinstance(g, int) and g == NG - 1:
                return 2 * NF + (g - 1) * (NF + NB) + NB + j
            return 2 * NF + g * (NF + NB) + j

        def setup_load(sp):
            for name, dst in {**w, **v}.items():
                sp.dma_start(dst[:], ins[f"{tag}_{name}"]).then_inc(loaded, 16)

        def load_ctx(sp, g, p):
            after(sp, scored, UNITS * (g - 1))
            sp.dma_start(cT[:, p], ins["ctxT"][:, :, g]).then_inc(ctx_in[p], 16)

        def setup_vector(dve):
            dve.wait_ge(loaded, 16 * n_loads)
            nc.vector.memset(va[:], 1.0).then_inc(ones_set, 1)
            for e in range(2):
                if biased:
                    nc.vector.tensor_scalar(bqm[:, e], v["bq"][:], v["mask"][:, e:e + 1], None, ALU.mult).then_inc(ready, 1)
                else:
                    nc.vector.memset(bqm[:, e], 0.0).then_inc(ready, 1)
            if biased:
                dve.wait_ge(recip, 1)
                nc.vector.tensor_scalar(share[:, 0], share[:, 1], -0.5, 0.5, ALU.mult, ALU.add).then_inc(ready, 1)
                dve.wait_ge(ready, 3)
                nc.vector.tensor_scalar(share[:, 1], share[:, 1], 0.5, 0.5, ALU.mult, ALU.add).then_inc(ready, 1)
                dve.wait_ge(ready, 4)

        def setup_scalar(act):
            act.wait_ge(loaded, 16 * n_loads)
            if biased:
                nc.scalar.activation(share[:, 1], v["gate"][:], ACT.Tanh, scale=0.5).then_inc(recip, 1)
            act.wait_ge(ready, 4 if biased else 2)
            act.wait_ge(ones_set, 1)

        recip0 = 1 if biased else 0

        def front_vector(dve, g, p):
            yield 0
            for k in range(GS):
                step = nc.vector.bn_stats(st[:, k], X[:, g, k])
            step.then_inc(vec, 1)
            after(dve, scaled_by, g)
            dve.wait_ge(vec, g + 1)
            nc.vector.tensor_copy(spare[:], eps[:, 0:1])
            for k in range(GS):
                step = nc.vector.bn_aggr(mvs[:, k], st[:, k])
            step.then_inc(mean, 1)
            if biased:
                for j, part in enumerate(front_parts):
                    if part[0] == "v":
                        yield front_at[j] + 1
                        n = product("front", g, j)
                        dve.wait_ge(full, n + 1)
                        a, h = part[1:]
                        for k in range(2):
                            step = nc.vector.tensor_tensor(
                                va[:, p, a, 2 * h + k, :, 0:DH], heads(FB[:, k * D:k * D + D]),
                                heads(v[f"bv{a}"][:]), ALU.add)
                        step.then_inc(empty, 1)

        def front_pool(pool, g, p):
            yield 1
            link = Chain(pool, pool_c, 9 if rms else 3, g)
            after(pool, mean, g + 1)
            m = mvs
            link(nc.gpsimd.tensor_tensor(rs[:, 0], m[:, :, 1], eps[:, 0:GS], ALU.add))
            link(nc.gpsimd.tensor_tensor(rs[:, 1], rs[:, 0], neg_half[:, 0:GS], ALU.pow))
            link(nc.gpsimd.tensor_tensor(rs[:, 2], m[:, :, 0], rs[:, 1], ALU.mult))
            step = nc.gpsimd.tensor_tensor(rs[:, 3], rs[:, 2], minus_one[:, 0:GS], ALU.mult)
            if rms:
                link(step)
                link(nc.gpsimd.tensor_tensor(rs[:, 4], rs[:, 1], rs[:, 1], ALU.mult))
                link(nc.gpsimd.tensor_tensor(rs[:, 5], rs[:, 4], m[:, :, 1], ALU.mult))
                link(nc.gpsimd.tensor_tensor(rs[:, 6], rs[:, 5], rms_eps[:, 0:GS], ALU.add))
                link(nc.gpsimd.tensor_tensor(rs[:, 7], rs[:, 6], neg_half[:, 0:GS], ALU.pow))
                link(nc.gpsimd.tensor_tensor(rs[:, 4], rs[:, 7], rs[:, 1], ALU.mult))
                step = nc.gpsimd.tensor_tensor(rs[:, 5], rs[:, 7], rs[:, 3], ALU.mult)
            step.then_inc(scaled_by, 1)
            link.turn_over()

        def front_scalar(act, g, p):
            yield norm_at
            after(act, scaled_by, g + 1)
            if rms:
                after(act, back_in, 2 * (g - 1) if not isinstance(g, int) or g > 1 else 0)
            after(act, full, product("front", g - 1, 1) + 1 if not isinstance(g, int) or g else 0)
            for k in range(GS):
                step = nc.scalar.activation(xn[:, p, k], X[:, g, k], ACT.Identity, bias=rs[:, 3, k:k + 1],
                                            scale=rs[:, 1, k:k + 1])
            if rms:
                for k in range(GS):
                    step = nc.scalar.activation(hn[:, k], X[:, g, k], ACT.Identity, bias=rs[:, 5, k:k + 1],
                                                scale=rs[:, 4, k:k + 1])
            step.then_inc(normed, 1)
            for j, part in enumerate(front_parts):
                if part[0] == "v" and biased:
                    continue
                yield front_at[j] + 1
                n = product("front", g, j)
                act.wait_ge(full, n + 1)
                if part[0] == "tr":
                    c = part[1]
                    step = nc.scalar.activation(xT[:, c], FB, ACT.Copy, scale=v["norm"][:, c:c + 1] if rms else 1.0)
                elif part[0] == "q":
                    c = part[1]
                    for e in range(2):
                        step = nc.scalar.activation(q[:, p, e, c], FB, ACT.Relu if relu else ACT.Identity,
                                                    bias=bqm[:, e, c:c + 1], scale=v["mask"][:, e:e + 1])
                elif part[0] == "k":
                    a, c = part[1:]
                    if biased:
                        step = nc.scalar.activation(kT[:, p, a, c], FB, ACT.Identity, bias=v[f"bk{a}"][:, c:c + 1])
                    else:
                        step = nc.scalar.activation(kT[:, p, a, c], FB, ACT.Relu if relu else ACT.Copy)
                else:
                    a, h = part[1:]
                    for k in range(2):
                        step = nc.scalar.activation(va[:, p, a, 2 * h + k, :, 0:DH], heads(FB[:, k * D:k * D + D]),
                                                    ACT.Relu if relu else ACT.Copy)
                step.then_inc(empty, 1)

        def front_tensor(pe, g, p):
            for j, part in enumerate(front_parts):
                yield front_at[j]
                n = product("front", g, j)
                after(pe, empty, n)
                if part[0] == "tr":
                    c = part[1]
                    after(pe, normed, g + 1)
                    for k in range(GS):
                        step = nc.tensor.transpose(FB[:, k * L:k * L + L], (hn[:, k] if rms else xn[:, p, k])[:, c * 128:c * 128 + 128],
                                                   ident[:])
                elif part[0] in "qk":
                    a, c = (0, part[1]) if part[0] == "q" else part[1:]
                    src = xT if part[0] == "q" or sets[a] == "x" else cT[:, p]
                    wt = halves["wq" if part[0] == "q" else f"wk{a}"]
                    if src is not xT:
                        wait_ctx(pe, g, p)
                    for h in range(KD):
                        step = nc.tensor.matmul(FB, wt[:, h, c * 128:c * 128 + 128], src[:, h], start=h == 0, stop=h == KD - 1)
                else:
                    a, h = part[1:]
                    src = xT if sets[a] == "x" else cT[:, p]
                    for k in range(2):
                        row = (2 * h + k) * L
                        for i in range(KD):
                            step = nc.tensor.matmul(FB[:, k * D:k * D + D], src[:, i, row:row + L], halves[f"wv{a}"][:, i],
                                                    start=i == 0, stop=i == KD - 1)
                step.then_inc(full, 1)

        def wait_ctx(pe, g, p):
            if isinstance(g, int):
                pe.wait_ge(ctx_in[p], 16 * (g // 2 + 1))
            else:
                pe.wait_ge(ctx_in[p], 8 * (g - p) + 16)

        def head_at(i, n):
            b, c, e = n // 4, n // 2 % 2, n % 2
            return 8 * c + 2 * (2 * unit(i)[2] + b) + e

        def unit(i):
            k, rest = divmod(i, A * KD)
            return (k, *divmod(rest, KD))

        def units_tensor(pe, g, p):
            def scores(i):
                k, a, jp = unit(i)
                u = UNITS * g + i
                after(pe, shifted, u - 1)
                for h in range(4):
                    for b in range(2):
                        (cc, e), j = divmod(h, 2), 2 * jp + b
                        step = nc.tensor.matmul(scores_of(i)[:, 4 * b + h], q[32 * j:32 * j + 32, p, e, cc, k * L:k * L + L],
                                                kT[32 * j:32 * j + 32, p, a, cc, k * L:k * L + L], start=True, stop=True)
                step.then_inc(scored, 1)

            def transposes(i):
                u = UNITS * g + i
                after(pe, exped, u + 1)
                after(pe, taken, u)
                for h in range(8):
                    step = nc.tensor.transpose(TR[:, h], pr[:, i % 2, h], ident[:])
                step.then_inc(turned, 1)

            def values(i):
                k, a, jp = unit(i)
                u = UNITS * g + i
                after(pe, taken, u + 1)
                if jp == 0:
                    after(pe, rowed, GS * A * g + i // KD)
                for h in range(8):
                    step = nc.tensor.matmul(PV[:, head_at(i, h)], pT[:, i % 2, h], va[:, p, a, k, head_at(i, h)],
                                            start=True, stop=True)
                step.then_inc(valued, 1)

            after(pe, empty, product("front", g, NF - 1) + 1)
            scores(0)
            for i in range(UNITS):
                if i + 1 < UNITS:
                    scores(i + 1)
                yield 3 * i
                transposes(i)
                yield 3 * i + 1
                if i:
                    values(i - 1)
                yield 3 * i + 2
            values(UNITS - 1)

        def units_vector(dve, g, p):
            def rows(i):
                k, a, c = unit(i)
                n = GS * A * g + i // KD
                after(dve, valued, UNITS * g + i + 1)
                if i == KD - 1 and out_w:
                    after(dve, full, product("back", g - 2, 1) + 1 if not isinstance(g, int) or g > 1 else 0)
                nc.vector.reciprocal(rec[:], PV[:, :, DH]).then_inc(recip, 1)
                if biased:
                    dve.wait_ge(recip, recip0 + 2 * n + 1)
                    nc.vector.tensor_tensor(rec[:], rec[:], share[:, a], ALU.mult).then_inc(recip, 1)
                    dve.wait_ge(recip, recip0 + 2 * n + 2)
                else:
                    dve.wait_ge(recip, n + 1)
                dst = heads(ctx_rows[:, p, k])
                wide_rec = rec[:].unsqueeze(2).broadcast_to([128, NH, DH])
                if a == 0:
                    nc.vector.tensor_tensor(dst, PV[:, :, 0:DH], wide_rec, ALU.mult).then_inc(rowed, 1)
                else:
                    nc.vector.tensor_tensor(part[:], PV[:, :, 0:DH], wide_rec, ALU.mult).then_inc(rowed, 1)
                    dve.wait_ge(rowed, n + 1)
                    nc.vector.tensor_tensor(dst, dst, part[:], ALU.add).then_inc(parted, 1)
                if not out_w:
                    dve.wait_ge(rowed, n + 1)
                    nc.vector.tensor_tensor(X[:, g, k], X[:, g, k], ctx_rows[:, p, k], ALU.add).then_inc(x_done, 1)

            for i in range(UNITS):
                u = UNITS * g + i
                dve.wait_ge(scored, u + 1)
                nc.vector.tensor_reduce(mx[:, i % 2], scores_of(i), AX.X, ALU.max).then_inc(maxed, 1)
                yield 3 * i
                dve.wait_ge(maxed, u + 1)
                after(dve, turned, u - 1)
                nc.vector.tensor_tensor(pr[:, i % 2], scores_of(i), mx[:, i % 2].unsqueeze(2).broadcast_to([128, 8, L]),
                                        ALU.subtract).then_inc(shifted, 1)
                yield 3 * i + 1
                if i >= 2 and unit(i - 2)[2] == KD - 1:
                    rows(i - 2)
                yield 3 * i + 2
            for i in (UNITS - 2, UNITS - 1):
                if unit(i)[2] == KD - 1:
                    rows(i)

        def units_scalar(act, g, p):
            def take(i):
                u = UNITS * g + i
                after(act, turned, u + 1)
                after(act, valued, u - 1)
                nc.scalar.activation(pT[:, i % 2].rearrange("p h q -> p (h q)"), flat(PS[:, 4:6]), ACT.Copy).then_inc(taken, 1)

            for i in range(UNITS):
                u = UNITS * g + i
                act.wait_ge(shifted, u + 1)
                nc.scalar.activation(pr[:, i % 2], pr[:, i % 2], ACT.Exp).then_inc(exped, 1)
                yield 3 * i
                if i:
                    take(i - 1)
                yield 3 * i + 1
                yield 3 * i + 2
            take(UNITS - 1)

        def units_pool(pool, g, p):
            for i in range(STEPS):
                yield i

        def back_tensor(pe, g, p):
            for j, part in enumerate(back_parts):
                yield back_at[j]
                n = product("back", g, j)
                after(pe, empty, n)
                if part[0] == "tb":
                    c = part[1]
                    after(pe, parted if A > 1 else rowed, GS * (g + 1))
                    if A > 1:
                        after(pe, rowed, GS * A * (g + 1))
                    for k in range(GS):
                        step = nc.tensor.transpose(FB[:, k * L:k * L + L], ctx_rows[:, p, k, c * 128:c * 128 + 128], ident[:])
                else:
                    for k in range(2):
                        row = (2 * part[1] + k) * L
                        for c in range(KD):
                            step = nc.tensor.matmul(FB[:, k * D:k * D + D], oT[:, c, row:row + L], halves["wo"][:, c],
                                                    start=c == 0, stop=c == KD - 1)
                step.then_inc(full, 1)

        def back_scalar(act, g, p):
            for j, part in enumerate(back_parts):
                if part[0] == "tb":
                    yield back_at[j] + 1
                    act.wait_ge(full, product("back", g, j) + 1)
                    nc.scalar.activation(oT[:, part[1]], FB, ACT.Copy).then_inc(empty, 1)

        def back_vector(dve, g, p):
            for j, part in enumerate(back_parts):
                if part[0] == "o":
                    yield back_at[j] + 1
                    h = part[1]
                    turn = 2 * g + h
                    dve.wait_ge(full, product("back", g, j) + 1)
                    o = FB.rearrange("p (k d) -> p k d", k=2)
                    if rms:
                        after(dve, x1_scale, turn)
                        nc.vector.tensor_tensor(x1[:], o, xn[:, p, 2 * h:2 * h + 2], ALU.add).then_inc(empty, 1)
                        dve.wait_ge(empty, product("back", g, j) + 1)
                        nc.vector.tensor_tensor(X[:, g, 2 * h:2 * h + 2], X[:, g, 2 * h:2 * h + 2], x1[:], ALU.add).then_inc(back_in, 1)
                        for k in range(2):
                            step = nc.vector.bn_stats(st2[:, k], x1[:, k])
                        step.then_inc(x1_in, 1)
                        dve.wait_ge(x1_in, turn + 1)
                        nc.vector.tensor_copy(spare[:], eps[:, 0:1])
                        for k in range(2):
                            step = nc.vector.bn_aggr(mvs2[:, k], st2[:, k])
                        step.then_inc(x1_mean, 1)
                    else:
                        after(dve, back_in, turn)
                        nc.vector.tensor_tensor(o2[:], o, v["bo"][:].unsqueeze(1).broadcast_to([128, 2, D]), ALU.add).then_inc(empty, 1)
                        dve.wait_ge(empty, product("back", g, j) + 1)
                        nc.vector.tensor_tensor(X[:, g, 2 * h:2 * h + 2], X[:, g, 2 * h:2 * h + 2], o2[:], ALU.add).then_inc(back_in, 1)

        o2 = t("o2", [128, 2, D]) if biased else None

        def back_pool(pool, g, p):
            if not rms:
                return
            for h in range(2):
                yield back_at[2 + h] + 3
                turn = 2 * g + h
                link = Chain(pool, s_x1c, 4, turn)
                pool.wait_ge(x1_mean, turn + 1)
                link(nc.gpsimd.tensor_tensor(rs2[:, 0], mvs2[:, :, 0], mvs2[:, :, 0], ALU.mult))
                link(nc.gpsimd.tensor_tensor(rs2[:, 0], rs2[:, 0], mvs2[:, :, 1], ALU.add))
                link(nc.gpsimd.tensor_tensor(rs2[:, 0], rs2[:, 0], rms_eps[:, 0:2], ALU.add))
                link(nc.gpsimd.tensor_tensor(rs2[:, 1], rs2[:, 0], neg_half[:, 0:2], ALU.pow))
                nc.gpsimd.tensor_tensor(H[:, g, 2 * h:2 * h + 2], x1[:],
                                        rs2[:, 1].unsqueeze(2).broadcast_to([128, 2, D]), ALU.mult).then_inc(x1_scale, 1)
                link.turn_over()

        s_x1c = s("x1c")

        def run(eng, front, units, back):
            def turn(g, p):
                sides = []
                if not isinstance(g, int) or g > 0:
                    sides.append(back(eng, g - 1, 1 - p))
                if not isinstance(g, int) or g + 1 < NG:
                    sides.append(front(eng, g + 1, 1 - p))
                weave(units(eng, g, p), merged(*sides))

            alone(front(eng, 0, 0))
            turn(0, 0)
            with eng.Fori(0, (NG - 2) // 2) as pair:
                turn(2 * pair + 1, 1)
                turn(2 * pair + 2, 0)
            turn(NG - 1, 1)
            alone(back(eng, NG - 1, 1))

        def none(eng, g, p):
            return
            yield

        def sync(sp):
            setup_load(sp)
            if cT is not None:
                load_ctx(sp, 0, 0)
                load_ctx(sp, 1, 1)
                with sp.Fori(0, (NG - 2) // 2) as pair:
                    load_ctx(sp, 2 * pair + 2, 0)
                    load_ctx(sp, 2 * pair + 3, 1)

        def tensor(pe):
            pe.wait_ge(loaded, 16 * n_loads)
            run(pe, front_tensor, units_tensor, back_tensor if out_w else none)

        def scalar(act):
            setup_scalar(act)
            run(act, front_scalar, units_scalar, back_scalar if out_w else none)

        def vector(dve):
            setup_vector(dve)
            run(dve, front_vector, units_vector, back_vector if out_w else none)

        def pool(pl):
            run(pl, front_pool, units_pool, back_pool if out_w else none)

        mem.end()
        return dict(x_done=x_done, back_in=back_in, sync=sync, tensor=tensor, scalar=scalar, vector=vector, pool=pool)

    def feature_rows(tag, mem, src, dst, norm=False, scale=None):
        t = lambda name, shape: mem.take(f"{tag}_{name}", shape)
        s = lambda name: mem.sem(f"{tag}_{name}")
        xn = t("xn", [128, 2, GS, D])
        st, mvs, rs = t("st", [128, 2, GS, 6]), t("mvs", [128, 2, GS, 2]), t("rs", [128, 2, 4, GS])
        spare = t("spare", [128, 1])
        vec, mean, chain, scaled_by, normed, turned, taken = map(s, ("vec", "mean", "chain", "scaled_by", "normed", "turned", "taken"))
        TB = lambda p: PS[:, 2 * p:2 * p + 2]
        dst_g = dst.rearrange("p k (g r) -> p k g r", r=GT)

        def each(eng, body):
            with eng.Fori(0, NG // 2) as pair:
                for p in range(2):
                    body(2 * pair + p, p, pair)

        def vector(dve):
            def take(g, p, pair):
                dve.wait_ge(turned, g + 1)
                for c in range(KD):
                    if scale is None:
                        step = nc.vector.tensor_copy(dst_g[:, c, g], TB(p)[:, c])
                    else:
                        step = nc.vector.tensor_tensor(dst_g[:, c, g], TB(p)[:, c], scale[:, c:c + 1].broadcast_to([128, GT]), ALU.mult)
                step.then_inc(taken, 1)

            def stats(g, p, pair):
                for k in range(GS):
                    step = nc.vector.bn_stats(st[:, p, k], src[:, g, k])
                step.then_inc(vec, 1)
                dve.wait_ge(vec, g + 1)
                nc.vector.tensor_copy(spare[:], eps[:, 0:1])
                for k in range(GS):
                    step = nc.vector.bn_aggr(mvs[:, p, k], st[:, p, k])
                step.then_inc(mean, 1)

            def body(g, p, pair):
                if norm:
                    stats(g, p, pair)
                take(g, p, pair)

            if not norm:
                each(dve, take)
                return
            stats(0, 0, None)
            with dve.Fori(0, NG // 2 - 1) as pair:
                for p in range(2):
                    stats(2 * pair + p + 1, 1 - p, None)
                    take(2 * pair + p, p, None)
            stats(NG - 1, 1, None)
            take(NG - 2, 0, None)
            take(NG - 1, 1, None)

        def pool(pl):
            if not norm:
                return

            def body(g, p, pair):
                link = Chain(pl, chain, 3, g)
                pl.wait_ge(mean, g + 1)
                link(nc.gpsimd.tensor_tensor(rs[:, p, 0], mvs[:, p, :, 1], eps[:, 0:GS], ALU.add))
                link(nc.gpsimd.tensor_tensor(rs[:, p, 1], rs[:, p, 0], neg_half[:, 0:GS], ALU.pow))
                link(nc.gpsimd.tensor_tensor(rs[:, p, 2], mvs[:, p, :, 0], rs[:, p, 1], ALU.mult))
                nc.gpsimd.tensor_tensor(rs[:, p, 3], rs[:, p, 2], minus_one[:, 0:GS], ALU.mult).then_inc(scaled_by, 1)

            each(pl, body)

        def scalar(act):
            def first(g):
                act.wait_ge(scaled_by, g + 1) if norm else None
                for k in range(GS):
                    if norm:
                        step = nc.scalar.activation(xn[:, g, k], src[:, g, k], ACT.Identity, bias=rs[:, g, 3, k:k + 1],
                                                    scale=rs[:, g, 1, k:k + 1])
                    else:
                        step = nc.scalar.activation(xn[:, g, k], src[:, g, k], ACT.Copy)
                step.then_inc(normed, 1)

            first(0)
            first(1)
            with act.Fori(0, NG // 2 - 1) as pair:
                for p in range(2):
                    g = 2 * pair + p + 2
                    if norm:
                        act.wait_ge(scaled_by, g + 1)
                    act.wait_ge(normed, g)
                    act.wait_ge(turned, g - 1)
                    nc.scalar.activation(spare_s[:], eps[:, 0:1], ACT.Copy)
                    for k in range(GS):
                        if norm:
                            step = nc.scalar.activation(xn[:, p, k], src[:, g, k], ACT.Identity, bias=rs[:, p, 3, k:k + 1],
                                                        scale=rs[:, p, 1, k:k + 1])
                        else:
                            step = nc.scalar.activation(xn[:, p, k], src[:, g, k], ACT.Copy)
                    step.then_inc(normed, 1)

        spare_s = t("spare_s", [128, 1])

        def tensor(pe):
            def turn(g, p):
                pe.wait_ge(normed, g + 1)
                after(pe, taken, g - 1)
                for c in range(KD):
                    for k in range(GS):
                        step = nc.tensor.transpose(TB(p)[:, c, k * L:k * L + L], xn[:, p, k, c * 128:c * 128 + 128], ident[:])
                step.then_inc(turned, 1)

            turn(0, 0)
            turn(1, 1)
            with pe.Fori(0, NG // 2 - 1) as pair:
                for p in range(2):
                    turn(2 * pair + p + 2, p)

        return dict(vector=vector, pool=pool, scalar=scalar, tensor=tensor, taken=taken)

    def recurrence(tag, turn):
        WIN = 8
        B = NG * GS
        TURNS = L // (2 * WIN)
        mem = Stage(nc, sem_set[turn])
        t = lambda name, shape: mem.take(f"{tag}_{name}", shape)
        s = lambda name: mem.sem(f"{tag}_{name}")
        wi, wh, bs = t("wi", [128, KD * D]), t("wh", [128, KD * D]), t("b", [128, 2 * KD])
        wi_k, wh_k = (a.rearrange("p (k o) -> p k o", k=KD) for a in (wi, wh))
        bias = t("bias", [128, KD])
        xT = t("xT", [128, KD, B * L])
        ring = t("ring", [128, KD, B, 2 * WIN])
        HS = t("HS", [128, KD, B, L])
        loaded, bias_set, pre, copied, summed, turned, added = map(
            s, ("loaded", "bias_set", "pre", "copied", "summed", "turned", "added"))
        tanhed, ready = [s("tanhed0"), s("tanhed1")], [s("ready0"), s("ready1")]
        rows = feature_rows(tag + "f", mem, X, xT, norm=True)
        xT_g = xT.rearrange("p k (g r) -> p k g r", r=GT)
        xT_t = xT.rearrange("p k (b w j) -> p k b w j", b=B, j=2 * WIN)

        def bank(step, m):
            return PS[:, 2 * (step % 2) + m, 0:B]

        def sync(sp):
            for dst, name in ((wi, "wi"), (wh, "wh"), (bs, "b")):
                sp.dma_start(dst[:], ins[f"{tag}_{name}"]).then_inc(loaded, 16)

        def tensor(pe):
            pe.wait_ge(loaded, 48)
            rows["tensor"](pe)
            pe.wait_ge(rows["taken"], NG)
            with pe.Fori(0, NG // 2) as pair:
                for p in range(2):
                    g = 2 * pair + p
                    pe.wait_ge(summed, g + 1)
                    for m in range(KD):
                        for k in range(KD):
                            step = nc.tensor.matmul(PS[:, 4 + 2 * p + m], wi_k[:, k, m * 128:m * 128 + 128], xT_g[:, k, g],
                                                    start=k == 0, stop=k == KD - 1)
                    step.then_inc(pre, 1)
            pe.wait_ge(summed, NG + 2)

            def start(turn, j):
                for m in range(KD):
                    nc.tensor.matmul(bank(j, m), ident[:], xT_t[:, m, :, turn, j], start=True, stop=False)

            def join(turn, j):
                for k in range(KD):
                    pe.wait_ge(tanhed[k], turn * (2 * WIN) + j + 1)
                    for m in range(KD):
                        sums = nc.tensor.matmul(bank(j, m), wh_k[:, k, m * 128:m * 128 + 128], ring[:, k, :, (j - 1) % (2 * WIN)],
                                                start=False, stop=k == KD - 1)
                        if k == KD - 1:
                            sums.then_inc(ready[m], 1)

            start(0, 0)
            with pe.Fori(0, TURNS - 1) as turn:
                for j in range(2 * WIN):
                    join(turn, j)
                    start(*((turn, j + 1) if j + 1 < 2 * WIN else (turn + 1, 0)))
            for j in range(2 * WIN):
                join(TURNS - 1, j)
                if j + 1 < 2 * WIN:
                    start(TURNS - 1, j + 1)
            pe.wait_ge(copied, 2 * TURNS + 1)
            for b in range(B):
                if b % 2 == 0 and b >= 4:
                    pe.wait_ge(added, b // 2 - 1)
                for c in range(KD):
                    step = nc.tensor.transpose(PS[:, b // 2 % 2, (b % 2 * KD + c) * 128:(b % 2 * KD + c) * 128 + 128], HS[:, c, b], ident[:])
                if b % 2:
                    step.then_inc(turned, 1)

        def scalar(act):
            rows["scalar"](act)
            act.wait_ge(copied, 1)

            def window(turn, place):
                after(act, copied, 2 * turn + place)
                for j in range(WIN):
                    step = turn * (2 * WIN) + place * WIN + j
                    for m in range(KD):
                        act.wait_ge(ready[m], step + 1)
                        nc.scalar.activation(ring[:, m, :, place * WIN + j], bank(j, m), ACT.Tanh).then_inc(tanhed[m], 1)

            window(0, 0)
            window(0, 1)
            with act.Fori(0, TURNS - 1) as turn:
                window(turn + 1, 0)
                window(turn + 1, 1)

        def vector(dve):
            dve.wait_ge(loaded, 48)
            nc.vector.memset(ring[:], 0.0).then_inc(copied, 1)
            dve.wait_ge(copied, 1)
            dve.sem_inc(tanhed[0], 1)
            dve.sem_inc(tanhed[1], 1)
            nc.vector.tensor_tensor(bias[:], bs[:, 0:KD], bs[:, KD:2 * KD], ALU.add).then_inc(bias_set, 1)
            dve.sem_inc(summed, 2)
            rows["vector"](dve)
            dve.wait_ge(bias_set, 1)
            with dve.Fori(0, NG // 2) as pair:
                for p in range(2):
                    g = 2 * pair + p
                    dve.wait_ge(pre, g + 1)
                    for m in range(KD):
                        step = nc.vector.tensor_tensor(xT_g[:, m, g], PS[:, 4 + 2 * p + m], bias[:, m:m + 1].broadcast_to([128, GT]), ALU.add)
                    step.then_inc(summed, 1)
            HS_w = HS.rearrange("p k b (w j) -> p (k b) w j", j=WIN)
            with dve.Fori(0, TURNS) as turn:
                for place in range(2):
                    for m in range(KD):
                        dve.wait_ge(tanhed[m], (2 * turn + place + 1) * WIN + 1)
                    nc.vector.tensor_copy(HS_w[:, :, 2 * turn + place],
                                          ring.rearrange("p k b j -> p (k b) j")[:, :, place * WIN:place * WIN + WIN]).then_inc(copied, 1)
            x_seq = X.rearrange("p g s d -> p (g s) d")
            for b in range(0, B, 2):
                dve.wait_ge(turned, b // 2 + 1)
                nc.vector.tensor_tensor(x_seq[:, b:b + 2], x_seq[:, b:b + 2],
                                        PS[:, b // 2 % 2].rearrange("p (b d) -> p b d", b=2), ALU.add).then_inc(added, 1)
            dve.wait_ge(added, B // 2)

        def pool(pl):
            rows["pool"](pl)

        mem.end()
        return dict(sync=sync, tensor=tensor, scalar=scalar, vector=vector, pool=pool)

    def experts(tag, turn, src, gated):
        E = 8
        SH = 1 if gated else 0
        N = E + SH
        F, FC = 512, 4
        TILES = NG * GS
        mem = Stage(nc, sem_set[turn])
        t = lambda name, shape: mem.take(f"{tag}_{name}", shape)
        s = lambda name: mem.sem(f"{tag}_{name}")
        UPS = KD * F if gated else 0
        WN = KD * F + UPS + FC * D
        w = t("w", [128, 2, WN])
        w_gate = w[:, :, 0:KD * F].rearrange("p r (k f) -> p r k f", k=KD)
        w_up = w[:, :, KD * F:2 * KD * F].rearrange("p r (k f) -> p r k f", k=KD)
        w_down = w[:, :, KD * F + UPS:].rearrange("p r (f d) -> p r f d", f=FC)
        wr = t("wr", [128, KD * E])
        vec = t("v", [128, KD if gated else E])
        xT = t("xT", [128, KD, NG * GT])
        xT_g = xT.rearrange("p k (g r) -> p k g r", r=GT)
        lT = t("lT", [E, NG * GT])
        lT_g = lT.rearrange("e (g r) -> e g r", r=GT)
        order = t("order", [128, E])
        lg = t("lg", [128, TILES, E])
        tmp = t("tmp", [128, TILES, E])
        best = t("best", [128, 2, TILES, E])
        top = t("top", [128, 6, TILES])
        share = t("share", [128, NG, GS, N])
        share_now = t("share_now", [128, GS])
        act_b = t("act_b", [128, 2, GT])
        hid = t("hid", [128, FC, GT])
        rows = feature_rows(tag + "f", mem, src, xT, norm=not gated, scale=vec if gated else None)
        GB = lambda c: PS[:, 2 * (c % 2)]
        UB = lambda c: PS[:, 2 * (c % 2) + 1]
        DB = PS[:, 4:8, 0:D]

        loaded, w_in = s("loaded"), [s("w_in0"), s("w_in1")]
        logit, logit_in, back, routed, exped, link_s = map(s, ("logit", "logit_in", "back", "routed", "exped", "link"))
        full, silued, hidden, down, added, shared_now = map(s, ("full", "silued", "hidden", "down", "added", "share_now"))

        def load(sp, k, p):
            after(sp, down, FC * NG * (k - 1))
            sp.dma_start(w[:, p], ins[f"{tag}_w"][k]).then_inc(w_in[p], 16)

        def sync(sp):
            for dst, name in ((wr, "wr"), (vec, "v"), (order, "order")):
                sp.dma_start(dst[:], ins[f"{tag}_{name}"]).then_inc(loaded, 16)
            load(sp, 0, 0)
            load(sp, 1, 1)
            with sp.Fori(0, N // 2 - 1) as pair:
                load(sp, 2 * pair + 2, 0)
                load(sp, 2 * pair + 3, 1)
            if N % 2:
                load(sp, N - 1, 0)

        def router_tensor(pe):
            pe.wait_ge(rows["taken"], NG)
            wr_k = wr.rearrange("p (k e) -> p k e", k=KD)
            with pe.Fori(0, NG // 2) as pair:
                for p in range(2):
                    g = 2 * pair + p
                    pe.wait_ge(logit_in, g + 1)
                    for k in range(KD):
                        step = nc.tensor.matmul(PS[0:E, p], wr_k[:, k], xT_g[:, k, g], start=k == 0, stop=k == KD - 1)
                    step.then_inc(logit, 1)
            pe.wait_ge(logit_in, NG + 2)
            for n in range(TILES):
                step = nc.tensor.transpose(PS[:, 7, n * E:n * E + E], lT[:, n * L:n * L + L], ident[0:E, 0:E])
            step.then_inc(back, 1)

        def router_vector(dve):
            with dve.Fori(0, NG // 2) as pair:
                for p in range(2):
                    dve.wait_ge(logit, 2 * pair + p + 1)
                    nc.vector.tensor_copy(lT_g[:, 2 * pair + p], PS[0:E, p]).then_inc(logit_in, 1)
            link = Chain(dve, link_s, 99, 0)
            V = nc.vector
            by_e = lambda a: a.unsqueeze(2).broadcast_to([128, TILES, E])
            from_p = PS[:, 7, 0:TILES * E].rearrange("p (n e) -> p n e", e=E)
            dve.wait_ge(back, 1)
            if gated:
                link(V.tensor_reduce(top[:, 0], from_p, AX.X, ALU.max))
                link(V.tensor_tensor(lg[:], from_p, by_e(top[:, 0]), ALU.subtract))
                dve.sem_inc(routed, 1)
                dve.wait_ge(exped, 1)
                link(V.tensor_reduce(top[:, 1], lg[:], AX.X, ALU.add))
                link(V.reciprocal(top[:, 1], top[:, 1]))
                link(V.tensor_tensor(lg[:], lg[:], by_e(top[:, 1]), ALU.mult))
            else:
                link(V.tensor_tensor(lg[:], from_p, vec[:].unsqueeze(1).broadcast_to([128, TILES, E]), ALU.add))
                dve.sem_inc(routed, 1)
                dve.wait_ge(exped, 1)
                link(V.tensor_scalar(lg[:], lg[:], 1.0, None, ALU.add))
                link(V.reciprocal(lg[:], lg[:]))
            rank = order[:].unsqueeze(1).broadcast_to([128, TILES, E])
            for j in range(2):
                link(V.tensor_reduce(top[:, 2 + j], lg[:], AX.X, ALU.max))
                link(V.tensor_tensor(tmp[:], lg[:], by_e(top[:, 2 + j]), ALU.is_equal))
                link(V.tensor_tensor(tmp[:], tmp[:], rank, ALU.mult))
                link(V.tensor_reduce(top[:, 4], tmp[:], AX.X, ALU.max))
                link(V.tensor_tensor(best[:, j], tmp[:], by_e(top[:, 4]), ALU.is_equal))
                if j == 0:
                    link(V.scalar_tensor_tensor(out=lg[:], in0=best[:, 0], scalar=-2.0, in1=lg[:], op0=ALU.mult, op1=ALU.add))
            if gated:
                link(V.tensor_tensor(top[:, 4], top[:, 3], top[:, 2], ALU.subtract))
                dve.sem_inc(routed, 1)
                dve.wait_ge(exped, 2)
                link(V.tensor_scalar(top[:, 0], top[:, 4], 1.0, None, ALU.add))
                link(V.reciprocal(top[:, 0], top[:, 0]))
                link(V.tensor_tensor(top[:, 1], top[:, 4], top[:, 0], ALU.mult))
            else:
                link(V.tensor_tensor(top[:, 4], top[:, 2], top[:, 3], ALU.add))
            if not gated:
                link(V.tensor_scalar(top[:, 4], top[:, 4], 1e-6, None, ALU.add))
                link(V.reciprocal(top[:, 4], top[:, 4]))
                for j in range(2):
                    step = V.tensor_tensor(top[:, j], top[:, 2 + j], top[:, 4], ALU.mult)
                link(step)
            V.tensor_tensor(best[:, 0], best[:, 0], by_e(top[:, 0]), ALU.mult)
            link(V.tensor_tensor(best[:, 1], best[:, 1], by_e(top[:, 1]), ALU.mult))
            out_s = share.rearrange("p g s n -> p (g s) n")
            if SH:
                V.memset(out_s[:, :, 0:1], 1.0)
            V.tensor_tensor(out_s[:, :, SH:N], best[:, 0], best[:, 1], ALU.add).then_inc(shared_now, 1)
            dve.wait_ge(shared_now, 1)

        def router_scalar(act):
            act.wait_ge(routed, 1)
            nc.scalar.activation(lg[:], lg[:], ACT.Exp, scale=1.0 if gated else -1.0).then_inc(exped, 1)
            if gated:
                act.wait_ge(routed, 2)
                nc.scalar.activation(top[:, 4], top[:, 4], ACT.Exp).then_inc(exped, 1)

        def go_down(pe, u, f, p):
            if f == 0:
                after(pe, added, u)
            pe.wait_ge(hidden, u * FC + (f + 1))
            for r in range(GS):
                step = nc.tensor.matmul(DB[:, r], hid[:, f, r * L:r * L + L], w_down[:, p, f], start=f == 0, stop=f == FC - 1)
            step.then_inc(down, 1)

        def unit_tensor(pe, u, g, k, p, before):
            for f in range(FC):
                after(pe, hidden, u * FC + (f - 1))
                for b, wt in ((GB(f), w_gate), (UB(f), w_up))[:2 if gated else 1]:
                    for c in range(KD):
                        step = nc.tensor.matmul(b, wt[:, p, c, f * 128:f * 128 + 128], xT_g[:, c, g], start=c == 0, stop=c == KD - 1)
                step.then_inc(full, 1)
                if f:
                    go_down(pe, u, f - 1, p)
                elif before is not None:
                    go_down(pe, u - 1, FC - 1, before[2])

        def unit_scalar(act, u, g, k, p, before):
            for f in range(FC):
                if gated:
                    after(act, hidden, u * FC + (f - 1))
                else:
                    after(act, down, u * FC + (f - FC + 1))
                act.wait_ge(full, u * FC + (f + 1))
                if gated:
                    nc.scalar.activation(act_b[:, f % 2], GB(f), ACT.Silu).then_inc(silued, 1)
                else:
                    nc.scalar.activation(hid[:, f], GB(f), ACT.Silu).then_inc(hidden, 1)

        def unit_vector(dve, u, g, k, p, before):
            for f in range(FC):
                if gated:
                    after(dve, down, u * FC + (f - FC + 1))
                    dve.wait_ge(silued, u * FC + (f + 1))
                    nc.vector.tensor_tensor(hid[:, f], act_b[:, f % 2], UB(f), ALU.mult).then_inc(hidden, 1)
                if f == 0 and before is not None:
                    add(dve, u - 1, *before)

        def add(dve, u, g, k, p):
            after(dve, added, u)
            nc.vector.tensor_copy(share_now[:], share[:, g, :, k]).then_inc(shared_now, 1)
            dve.wait_ge(shared_now, u + 2)
            dve.wait_ge(down, u * FC + FC)
            for r in range(GS):
                step = nc.vector.scalar_tensor_tensor(out=X[:, g, r], in0=DB[:, r], scalar=share_now[:, r:r + 1], in1=X[:, g, r],
                                                      op0=ALU.mult, op1=ALU.add)
            step.then_inc(added, 1)

        def run(eng, unit, last):
            def expert(k, p, loads):
                if eng is nc.tensor:
                    eng.wait_ge(w_in[p], 16 * loads)
                first = isinstance(k, int) and k == 0
                unit(eng, k * NG, 0, k, p, None if first else (NG - 1, k - 1, 1 - p))
                with eng.Fori(0, NG - 1) as n:
                    unit(eng, k * NG + n + 1, n + 1, k, p, (n, k, p))

            expert(0, 0, 1)
            with eng.Fori(0, (N - 1) // 2) as pair:
                expert(2 * pair + 1, 1, pair + 1)
                expert(2 * pair + 2, 0, pair + 2)
            if N % 2 == 0:
                expert(N - 1, 1, N // 2)
            last(eng)

        def tensor(pe):
            pe.wait_ge(loaded, 48)
            rows["tensor"](pe)
            router_tensor(pe)
            run(pe, unit_tensor, lambda pe: go_down(pe, N * NG - 1, FC - 1, (N - 1) % 2))

        def scalar(act):
            rows["scalar"](act)
            router_scalar(act)
            run(act, unit_scalar, lambda act: None)

        def vector(dve):
            dve.wait_ge(loaded, 48)
            dve.sem_inc(logit_in, 2)
            rows["vector"](dve)
            router_vector(dve)
            run(dve, unit_vector, lambda dve: add(dve, N * NG - 1, NG - 1, N - 1, 0))
            dve.wait_ge(added, N * NG)

        def pool(pl):
            rows["pool"](pl)

        mem.end()
        return dict(sync=sync, tensor=tensor, scalar=scalar, vector=vector, pool=pool)

    h_mem = Stage(nc, ())
    H = h_mem.take("H", [128, NG, GS, D])

    b_attn = attention("b", 1, ["ctx"], relu=True)
    c_attn = attention("c", 0, ["x"], rms=True, out_w=True)
    experts0 = experts("d", 1, H, True)
    h_mem.end()
    recur = recurrence("r", 0)
    e_attn = attention("e", 1, ["x", "ctx"], out_w=True)
    experts1 = experts("f", 0, X, False)

    stages = [b_attn, c_attn, experts0, recur, e_attn, experts1]

    def pass_stage(eng, n):
        eng.drain().then_inc(passed[n], 1)
        eng.wait_ge(passed[n], 5)
        after(eng, cleared, n)
        eng.drain()

    block = ctx.enter_context(nc.Block())

    @block.sync
    def _(sp):
        sp.dma_start(ident[:], ins["ident"]).then_inc(setup, 16)
        for t, name in ((m_w_sb, "m_w"), (m_v_sb, "m_v"), (b_bc, "m_bbc"), (m_rows, "m_rows"), (selector, "m_sel")):
            sp.dma_start(t[:], ins[name]).then_inc(m_loaded, 16)
        for g in range(NG):
            sp.dma_start(X[:, g], ins["x"][g * GS:g * GS + GS].rearrange("s t d -> t s d")).then_inc(x_first[g] if g < 2 else x_rest, 16)
        for n, st in enumerate(stages):
            sp.sem_inc(passed[n], 1)
            sp.wait_ge(passed[n], 5)
            after(sp, cleared, n)
            sp.drain()
            st["sync"](sp)
        sp.sem_inc(passed[len(stages)], 1)
        sp.wait_ge(passed[len(stages)], 5)
        for g in range(NG):
            sp.dma_start(out[g * GS:g * GS + GS].rearrange("s t d -> t s d"), X[:, g]).then_inc(stored, 16)
        sp.wait_ge(stored, 16 * NG)

    @block.gpsimd
    def _(pool):
        nc.gpsimd.memset(eps[:], EPS)
        nc.gpsimd.memset(rms_eps[:], RMS_EPS)
        nc.gpsimd.memset(minus_one[:], -1.0)
        nc.gpsimd.memset(neg_half[:], -0.5).then_inc(setup, 1)
        mamba_setup_pool(pool)
        pool.wait_ge(setup, 17)
        mamba(pool, mamba_early_pool, mamba_late_pool, mamba_scan_pool, mamba_back_pool)
        for n, st in enumerate(stages):
            pass_stage(pool, n)
            pool.sem_clear(sem_set[n % 2])
            pool.drain().then_inc(cleared, 1)
            st["pool"](pool)
        pass_stage(pool, len(stages))

    @block.scalar
    def _(act):
        mamba_setup_scalar(act)
        act.wait_ge(m_half, 1)
        act.wait_ge(m_prep, 2)
        act.wait_ge(m_edge, 2)
        mamba(act, mamba_early_scalar, mamba_late_scalar, mamba_scan_scalar, mamba_back_scalar)
        for n, st in enumerate(stages):
            pass_stage(act, n)
            st["scalar"](act)
        pass_stage(act, len(stages))

    @block.vector
    def _(dve):
        mamba_setup_vector(dve)
        mamba(dve, mamba_early_vector, mamba_late_vector, mamba_scan_vector, mamba_back_vector)
        for n, st in enumerate(stages):
            pass_stage(dve, n)
            st["vector"](dve)
        pass_stage(dve, len(stages))

    @block.tensor
    def _(pe):
        pe.wait_ge(setup, 17)
        pe.wait_ge(m_loaded, 16 * 5)
        pe.wait_ge(m_skip, KD)
        mamba(pe, mamba_early_tensor, mamba_late_tensor, mamba_scan_tensor, mamba_back_tensor)
        for n, st in enumerate(stages):
            pass_stage(pe, n)
            st["tensor"](pe)
        pass_stage(pe, len(stages))

    ctx.close()


def kernel(**inputs):
    import ml_dtypes
    import concourse.bacc as bacc
    from concourse.bass_utils import run_bass_kernel_spmd as run

    a = {k: np.asarray(v) for k, v in inputs.items()}
    seqs_n = a["x"].shape[0]

    def rows_in(w):
        k = w.shape[0] // 128
        return w.reshape(k, 128, w.shape[1]).transpose(1, 0, 2).reshape(128, -1)

    def per_row(v):
        return v.reshape(v.shape[0] // 128, 128, -1).transpose(1, 0, 2).reshape(128, -1)

    def to_all(v):
        return np.broadcast_to(v.reshape(1, -1), (128, v.size))

    m = {k[8:]: v for k, v in a.items() if k.startswith("L0_attn_")}
    bc3 = np.concatenate([m["bc_w"].T] * 3, axis=1)
    selector = np.zeros((96, 32, 128), ml_dtypes.bfloat16)
    for n in range(32):
        selector[n::32, n] = 1
    arrays = {
        "x": a["x"],
        "ident": np.eye(128, dtype=np.float32),
        "m_w": np.concatenate([rows_in(m["in_proj_w"].T), rows_in(m["dt_w"].T), rows_in(m["out_w"].T), rows_in(bc3)], 1),
        "m_v": np.concatenate([per_row(m["in_proj_b"]), per_row(m["conv_w"][:, 0]), per_row(m["conv_b"]),
                               per_row(m["dt_b"]), per_row(m["A_log"]), per_row(m["D"])], 1),
        "m_bbc": np.concatenate([m["bc_b"]] * 3).reshape(96, 1),
        "m_rows": np.stack([to_all(m["out_b"]), to_all(m["ln_g"]), to_all(m["ln_b"])], 1),
        "m_sel": selector,
    }
    strip_mask = np.zeros((128, 2), np.float32)
    for e in range(2):
        strip_mask[(np.arange(128) // 16) % 2 == e, e] = 16 ** -0.5
    groups = seqs_n // GS
    arrays |= {
        "ctxT": a["ctx_1024"].transpose(2, 0, 1).reshape(2, 128, groups, GS * 128).transpose(1, 0, 2, 3),
        "b_wq": rows_in(a["L0_xattn_Wq"].T), "b_wk0": rows_in(a["L0_xattn_Wk"].T), "b_wv0": rows_in(a["L0_xattn_Wv"].T),
        "b_mask": strip_mask,
    }
    f = {k[7:]: v for k, v in a.items() if k.startswith("L0_ffn_")}
    arrays |= {
        "c_wq": rows_in(f["wq"]), "c_wk0": rows_in(f["wk"]), "c_wv0": rows_in(f["wv"]), "c_wo": rows_in(f["wo"]),
        "c_norm": per_row(f["norm1_w"]), "c_mask": strip_mask,
    }
    e = {k[9:]: v for k, v in a.items() if k.startswith("L1_xattn_")}
    wq, wk, wv = np.split(e["Wqkv"], 3, axis=1)
    _, wka, wva = np.split(e["Wqkv_aux"], 3, axis=1)
    bq, bk, bv = np.split(e["bqkv"], 3)
    _, bka, bva = np.split(e["bqkv_aux"], 3)
    arrays |= {
        "e_wq": rows_in(wq), "e_wk0": rows_in(wk), "e_wv0": rows_in(wv), "e_wk1": rows_in(wka), "e_wv1": rows_in(wva),
        "e_wo": rows_in(e["Wo"]), "e_bq": per_row(bq), "e_bk0": per_row(bk), "e_bk1": per_row(bka),
        "e_bv0": to_all(bv), "e_bv1": to_all(bva), "e_bo": to_all(e["bo"]), "e_gate": to_all(e["g"]), "e_mask": strip_mask,
    }
    r = {k[8:]: v for k, v in a.items() if k.startswith("L1_attn_")}
    arrays |= {"r_wi": rows_in(r["Wi"].T), "r_wh": rows_in(r["Wh"].T),
               "r_b": np.concatenate([per_row(r["bi"]), per_row(r["bh"])], 1)}
    experts = lambda parts: np.stack([np.concatenate([rows_in(w[e]) for w in parts], 1) for e in range(8)])
    order = to_all(np.arange(8, 0, -1, dtype=np.float32))
    shared = np.concatenate([rows_in(f[n]) for n in ("sh_gate", "sh_up", "sh_down")], 1)
    n = {k[7:]: v for k, v in a.items() if k.startswith("L1_ffn_")}
    arrays |= {
        "d_w": np.concatenate([shared[None], experts([f["e_gate"], f["e_up"], f["e_down"]])]), "d_wr": rows_in(f["router_w"]),
        "d_v": per_row(f["norm2_w"]), "d_order": order,
        "f_w": experts([n["w1"].transpose(0, 2, 1), n["w2"].transpose(0, 2, 1)]), "f_wr": rows_in(n["gate_w"].T),
        "f_v": to_all(n["balance_bias"]), "f_order": order,
    }
    nc = bacc.Bacc("TRN2", target_bir_lowering=False, num_devices=1)
    fed, ins = {}, {}
    for name, v in arrays.items():
        v = np.ascontiguousarray(v)
        fed[f"in_{name}"] = v
        ins[name] = nc.dram_tensor(f"in_{name}", v.shape, mybir.dt.from_np(v.dtype), kind="ExternalInput").ap()
    out = nc.dram_tensor("out_0", a["x"].shape, F32, kind="ExternalOutput").ap()
    decoder_kernel(nc, ins, out)
    r = run(nc, [fed], core_ids=[0])
    return r.results[0]["out_0"]
```

```python
import numpy as np

import concourse.bass as bass
from concourse import mybir
from contextlib import ExitStack

F32 = mybir.dt.float32
BF16 = mybir.dt.bfloat16
U32 = mybir.dt.uint32
I32 = mybir.dt.int32
ALU = mybir.AluOpType
ACT = mybir.ActivationFunctionType
AX = mybir.AxisListType


def after(eng, sem, count):
    if not isinstance(count, int) or count > 0:
        eng.wait_ge(sem, count)


def weave(main, side):
    due = next(side, None)
    for step in main:
        while due is not None and due <= step:
            due = next(side, None)
    while due is not None:
        due = next(side, None)


def alone(side):
    for _ in side:
        pass


def merged(*sides):
    heads = [next(s, None) for s in sides]
    while any(h is not None for h in heads):
        n = min((h, n) for n, h in enumerate(heads) if h is not None)[1]
        yield heads[n]
        heads[n] = next(sides[n], None)


class Chain:

    def __init__(self, eng, sem, per, turn):
        self.eng, self.sem, self.per, self.turn, self.k = eng, sem, per, turn, 0

    def __call__(self, step):
        self.k += 1
        assert self.k <= self.per
        step.then_inc(self.sem, 1)
        self.eng.wait_ge(self.sem, self.turn * self.per + self.k)

    def turn_over(self):
        assert self.k == self.per, (self.k, self.per)


class Stage:

    def __init__(self, nc, numbers):
        self.nc, self.stack, self.numbers, self.left = nc, ExitStack(), numbers, iter(numbers)

    def take(self, name, shape, dtype=F32):
        return self.stack.enter_context(self.nc.sbuf_tensor(name, shape, dtype))

    def sem(self, name):
        return self.stack.enter_context(self.nc.semaphore(name, num=next(self.left)))

    def end(self):
        self.stack.close()


def flat(a):
    return a.rearrange("p a b -> p (a b)")


EPS, TINY = 1e-5, 1e-30
D, L, KD, NS = 256, 128, 2, 16
GS = 4
GT = GS * L
STAGES, SET = 7, 60


def units_of_list(groups):
    return 2 * groups + 7


NH, DH = 16, 16
RMS_EPS = 1e-6


def heads(a):
    return a.rearrange("p (h d) -> p h d", h=NH)


def seqs(a):
    return a.rearrange("p (s t) -> p s t", s=GS)


def decoder_kernel(nc, ins, out):
    NG = ins["x"].shape[0] // GS
    ctx = ExitStack()

    def sem(name):
        return ctx.enter_context(nc.semaphore(name))

    def keep(name, shape, dtype=F32):
        return ctx.enter_context(nc.sbuf_tensor(name, shape, dtype))

    X = keep("X", [128, NG, GS, D])
    ident = keep("ident", [128, 128])
    neg_half, eps = keep("neg_half", [128, 16]), keep("eps", [128, 16])
    rms_eps, minus_one = keep("rms_eps", [128, 16]), keep("minus_one", [128, 16])
    PS = ctx.enter_context(nc.psum_tensor("PS", [128, 8, 512], F32))
    x_first, x_rest = [sem("x_first0"), sem("x_first1")], sem("x_rest")
    setup, stored = sem("setup"), sem("stored")
    cleared, zeroed, listed = sem("cleared"), sem("zeroed"), sem("listed")
    UNITS = units_of_list(NG)
    rows_by_expert = nc.dram_tensor("rows_by_expert", (UNITS * GT, D), F32, kind="Internal").ap()
    out_by_expert = nc.dram_tensor("out_by_expert", (UNITS * GT, D), F32, kind="Internal").ap()
    passed = [sem(f"passed{n}") for n in range(STAGES)]
    own = passed[-1].num + 1
    sem_set = [range(own, own + SET), range(own + SET, own + 2 * SET)]

    mamba_mem = Stage(nc, sem_set[0])
    m_w_sb = mamba_mem.take("m_w", [128, 2240])
    w_in = m_w_sb[:, 0:1024].rearrange("p (k o) -> p k o", k=KD)
    w_dt = m_w_sb[:, 1024:1536].rearrange("p (k o) -> p k o", k=KD)
    w_out = m_w_sb[:, 1536:2048].rearrange("p (k o) -> p k o", k=KD)
    w_bc = m_w_sb[:, 2048:2240].rearrange("p (k o) -> p k o", k=KD)
    m_v_sb = mamba_mem.take("m_v", [128, 50])
    b_in, cw, cb = m_v_sb[:, 0:4], m_v_sb[:, 4:12], m_v_sb[:, 12:14]
    b_dt, a_log, d_skip = m_v_sb[:, 14:16], m_v_sb[:, 16:48], m_v_sb[:, 48:50]
    b_bc = mamba_mem.take("b_bc", [96, 1])
    m_rows = mamba_mem.take("m_rows", [128, 3, D])
    selector = mamba_mem.take("selector", [96, 2 * NS, 128], BF16)
    decay_rate = mamba_mem.take("decay_rate", [128, KD * NS])
    half_v = mamba_mem.take("half_v", [128, 14])
    hb_in, hcw, hcb = half_v[:, 0:4], half_v[:, 4:12], half_v[:, 12:14]

    RD, RU, RC = 4, 4, 4
    xn = mamba_mem.take("xn", [128, 2, GS, D])
    xnb = mamba_mem.take("xnb", [128, 2, GS, D])
    xnT = mamba_mem.take("xnT", [128, 2, KD, GT])
    xpad = mamba_mem.take("xpad", [128, KD, GS, L + 3])
    half_conv = mamba_mem.take("half_conv", [128, KD, GS, L])
    conv_tanh = mamba_mem.take("conv_tanh", [128, KD * GT])
    xconv = mamba_mem.take("xconv", [128, 2, KD, GT])
    half_gate = mamba_mem.take("half_gate", [128, KD, GT])
    gate_tanh = mamba_mem.take("gate_tanh", [128, KD, GT])
    gate = mamba_mem.take("gate", [128, 2, KD * GT])
    bc96 = mamba_mem.take("bc96", [96, GT])
    bc_rest = mamba_mem.take("bc_rest", [64, GT])
    bc16 = mamba_mem.take("bc16", [96, 2, GT], BF16)
    dt_pre = mamba_mem.take("dt_pre", [128, KD * GT])
    dt_e = mamba_mem.take("dt_e", [128, KD * GT])
    dt_u = mamba_mem.take("dt_u", [128, KD * GT])
    dt_l = mamba_mem.take("dt_l", [128, KD * GT])
    dt_c = mamba_mem.take("dt_c", [128, KD * GT])
    dt = mamba_mem.take("dt", [128, 2, KD, GT])
    dtx = mamba_mem.take("dtx", [128, 2, KD, GT])
    b_rep = mamba_mem.take("b_rep", [128, 2, GT])
    decay = mamba_mem.take("decay", [128, RD, GS, L])
    u_in = mamba_mem.take("u_in", [128, RU, GT])
    state = mamba_mem.take("state", [128, 2, GT])
    scaled = mamba_mem.take("scaled", [128, RC, GT])
    skip_w = mamba_mem.take("skip_w", [128, KD, 128])
    bc_mid = mamba_mem.take("bc_mid", [32, GT])
    y_gated = mamba_mem.take("y_gated", [128, KD, GT])
    z_row = mamba_mem.take("z_row", [128, GS, D])
    z_norm = mamba_mem.take("z_norm", [128, GS, D])
    spare = mamba_mem.take("spare", [128, 1])
    stat = mamba_mem.take("stat", [128, 2, GS, 6])
    mv = mamba_mem.take("mv", [128, 2, GS, 2])
    rst = mamba_mem.take("rst", [128, 2, 4, GS])

    FB, BB, CB, YB = PS[:, 0:2], PS[:, 2:4], PS[:, 4:6], PS[:, 6:8]
    m_loaded, m_prep, m_edge = mamba_mem.sem("m_loaded"), mamba_mem.sem("m_prep"), mamba_mem.sem("m_edge")
    m_half, m_skip = mamba_mem.sem("m_half"), mamba_mem.sem("m_skip")
    m_vec, m_vec3, m_pool = mamba_mem.sem("m_vec"), mamba_mem.sem("m_vec3"), mamba_mem.sem("m_pool")
    m_vec2, m_pool2 = mamba_mem.sem("m_vec2"), mamba_mem.sem("m_pool2")
    m_mv, m_nb, m_xn, m_tr, m_fev1, m_fev2, m_xnb = map(
        mamba_mem.sem, ("m_mv", "m_nb", "m_xn", "m_tr", "m_fev1", "m_fev2", "m_xnb"))
    m_ip, m_ipg, m_gate, m_conv, m_th, m_xc, m_bcp, m_bcs, m_br = map(
        mamba_mem.sem, ("m_ip", "m_ipg", "m_gate", "m_conv", "m_th", "m_xc", "m_bcp", "m_bcs", "m_br"))
    m_dtp, m_e, m_u1, m_ln, m_q, m_dt, m_dtx = map(
        mamba_mem.sem, ("m_dtp", "m_e", "m_u1", "m_ln", "m_q", "m_dt", "m_dtx"))
    m_bb, m_cb, m_brep, m_da, m_u, m_h, m_hc, m_y = map(
        mamba_mem.sem, ("m_bb", "m_cb", "m_brep", "m_da", "m_u", "m_h", "m_hc", "m_y"))
    m_abs, m_yg, m_op, m_z, m_mv2, m_nb2, m_zn, m_zb, m_x = map(
        mamba_mem.sem, ("m_abs", "m_yg", "m_op", "m_z", "m_mv2", "m_nb2", "m_zn", "m_zb", "m_x"))

    NU = KD * NS
    EV1, EV2 = 3, 5

    def rstd_of(pool, turn, which, chain, counted, done):
        after(pool, counted, turn + 1)
        m, r = mv[:, which], rst[:, which]
        chain(nc.gpsimd.tensor_tensor(r[:, 0], m[:, :, 1], eps[:, 0:GS], ALU.add))
        chain(nc.gpsimd.tensor_tensor(r[:, 1], r[:, 0], neg_half[:, 0:GS], ALU.pow))
        chain(nc.gpsimd.tensor_tensor(r[:, 2], m[:, :, 0], r[:, 1], ALU.mult))
        nc.gpsimd.tensor_tensor(r[:, 3], r[:, 2], minus_one[:, 0:GS], ALU.mult).then_inc(done, 1)

    def mamba_setup_scalar(act):
        act.wait_ge(m_loaded, 16 * 5)
        nc.scalar.activation(decay_rate[:], a_log, ACT.Exp).then_inc(m_prep, 1)

    def mamba_setup_vector(dve):
        dve.sem_inc(m_z, 1)
        dve.wait_ge(m_loaded, 16 * 5)
        dve.wait_ge(setup, 17)
        for c in range(KD):
            nc.vector.tensor_scalar(skip_w[:, c], ident[:], d_skip[:, c:c + 1], None, ALU.mult).then_inc(m_skip, 1)
        dve.wait_ge(m_half, 1)
        dve.wait_ge(m_edge, 2)

    def mamba_setup_pool(pool):
        nc.gpsimd.memset(decay[:], 0.0).then_inc(m_edge, 1)
        nc.gpsimd.memset(xpad[:], 0.0).then_inc(m_edge, 1)
        pool.wait_ge(m_loaded, 16 * 5)
        nc.gpsimd.tensor_scalar(half_v[:], m_v_sb[:, 0:14], 0.5, None, ALU.mult).then_inc(m_half, 1)
        pool.wait_ge(m_prep, 1)
        nc.gpsimd.tensor_scalar(decay_rate[:], decay_rate[:], -1.0, None, ALU.mult).then_inc(m_prep, 1)

    def mamba_early_vector(dve, g, p):
        link = Chain(dve, m_vec, 1, g)
        yield 12
        if isinstance(g, int) and g < 2:
            dve.wait_ge(x_first[g], 16)
        else:
            dve.wait_ge(x_rest, 16 * (NG - 2))
        for s in range(GS):
            step = nc.vector.bn_stats(stat[:, 0, s], X[:, g, s])
        link(step)
        after(dve, m_nb, g)
        nc.vector.tensor_copy(spare[:], eps[:, 0:1])
        for s in range(GS):
            step = nc.vector.bn_aggr(mv[:, 0, s], stat[:, 0, s])
        step.then_inc(m_mv, 1)

    def mamba_early_pool(pool, g, p):
        yield 17
        rstd_of(pool, g, 0, Chain(pool, m_pool, 3, g), m_mv, m_nb)

    def mamba_early_scalar(act, g, p):
        yield 19
        after(act, m_nb, g + 1)
        after(act, m_xnb, g - 1)
        for s in range(GS):
            step = nc.scalar.activation(xn[:, p, s], X[:, g, s], ACT.Identity, bias=rst[:, 0, 3, s:s + 1],
                                        scale=rst[:, 0, 1, s:s + 1])
        step.then_inc(m_xn, 1)
        yield 27
        after(act, m_tr, g + 1)
        after(act, m_ipg, 2 * g - 2)
        nc.scalar.activation(flat(xnT[:, p]), flat(FB), ACT.Copy).then_inc(m_fev1, 1)
        yield 31
        for m in range(2):
            after(act, m_ip, 2 * g + m + 1)
            after(act, m_conv, KD * g - KD + m + 1 if not isinstance(g, int) or g else 0)
            nc.scalar.activation(xpad[:, m, :, 3:L + 3], seqs(FB[:, m]), ACT.Identity,
                                 bias=b_in[:, m:m + 1]).then_inc(m_fev1, 1)

    def mamba_early_tensor(pe, g, p):
        yield 22
        after(pe, m_xn, g + 1)
        after(pe, m_fev2, EV2 * g)
        for c in range(KD):
            for s in range(GS):
                step = nc.tensor.transpose(FB[:, c, s * L:s * L + L], xn[:, p, s, c * 128:c * 128 + 128], ident[:])
        step.then_inc(m_tr, 1)
        yield 25
        after(pe, m_fev1, EV1 * g + 1)
        for m in range(2):
            for c in range(KD):
                step = nc.tensor.matmul(FB[:, m], w_in[:, c, m * 128:m * 128 + 128], xnT[:, p, c],
                                        start=c == 0, stop=c == KD - 1)
            step.then_inc(m_ip, 1)

    def mamba_late_vector(dve, g, p):
        link = Chain(dve, m_vec3, 7, g)
        for c in range(KD):
            yield 2 + 2 * c
            after(dve, m_fev1, EV1 * g + 2 + c)
            after(dve, m_th, g)
            link(nc.vector.tensor_scalar(half_conv[:, c], xpad[:, c, :, 0:L], hcw[:, 4 * c:4 * c + 1],
                                         hcb[:, c:c + 1], ALU.mult, ALU.add))
            for j in range(1, 4):
                step = nc.vector.scalar_tensor_tensor(
                    out=half_conv[:, c], in0=xpad[:, c, :, j:j + L], scalar=hcw[:, 4 * c + j:4 * c + j + 1],
                    in1=half_conv[:, c], op0=ALU.mult, op1=ALU.add)
                if j < 3:
                    link(step)
            step.then_inc(m_conv, 1)
        yield 8
        after(dve, m_th, g + 1)
        after(dve, m_conv, KD * g + KD)
        nc.vector.scalar_tensor_tensor(out=flat(xconv[:, p]), in0=conv_tanh[:], scalar=1.0,
                                       in1=half_conv.rearrange("p c s t -> p (c s t)"),
                                       op0=ALU.add, op1=ALU.mult).then_inc(m_xc, 1)
        yield 19
        after(dve, m_e, g + 1)
        nc.vector.tensor_scalar(dt_u[:], dt_e[:], 1.0, None, ALU.add).then_inc(m_u1, 1)
        yield 20
        dve.wait_ge(m_u1, g + 1)
        nc.vector.scalar_tensor_tensor(out=dt_c[:], in0=dt_u[:], scalar=1.0, in1=dt_e[:],
                                       op0=ALU.subtract, op1=ALU.subtract).then_inc(m_q, 1)
        yield 22
        after(dve, m_fev2, EV2 * g + 5)
        link(nc.vector.scalar_tensor_tensor(out=gate[:, p], in0=flat(gate_tanh), scalar=1.0, in1=flat(half_gate),
                                            op0=ALU.add, op1=ALU.mult))
        yield 24
        after(dve, m_ln, g + 1)
        nc.vector.scalar_tensor_tensor(out=dt_l[:], in0=dt_pre[:], scalar=0.0, in1=dt_l[:],
                                       op0=ALU.max, op1=ALU.add).then_inc(m_q, 1)
        link.turn_over()

    def mamba_late_pool(pool, g, p):
        yield 10
        after(pool, m_xn, g + 1)
        after(pool, m_z, g)
        nc.gpsimd.tensor_tensor(xnb[:, p], xn[:, p], m_rows[:, 0:1].broadcast_to([128, GS, D]),
                                ALU.add).then_inc(m_xnb, 1)
        yield 18
        after(pool, m_bcs, 3 * g + 1)
        nc.gpsimd.tensor_tensor(bc_rest[:], bc96[0:64], bc16[0:64, p], ALU.subtract).then_inc(m_br, 1)
        yield 21
        after(pool, m_bcs, 3 * g + 2)
        nc.gpsimd.tensor_tensor(bc_mid[:], bc_rest[0:32], bc16[0:32, p], ALU.subtract).then_inc(m_br, 1)
        yield 28
        after(pool, m_q, 2 * g + 2)
        after(pool, m_h, NU * g - NU)
        nc.gpsimd.tensor_tensor(flat(dt[:, p]), dt_l[:], dt_c[:], ALU.subtract).then_inc(m_dt, 1)
        yield 29
        pool.wait_ge(m_dt, g + 1)
        nc.gpsimd.tensor_tensor(dtx[:, p], dt[:, p], xconv[:, p], ALU.mult).then_inc(m_dtx, 1)

    def mamba_late_scalar(act, g, p):
        yield 11
        after(act, m_conv, KD * g + KD)
        nc.scalar.activation(conv_tanh[:], half_conv.rearrange("p c s t -> p (c s t)"), ACT.Tanh).then_inc(m_th, 1)
        yield 16
        after(act, m_bcp, g + 1)
        after(act, m_br, 2 * g)
        after(act, m_cb, NS * g - NS)
        nc.scalar.activation(bc96[:], PS[0:96, 0], ACT.Identity, bias=b_bc[:])
        nc.scalar.activation(bc16[:, p], PS[0:96, 0], ACT.Identity, bias=b_bc[:]).then_inc(m_bcs, 1)
        act.wait_ge(m_bcs, 3 * g + 1)
        act.sem_inc(m_fev2, 1)
        for m in range(KD):
            yield 16 + 3 * m
            after(act, m_dtp, KD * g + m + 1)
            after(act, m_dt, g)
            nc.scalar.activation(dt_pre[:, m * GT:m * GT + GT], FB[:, 1 - m], ACT.Identity,
                                 bias=b_dt[:, m:m + 1]).then_inc(m_fev2, 1)
        yield 20
        after(act, m_br, 2 * g + 1)
        nc.scalar.activation(bc16[0:64, p], bc_rest[:], ACT.Copy).then_inc(m_bcs, 1)
        yield 21
        act.wait_ge(m_fev2, EV2 * g + 3)
        nc.scalar.activation(dt_e[:], dt_pre[:], ACT.Abs).then_inc(m_abs, 1)
        act.wait_ge(m_abs, g + 1)
        nc.scalar.activation(dt_e[:], dt_e[:], ACT.Exp, scale=-1.0).then_inc(m_e, 1)
        yield 22
        after(act, m_br, 2 * g + 2)
        nc.scalar.activation(bc16[0:32, p], bc_mid[:], ACT.Copy).then_inc(m_bcs, 1)
        for m in range(2):
            yield 24
            after(act, m_ipg, 2 * g + m + 1)
            after(act, m_vec3, 7 * g)
            nc.scalar.activation(half_gate[:, m], FB[:, 1 - m], ACT.Identity, bias=hb_in[:, 2 + m:3 + m], scale=0.5)
            nc.scalar.activation(gate_tanh[:, m], FB[:, 1 - m], ACT.Tanh, bias=hb_in[:, 2 + m:3 + m],
                                 scale=0.5).then_inc(m_fev2, 1)
        yield 25
        after(act, m_u1, g + 1)
        nc.scalar.activation(dt_l[:], dt_u[:], ACT.Ln).then_inc(m_ln, 1)

    def mamba_late_tensor(pe, g, p):
        yield 9
        after(pe, m_xc, g + 1)
        after(pe, m_z, g)
        after(pe, m_fev1, EV1 * g + 3)
        for c in range(KD):
            step = nc.tensor.matmul(PS[0:96, 0], w_bc[:, c], xconv[:, p, c], start=c == 0, stop=c == KD - 1)
        step.then_inc(m_bcp, 1)
        for m in range(KD):
            yield 9 + 3 * m
            after(pe, m_fev2, EV2 * g + m)
            for c in range(KD):
                step = nc.tensor.matmul(FB[:, 1 - m], w_dt[:, c, m * 128:m * 128 + 128], xconv[:, p, c],
                                        start=c == 0, stop=c == KD - 1)
            step.then_inc(m_dtp, 1)
        for m in range(2):
            yield 16 + m
            after(pe, m_fev2, EV2 * g + 2 + m)
            for c in range(KD):
                step = nc.tensor.matmul(FB[:, 1 - m], w_in[:, c, 256 + m * 128:384 + m * 128], xnT[:, p, c],
                                        start=c == 0, stop=c == KD - 1)
            step.then_inc(m_ipg, 1)

    def mamba_scan_tensor(pe, g, p):
        def rep_b(n):
            after(pe, m_brep, NS * g + n - 1)
            nc.tensor.matmul(BB[:, n % 2], selector[:, n], bc16[:, p], start=True, stop=True).then_inc(m_bb, 1)

        def rep_c(n):
            after(pe, m_hc, KD * (NS * g + n - 1))
            nc.tensor.matmul(CB[:, n % 2], selector[:, NS + n], bc16[:, p], start=True, stop=True).then_inc(m_cb, 1)

        after(pe, m_bcs, 3 * g + 3)
        rep_b(0)
        rep_c(0)
        rep_b(1)
        rep_c(1)
        after(pe, m_yg, g)
        for c in range(KD):
            nc.tensor.matmul(YB[:, c], skip_w[:, c], xconv[:, p, c], start=True, stop=False)
        for n in range(NS):
            if n + 2 < NS:
                rep_b(n + 2)
            for c in range(KD):
                unit = NU * g + KD * n + c
                after(pe, m_hc, unit + 1)
                nc.tensor.matmul(YB[:, c], ident[:], scaled[:, (KD * n + c) % RC], start=False,
                                 stop=n == NS - 1).then_inc(m_y, 1)
                if c == KD - 1 and n + 2 < NS:
                    rep_c(n + 2)
                yield KD * n + c

    def mamba_scan_scalar(act, g, p):
        after(act, m_dt, g + 1)
        for n in range(NS):
            after(act, m_bb, NS * g + n + 1)
            after(act, m_u, KD * (NS * g + n - 1))
            nc.scalar.activation(b_rep[:, n % 2], BB[:, n % 2], ACT.Copy).then_inc(m_brep, 1)
            for c in range(KD):
                k = KD * n + c
                after(act, m_h, NU * g + k - RD + 1)
                nc.scalar.activation(decay[:, k % RD, :, 1:L], seqs(dt[:, p, c])[:, :, 1:L], ACT.Exp,
                                     scale=decay_rate[:, c * NS + n:c * NS + n + 1]).then_inc(m_da, 1)
                yield k

    def mamba_scan_pool(pool, g, p):
        after(pool, m_dtx, g + 1)
        for n in range(NS):
            after(pool, m_brep, NS * g + n + 1)
            for c in range(KD):
                k = KD * n + c
                after(pool, m_h, NU * g + k - RU + 1)
                nc.gpsimd.tensor_tensor(u_in[:, k % RU], dtx[:, p, c], b_rep[:, n % 2],
                                        ALU.mult).then_inc(m_u, 1)
                yield k

    def mamba_scan_vector(dve, g, p):
        def scale_by_c(k):
            n = k // KD
            after(dve, m_h, NU * g + k + 1)
            after(dve, m_cb, NS * g + n + 1)
            after(dve, m_y, NU * g + k - RC + 1)
            nc.vector.tensor_tensor(scaled[:, k % RC], state[:, k % 2], CB[:, n % 2], ALU.mult).then_inc(m_hc, 1)

        for k in range(NU):
            after(dve, m_da, NU * g + k + 1)
            after(dve, m_u, NU * g + k + 1)
            after(dve, m_hc, NU * g + k - 1)
            nc.vector.tensor_tensor_scan(state[:, k % 2], decay[:, k % RD].rearrange("p s t -> p (s t)"), u_in[:, k % RU],
                                         0.0, ALU.mult, ALU.add).then_inc(m_h, 1)
            if k:
                scale_by_c(k - 1)
            yield k
        scale_by_c(NU - 1)

    def mamba_back_vector(dve, g, p):
        link = Chain(dve, m_vec2, 1, g)
        yield 1
        after(dve, m_op, g)
        after(dve, m_y, NU * g + NU)
        nc.vector.tensor_tensor(flat(y_gated), flat(YB), gate[:, p], ALU.mult).then_inc(m_yg, 1)
        yield 6
        after(dve, m_op, g + 1)
        after(dve, m_zn, g)
        nc.vector.tensor_tensor(flat(z_row), flat(FB), flat(xnb[:, p]), ALU.add).then_inc(m_z, 1)
        dve.wait_ge(m_z, g + 2)
        for s in range(GS):
            step = nc.vector.bn_stats(stat[:, 1, s], z_row[:, s])
        link(step)
        after(dve, m_nb2, g)
        nc.vector.tensor_copy(spare[:], eps[:, 0:1])
        for s in range(GS):
            step = nc.vector.bn_aggr(mv[:, 1, s], stat[:, 1, s])
        step.then_inc(m_mv2, 1)
        yield 17
        after(dve, m_zb, g + 1)
        nc.vector.tensor_tensor(X[:, g], X[:, g], z_norm[:], ALU.add).then_inc(m_x, 1)

    def mamba_back_tensor(pe, g, p):
        yield 2
        after(pe, m_yg, g + 1)
        after(pe, m_fev1, EV1 * (g + 3) if not isinstance(g, int) else EV1 * min(g + 3, NG))
        after(pe, m_fev2, EV2 * (g + 2) if not isinstance(g, int) else EV2 * min(g + 2, NG))
        after(pe, m_z, g + 1)
        for s in range(GS):
            for c in range(KD):
                step = nc.tensor.matmul(flat(FB)[:, s * D:s * D + D], y_gated[:, c, s * L:s * L + L],
                                        w_out[:, c], start=c == 0, stop=c == KD - 1)
        step.then_inc(m_op, 1)

    def mamba_back_scalar(act, g, p):
        yield 13
        after(act, m_nb2, g + 1)
        after(act, m_x, g)
        for s in range(GS):
            step = nc.scalar.activation(z_norm[:, s], z_row[:, s], ACT.Identity, bias=rst[:, 1, 3, s:s + 1],
                                        scale=rst[:, 1, 1, s:s + 1])
        step.then_inc(m_zn, 1)

    def mamba_back_pool(pool, g, p):
        yield 11
        link = Chain(pool, m_pool2, 4, g)
        rstd_of(pool, g, 1, link, m_mv2, m_nb2)
        yield 15
        after(pool, m_zn, g + 1)
        link(nc.gpsimd.tensor_tensor(z_norm[:], z_norm[:], m_rows[:, 1:2].broadcast_to([128, GS, D]), ALU.mult))
        yield 16
        nc.gpsimd.tensor_tensor(z_norm[:], z_norm[:], m_rows[:, 2:3].broadcast_to([128, GS, D]),
                                ALU.add).then_inc(m_zb, 1)
        link.turn_over()

    def mamba(eng, early, late, scan, back):
        def turn(g, p):
            sides = []
            if not isinstance(g, int) or g > 0:
                sides.append(back(eng, g - 1, 1 - p))
            if not isinstance(g, int) or g + 1 < NG:
                sides.append(late(eng, g + 1, 1 - p))
            if not isinstance(g, int) or g + 2 < NG:
                sides.append(early(eng, g + 2, p))
            weave(scan(eng, g, p), merged(*sides))

        alone(early(eng, 0, 0))
        alone(late(eng, 0, 0))
        alone(early(eng, 1, 1))
        turn(0, 0)
        turn(1, 1)
        with eng.Fori(0, (NG - 4) // 2) as pair:
            turn(2 * pair + 2, 0)
            turn(2 * pair + 3, 1)
        turn(NG - 2, 0)
        turn(NG - 1, 1)
        alone(back(eng, NG - 1, 1))
    mamba_mem.end()

    SH = NH // KD

    def attention(tag, turn, sets, relu=False, rms=None, out_w=None):
        A = len(sets)
        UNITS = GS * A * KD
        mem = Stage(nc, sem_set[turn])
        t = lambda name, shape, dtype=F32: mem.take(f"{tag}_{name}", shape, dtype)
        s = lambda name: mem.sem(f"{tag}_{name}")
        wide = {"wq": KD * D}
        for a in range(A):
            wide |= {f"wk{a}": KD * D, f"wv{a}": KD * D}
        if out_w:
            wide["wo"] = KD * D
        w = {name: t(name, [128, n]) for name, n in wide.items()}
        halves = {name: a.rearrange("p (k o) -> p k o", k=KD) for name, a in w.items()}
        vecs = {"mask": [128, SH]}
        if rms:
            vecs["norm"] = [128, KD]
        if not relu and not rms:
            vecs |= {"bq": [128, KD], "bo": [128, D], "gate": [128, NH]}
            for a in range(A):
                vecs |= {f"bk{a}": [128, KD], f"bv{a}": [128, D]}
        biased = "bq" in vecs
        v = {name: t(name, shape) for name, shape in vecs.items()}
        q_all = t("q_all", [128, KD, GT])
        share = t("share", [128, A, NH])
        xn = t("xn", [128, 2, GS, D])
        hn = q_all[:].rearrange("p k t -> p (k t)").rearrange("p (s d) -> p s d", s=GS) if rms else None
        xT = t("xT", [128, KD, GT])
        cT = t("cT", [128, 2, KD, GT]) if "ctx" in sets else None
        q = t("q", [128, 2, SH, KD, GT])
        kT = t("kT", [128, 2, A, KD, GT])
        va = t("va", [128, 2, A, GS, NH, DH + 1])
        pr = t("pr", [128, 2, 8, L])
        pT = t("pT", [128, 2, 8, L])
        mx = t("mx", [128, 2, 8])
        rec = t("rec", [128, NH])
        part = t("part", [128, NH, DH])
        ctx_rows = t("ctx_rows", [128, 2, GS, D])
        oT = t("oT", [128, KD, GT]) if out_w else None
        st, mvs, rs = t("st", [128, GS, 6]), t("mvs", [128, GS, 2]), t("rs", [128, 8, GS])
        spare = t("spare", [128, 1])
        x1 = t("x1", [128, 2, D]) if rms else None
        st2, mvs2, rs2 = t("st2", [128, 2, 6]), t("mvs2", [128, 2, 2]), t("rs2", [128, 2, 2])
        scores_of = lambda i: PS[:, 2 * (i % 2):2 * (i % 2) + 2].rearrange("p b (h k) -> p (b h) k", h=4)
        TR = PS[:, 4:6].rearrange("p b (h q) -> p (b h) q", h=4)
        PV = PS[:, 6, 0:NH * (DH + 1)].rearrange("p (h d) -> p h d", h=NH)
        FB = PS[:, 7]

        loaded, ready, ctx_in, ones_set = s("loaded"), s("ready"), [s("ctx_in0"), s("ctx_in1")], s("ones_set")
        mean, scaled_by, normed, vec, pool_c = s("mean"), s("scaled_by"), s("normed"), s("vec"), s("pool_c")
        masked = s("masked")
        full, empty = s("full"), s("empty")
        scored, shifted, maxed, exped, turned, taken, valued, rowed, recip, parted, back_in, x_done = map(s, (
            "scored", "shifted", "maxed", "exped", "turned", "taken", "valued", "rowed", "recip", "parted",
            "back_in", "x_done"))
        x1_in, x1_mean, x1_scale = s("x1_in"), s("x1_mean"), s("x1_scale")
        n_loads = len(wide) + len(vecs)

        front_parts = [("tr", 0), ("tr", 1), ("q", 0), ("q", 1)]
        for a in range(A):
            front_parts += [("k", a, 0), ("k", a, 1), ("v", a, 0), ("v", a, 1)]
        back_parts = [("tb", 0), ("tb", 1), ("o", 0), ("o", 1)] if out_w else []
        NF, NB = len(front_parts), len(back_parts)
        STEPS = 3 * UNITS
        back_at = {j: 2 + 2 * j for j in range(NB)}
        norm_at = 2 + 2 * NB if rms else 2
        first_front = max(norm_at + 2, 2 + 2 * NB)
        pace = (STEPS - 2 - first_front) / NF
        front_at = {j: int(first_front + pace * j) for j in range(NF)}

        def product(kind, g, j):
            if kind == "front":
                if isinstance(g, int) and g < 2:
                    return g * NF + j
                return 2 * NF + (g - 2) * (NF + NB) + NB + j
            if isinstance(g, int) and g == NG - 1:
                return 2 * NF + (g - 1) * (NF + NB) + NB + j
            return 2 * NF + g * (NF + NB) + j

        def setup_load(sp):
            for name, dst in {**w, **v}.items():
                sp.dma_start(dst[:], ins[f"{tag}_{name}"]).then_inc(loaded, 16)

        def load_ctx(sp, g, p):
            after(sp, scored, UNITS * (g - 1))
            sp.dma_start(cT[:, p], ins["ctxT"][:, :, g]).then_inc(ctx_in[p], 16)

        def setup_vector(dve):
            dve.wait_ge(loaded, 16 * n_loads)
            nc.vector.memset(va[:], 1.0).then_inc(ones_set, 1)
            if biased:
                dve.wait_ge(recip, 1)
                nc.vector.tensor_scalar(share[:, 0], share[:, 1], -0.5, 0.5, ALU.mult, ALU.add).then_inc(ready, 1)
                dve.wait_ge(ready, 1)
                nc.vector.tensor_scalar(share[:, 1], share[:, 1], 0.5, 0.5, ALU.mult, ALU.add).then_inc(ready, 1)
                dve.wait_ge(ready, 2)

        def setup_scalar(act):
            act.wait_ge(loaded, 16 * n_loads)
            if biased:
                nc.scalar.activation(share[:, 1], v["gate"][:], ACT.Tanh, scale=0.5).then_inc(recip, 1)
            if biased:
                act.wait_ge(ready, 2)
            act.wait_ge(ones_set, 1)

        recip0 = 1 if biased else 0

        def front_vector(dve, g, p):
            yield 0
            for k in range(GS):
                step = nc.vector.bn_stats(st[:, k], X[:, g, k])
            step.then_inc(vec, 1)
            after(dve, scaled_by, g)
            dve.wait_ge(vec, g + 1)
            nc.vector.tensor_copy(spare[:], eps[:, 0:1])
            for k in range(GS):
                step = nc.vector.bn_aggr(mvs[:, k], st[:, k])
            step.then_inc(mean, 1)
            for j, part in enumerate(front_parts):
                n = product("front", g, j)
                if part[0] == "q":
                    yield front_at[j] + 2
                    dve.wait_ge(empty, n + 1)
                    for e in range(SH):
                        step = nc.vector.tensor_scalar(q[:, p, e, part[1]], q_all[:, part[1]], v["mask"][:, e:e + 1], None, ALU.mult)
                    step.then_inc(masked, 1)
                if part[0] == "v" and biased:
                    yield front_at[j] + 1
                    dve.wait_ge(full, n + 1)
                    a, h = part[1:]
                    for k in range(2):
                        step = nc.vector.tensor_tensor(
                            va[:, p, a, 2 * h + k, :, 0:DH], heads(FB[:, k * D:k * D + D]),
                            heads(v[f"bv{a}"][:]), ALU.add)
                    step.then_inc(empty, 1)

        def front_pool(pool, g, p):
            yield 1
            link = Chain(pool, pool_c, 9 if rms else 3, g)
            after(pool, mean, g + 1)
            m = mvs
            link(nc.gpsimd.tensor_tensor(rs[:, 0], m[:, :, 1], eps[:, 0:GS], ALU.add))
            link(nc.gpsimd.tensor_tensor(rs[:, 1], rs[:, 0], neg_half[:, 0:GS], ALU.pow))
            link(nc.gpsimd.tensor_tensor(rs[:, 2], m[:, :, 0], rs[:, 1], ALU.mult))
            step = nc.gpsimd.tensor_tensor(rs[:, 3], rs[:, 2], minus_one[:, 0:GS], ALU.mult)
            if rms:
                link(step)
                link(nc.gpsimd.tensor_tensor(rs[:, 4], rs[:, 1], rs[:, 1], ALU.mult))
                link(nc.gpsimd.tensor_tensor(rs[:, 5], rs[:, 4], m[:, :, 1], ALU.mult))
                link(nc.gpsimd.tensor_tensor(rs[:, 6], rs[:, 5], rms_eps[:, 0:GS], ALU.add))
                link(nc.gpsimd.tensor_tensor(rs[:, 7], rs[:, 6], neg_half[:, 0:GS], ALU.pow))
                link(nc.gpsimd.tensor_tensor(rs[:, 4], rs[:, 7], rs[:, 1], ALU.mult))
                step = nc.gpsimd.tensor_tensor(rs[:, 5], rs[:, 7], rs[:, 3], ALU.mult)
            step.then_inc(scaled_by, 1)
            link.turn_over()

        def front_scalar(act, g, p):
            yield norm_at
            after(act, scaled_by, g + 1)
            if rms:
                after(act, masked, KD * g)
                after(act, back_in, 2 * (g - 1) if not isinstance(g, int) or g > 1 else 0)
            after(act, full, product("front", g - 1, 1) + 1 if not isinstance(g, int) or g else 0)
            for k in range(GS):
                step = nc.scalar.activation(xn[:, p, k], X[:, g, k], ACT.Identity, bias=rs[:, 3, k:k + 1],
                                            scale=rs[:, 1, k:k + 1])
            if rms:
                for k in range(GS):
                    step = nc.scalar.activation(hn[:, k], X[:, g, k], ACT.Identity, bias=rs[:, 5, k:k + 1],
                                                scale=rs[:, 4, k:k + 1])
            step.then_inc(normed, 1)
            for j, part in enumerate(front_parts):
                if part[0] == "v" and biased:
                    continue
                yield front_at[j] + 1
                n = product("front", g, j)
                act.wait_ge(full, n + 1)
                if part[0] == "tr":
                    c = part[1]
                    step = nc.scalar.activation(xT[:, c], FB, ACT.Copy, scale=v["norm"][:, c:c + 1] if rms else 1.0)
                elif part[0] == "q":
                    c = part[1]
                    after(act, masked, KD * g)
                    if biased:
                        step = nc.scalar.activation(q_all[:, c], FB, ACT.Identity, bias=v["bq"][:, c:c + 1])
                    else:
                        step = nc.scalar.activation(q_all[:, c], FB, ACT.Relu if relu else ACT.Copy)
                elif part[0] == "k":
                    a, c = part[1:]
                    if biased:
                        step = nc.scalar.activation(kT[:, p, a, c], FB, ACT.Identity, bias=v[f"bk{a}"][:, c:c + 1])
                    else:
                        step = nc.scalar.activation(kT[:, p, a, c], FB, ACT.Relu if relu else ACT.Copy)
                else:
                    a, h = part[1:]
                    for k in range(2):
                        step = nc.scalar.activation(va[:, p, a, 2 * h + k, :, 0:DH], heads(FB[:, k * D:k * D + D]),
                                                    ACT.Relu if relu else ACT.Copy)
                step.then_inc(empty, 1)

        def front_tensor(pe, g, p):
            for j, part in enumerate(front_parts):
                yield front_at[j]
                n = product("front", g, j)
                after(pe, empty, n)
                if part[0] == "tr":
                    c = part[1]
                    after(pe, normed, g + 1)
                    for k in range(GS):
                        step = nc.tensor.transpose(FB[:, k * L:k * L + L], (hn[:, k] if rms else xn[:, p, k])[:, c * 128:c * 128 + 128],
                                                   ident[:])
                elif part[0] in "qk":
                    a, c = (0, part[1]) if part[0] == "q" else part[1:]
                    src = xT if part[0] == "q" or sets[a] == "x" else cT[:, p]
                    wt = halves["wq" if part[0] == "q" else f"wk{a}"]
                    if src is not xT:
                        wait_ctx(pe, g, p)
                    for h in range(KD):
                        step = nc.tensor.matmul(FB, wt[:, h, c * 128:c * 128 + 128], src[:, h], start=h == 0, stop=h == KD - 1)
                else:
                    a, h = part[1:]
                    src = xT if sets[a] == "x" else cT[:, p]
                    for k in range(2):
                        row = (2 * h + k) * L
                        for i in range(KD):
                            step = nc.tensor.matmul(FB[:, k * D:k * D + D], src[:, i, row:row + L], halves[f"wv{a}"][:, i],
                                                    start=i == 0, stop=i == KD - 1)
                step.then_inc(full, 1)

        def wait_ctx(pe, g, p):
            if isinstance(g, int):
                pe.wait_ge(ctx_in[p], 16 * (g // 2 + 1))
            else:
                pe.wait_ge(ctx_in[p], 8 * (g - p) + 16)

        def head_at(i, n):
            return SH * unit(i)[2] + n

        def unit(i):
            k, rest = divmod(i, A * KD)
            return (k, *divmod(rest, KD))

        def units_tensor(pe, g, p):
            def scores(i):
                k, a, c = unit(i)
                u = UNITS * g + i
                after(pe, shifted, u - 1)
                for e in range(SH):
                    step = nc.tensor.matmul(scores_of(i)[:, e], q[:, p, e, c, k * L:k * L + L],
                                            kT[:, p, a, c, k * L:k * L + L], start=True, stop=True)
                step.then_inc(scored, 1)

            def transposes(i):
                u = UNITS * g + i
                after(pe, exped, u + 1)
                after(pe, taken, u)
                for h in range(8):
                    step = nc.tensor.transpose(TR[:, h], pr[:, i % 2, h], ident[:])
                step.then_inc(turned, 1)

            def values(i):
                k, a, jp = unit(i)
                u = UNITS * g + i
                after(pe, taken, u + 1)
                if jp == 0:
                    after(pe, rowed, GS * A * g + i // KD)
                for h in range(8):
                    step = nc.tensor.matmul(PV[:, head_at(i, h)], pT[:, i % 2, h], va[:, p, a, k, head_at(i, h)],
                                            start=True, stop=True)
                step.then_inc(valued, 1)

            after(pe, masked, KD * (g + 1))
            after(pe, empty, product("front", g, NF - 1) + 1)
            scores(0)
            for i in range(UNITS):
                if i + 1 < UNITS:
                    scores(i + 1)
                yield 3 * i
                transposes(i)
                yield 3 * i + 1
                if i:
                    values(i - 1)
                yield 3 * i + 2
            values(UNITS - 1)

        def units_vector(dve, g, p):
            def rows(i):
                k, a, c = unit(i)
                n = GS * A * g + i // KD
                after(dve, valued, UNITS * g + i + 1)
                if i == KD - 1 and out_w:
                    after(dve, full, product("back", g - 2, 1) + 1 if not isinstance(g, int) or g > 1 else 0)
                nc.vector.reciprocal(rec[:], PV[:, :, DH]).then_inc(recip, 1)
                if biased:
                    dve.wait_ge(recip, recip0 + 2 * n + 1)
                    nc.vector.tensor_tensor(rec[:], rec[:], share[:, a], ALU.mult).then_inc(recip, 1)
                    dve.wait_ge(recip, recip0 + 2 * n + 2)
                else:
                    dve.wait_ge(recip, n + 1)
                dst = heads(ctx_rows[:, p, k])
                wide_rec = rec[:].unsqueeze(2).broadcast_to([128, NH, DH])
                if a == 0:
                    nc.vector.tensor_tensor(dst, PV[:, :, 0:DH], wide_rec, ALU.mult).then_inc(rowed, 1)
                else:
                    nc.vector.tensor_tensor(part[:], PV[:, :, 0:DH], wide_rec, ALU.mult).then_inc(rowed, 1)
                    dve.wait_ge(rowed, n + 1)
                    nc.vector.tensor_tensor(dst, dst, part[:], ALU.add).then_inc(parted, 1)
                if not out_w:
                    dve.wait_ge(rowed, n + 1)
                    nc.vector.tensor_tensor(X[:, g, k], X[:, g, k], ctx_rows[:, p, k], ALU.add).then_inc(x_done, 1)

            for i in range(UNITS):
                u = UNITS * g + i
                dve.wait_ge(scored, u + 1)
                nc.vector.tensor_reduce(mx[:, i % 2], scores_of(i), AX.X, ALU.max).then_inc(maxed, 1)
                yield 3 * i
                dve.wait_ge(maxed, u + 1)
                after(dve, turned, u - 1)
                nc.vector.tensor_tensor(pr[:, i % 2], scores_of(i), mx[:, i % 2].unsqueeze(2).broadcast_to([128, 8, L]),
                                        ALU.subtract).then_inc(shifted, 1)
                yield 3 * i + 1
                if i >= 2 and unit(i - 2)[2] == KD - 1:
                    rows(i - 2)
                yield 3 * i + 2
            for i in (UNITS - 2, UNITS - 1):
                if unit(i)[2] == KD - 1:
                    rows(i)

        def units_scalar(act, g, p):
            def take(i):
                u = UNITS * g + i
                after(act, turned, u + 1)
                after(act, valued, u - 1)
                nc.scalar.activation(pT[:, i % 2].rearrange("p h q -> p (h q)"), flat(PS[:, 4:6]), ACT.Copy).then_inc(taken, 1)

            for i in range(UNITS):
                u = UNITS * g + i
                act.wait_ge(shifted, u + 1)
                nc.scalar.activation(pr[:, i % 2], pr[:, i % 2], ACT.Exp).then_inc(exped, 1)
                yield 3 * i
                if i:
                    take(i - 1)
                yield 3 * i + 1
                yield 3 * i + 2
            take(UNITS - 1)

        def units_pool(pool, g, p):
            for i in range(STEPS):
                yield i

        def back_tensor(pe, g, p):
            for j, part in enumerate(back_parts):
                yield back_at[j]
                n = product("back", g, j)
                after(pe, empty, n)
                if part[0] == "tb":
                    c = part[1]
                    after(pe, parted if A > 1 else rowed, GS * (g + 1))
                    if A > 1:
                        after(pe, rowed, GS * A * (g + 1))
                    for k in range(GS):
                        step = nc.tensor.transpose(FB[:, k * L:k * L + L], ctx_rows[:, p, k, c * 128:c * 128 + 128], ident[:])
                else:
                    for k in range(2):
                        row = (2 * part[1] + k) * L
                        for c in range(KD):
                            step = nc.tensor.matmul(FB[:, k * D:k * D + D], oT[:, c, row:row + L], halves["wo"][:, c],
                                                    start=c == 0, stop=c == KD - 1)
                step.then_inc(full, 1)

        def back_scalar(act, g, p):
            for j, part in enumerate(back_parts):
                if part[0] == "tb":
                    yield back_at[j] + 1
                    act.wait_ge(full, product("back", g, j) + 1)
                    nc.scalar.activation(oT[:, part[1]], FB, ACT.Copy).then_inc(empty, 1)

        def back_vector(dve, g, p):
            for j, part in enumerate(back_parts):
                if part[0] == "o":
                    yield back_at[j] + 1
                    h = part[1]
                    turn = 2 * g + h
                    dve.wait_ge(full, product("back", g, j) + 1)
                    o = FB.rearrange("p (k d) -> p k d", k=2)
                    if rms:
                        after(dve, x1_scale, turn)
                        nc.vector.tensor_tensor(x1[:], o, xn[:, p, 2 * h:2 * h + 2], ALU.add).then_inc(empty, 1)
                        dve.wait_ge(empty, product("back", g, j) + 1)
                        nc.vector.tensor_tensor(X[:, g, 2 * h:2 * h + 2], X[:, g, 2 * h:2 * h + 2], x1[:], ALU.add).then_inc(back_in, 1)
                        for k in range(2):
                            step = nc.vector.bn_stats(st2[:, k], x1[:, k])
                        step.then_inc(x1_in, 1)
                        dve.wait_ge(x1_in, turn + 1)
                        nc.vector.tensor_copy(spare[:], eps[:, 0:1])
                        for k in range(2):
                            step = nc.vector.bn_aggr(mvs2[:, k], st2[:, k])
                        step.then_inc(x1_mean, 1)
                    else:
                        after(dve, back_in, turn)
                        nc.vector.tensor_tensor(o2[:], o, v["bo"][:].unsqueeze(1).broadcast_to([128, 2, D]), ALU.add).then_inc(empty, 1)
                        dve.wait_ge(empty, product("back", g, j) + 1)
                        nc.vector.tensor_tensor(X[:, g, 2 * h:2 * h + 2], X[:, g, 2 * h:2 * h + 2], o2[:], ALU.add).then_inc(back_in, 1)

        o2 = t("o2", [128, 2, D]) if biased else None

        def back_pool(pool, g, p):
            if not rms:
                return
            for h in range(2):
                yield back_at[2 + h] + 3
                turn = 2 * g + h
                link = Chain(pool, s_x1c, 4, turn)
                pool.wait_ge(x1_mean, turn + 1)
                link(nc.gpsimd.tensor_tensor(rs2[:, 0], mvs2[:, :, 0], mvs2[:, :, 0], ALU.mult))
                link(nc.gpsimd.tensor_tensor(rs2[:, 0], rs2[:, 0], mvs2[:, :, 1], ALU.add))
                link(nc.gpsimd.tensor_tensor(rs2[:, 0], rs2[:, 0], rms_eps[:, 0:2], ALU.add))
                link(nc.gpsimd.tensor_tensor(rs2[:, 1], rs2[:, 0], neg_half[:, 0:2], ALU.pow))
                nc.gpsimd.tensor_tensor(H[:, g, 2 * h:2 * h + 2], x1[:],
                                        rs2[:, 1].unsqueeze(2).broadcast_to([128, 2, D]), ALU.mult).then_inc(x1_scale, 1)
                link.turn_over()

        s_x1c = s("x1c")

        def run(eng, front, units, back):
            def turn(g, p):
                sides = []
                if not isinstance(g, int) or g > 0:
                    sides.append(back(eng, g - 1, 1 - p))
                if not isinstance(g, int) or g + 1 < NG:
                    sides.append(front(eng, g + 1, 1 - p))
                weave(units(eng, g, p), merged(*sides))

            alone(front(eng, 0, 0))
            turn(0, 0)
            with eng.Fori(0, (NG - 2) // 2) as pair:
                turn(2 * pair + 1, 1)
                turn(2 * pair + 2, 0)
            turn(NG - 1, 1)
            alone(back(eng, NG - 1, 1))

        def none(eng, g, p):
            return
            yield

        def sync(sp):
            setup_load(sp)
            if cT is not None:
                load_ctx(sp, 0, 0)
                load_ctx(sp, 1, 1)
                with sp.Fori(0, (NG - 2) // 2) as pair:
                    load_ctx(sp, 2 * pair + 2, 0)
                    load_ctx(sp, 2 * pair + 3, 1)

        def tensor(pe):
            pe.wait_ge(loaded, 16 * n_loads)
            run(pe, front_tensor, units_tensor, back_tensor if out_w else none)

        def scalar(act):
            setup_scalar(act)
            run(act, front_scalar, units_scalar, back_scalar if out_w else none)

        def vector(dve):
            setup_vector(dve)
            run(dve, front_vector, units_vector, back_vector if out_w else none)

        def pool(pl):
            run(pl, front_pool, units_pool, back_pool if out_w else none)

        mem.end()
        return dict(x_done=x_done, back_in=back_in, sync=sync, tensor=tensor, scalar=scalar, vector=vector, pool=pool)

    def feature_rows(tag, mem, src, dst, norm=False, scale=None, xn=None, keep_rows=None):
        t = lambda name, shape: mem.take(f"{tag}_{name}", shape)
        s = lambda name: mem.sem(f"{tag}_{name}")
        xn = t("xn", [128, 2, GS, D]) if xn is None else xn
        st, mvs, rs = t("st", [128, 2, GS, 6]), t("mvs", [128, 2, GS, 2]), t("rs", [128, 2, 4, GS])
        spare = t("spare", [128, 1])
        vec, mean, chain, scaled_by, normed, turned, taken, kept = map(s, (
            "vec", "mean", "chain", "scaled_by", "normed", "turned", "taken", "kept"))
        TB = lambda p: PS[:, 2 * p:2 * p + 2]
        dst_g = dst.rearrange("p k (g r) -> p k g r", r=GT)

        def each(eng, body):
            with eng.Fori(0, NG // 2) as pair:
                for p in range(2):
                    body(2 * pair + p, p, pair)

        def vector(dve):
            def take(g, p, pair):
                dve.wait_ge(turned, g + 1)
                for c in range(KD):
                    if scale is None:
                        step = nc.vector.tensor_copy(dst_g[:, c, g], TB(p)[:, c])
                    else:
                        step = nc.vector.tensor_tensor(dst_g[:, c, g], TB(p)[:, c], scale[:, c:c + 1].broadcast_to([128, GT]), ALU.mult)
                step.then_inc(taken, 1)

            def stats(g, p, pair):
                for k in range(GS):
                    step = nc.vector.bn_stats(st[:, p, k], src[:, g, k])
                step.then_inc(vec, 1)
                dve.wait_ge(vec, g + 1)
                nc.vector.tensor_copy(spare[:], eps[:, 0:1])
                for k in range(GS):
                    step = nc.vector.bn_aggr(mvs[:, p, k], st[:, p, k])
                step.then_inc(mean, 1)

            def body(g, p, pair):
                if norm:
                    stats(g, p, pair)
                take(g, p, pair)

            if not norm:
                each(dve, take)
                return
            stats(0, 0, None)
            with dve.Fori(0, NG // 2 - 1) as pair:
                for p in range(2):
                    stats(2 * pair + p + 1, 1 - p, None)
                    take(2 * pair + p, p, None)
            stats(NG - 1, 1, None)
            take(NG - 2, 0, None)
            take(NG - 1, 1, None)

        def pool(pl):
            if not norm:
                return

            def rstd(g, p):
                link = Chain(pl, chain, 3, g)
                pl.wait_ge(mean, g + 1)
                link(nc.gpsimd.tensor_tensor(rs[:, p, 0], mvs[:, p, :, 1], eps[:, 0:GS], ALU.add))
                link(nc.gpsimd.tensor_tensor(rs[:, p, 1], rs[:, p, 0], neg_half[:, 0:GS], ALU.pow))
                link(nc.gpsimd.tensor_tensor(rs[:, p, 2], mvs[:, p, :, 0], rs[:, p, 1], ALU.mult))
                nc.gpsimd.tensor_tensor(rs[:, p, 3], rs[:, p, 2], minus_one[:, 0:GS], ALU.mult).then_inc(scaled_by, 1)

            def keep_group(g, p):
                if keep_rows is not None:
                    pl.wait_ge(normed, g + 1)
                    nc.gpsimd.tensor_copy(keep_rows[:, g], xn[:, p]).then_inc(kept, 1)

            rstd(0, 0)
            rstd(1, 1)
            with pl.Fori(0, NG // 2 - 1) as pair:
                for p in range(2):
                    keep_group(2 * pair + p, p)
                    rstd(2 * pair + p + 2, p)
            keep_group(NG - 2, 0)
            keep_group(NG - 1, 1)

        def scalar(act):
            def first(g):
                act.wait_ge(scaled_by, g + 1) if norm else None
                for k in range(GS):
                    if norm:
                        step = nc.scalar.activation(xn[:, g, k], src[:, g, k], ACT.Identity, bias=rs[:, g, 3, k:k + 1],
                                                    scale=rs[:, g, 1, k:k + 1])
                    else:
                        step = nc.scalar.activation(xn[:, g, k], src[:, g, k], ACT.Copy)
                step.then_inc(normed, 1)

            first(0)
            first(1)
            with act.Fori(0, NG // 2 - 1) as pair:
                for p in range(2):
                    g = 2 * pair + p + 2
                    if norm:
                        act.wait_ge(scaled_by, g + 1)
                    act.wait_ge(normed, g)
                    if keep_rows is not None:
                        act.wait_ge(kept, g - 1)
                    act.wait_ge(turned, g - 1)
                    nc.scalar.activation(spare_s[:], eps[:, 0:1], ACT.Copy)
                    for k in range(GS):
                        if norm:
                            step = nc.scalar.activation(xn[:, p, k], src[:, g, k], ACT.Identity, bias=rs[:, p, 3, k:k + 1],
                                                        scale=rs[:, p, 1, k:k + 1])
                        else:
                            step = nc.scalar.activation(xn[:, p, k], src[:, g, k], ACT.Copy)
                    step.then_inc(normed, 1)

        spare_s = t("spare_s", [128, 1])

        def tensor(pe):
            def turn(g, p):
                pe.wait_ge(normed, g + 1)
                after(pe, taken, g - 1)
                for c in range(KD):
                    for k in range(GS):
                        step = nc.tensor.transpose(TB(p)[:, c, k * L:k * L + L], xn[:, p, k, c * 128:c * 128 + 128], ident[:])
                step.then_inc(turned, 1)

            turn(0, 0)
            turn(1, 1)
            with pe.Fori(0, NG // 2 - 1) as pair:
                for p in range(2):
                    turn(2 * pair + p + 2, p)

        return dict(vector=vector, pool=pool, scalar=scalar, tensor=tensor, taken=taken, kept=kept)

    def recurrence(tag, turn):
        WIN = 8
        B = NG * GS
        TURNS = L // (2 * WIN)
        mem = Stage(nc, sem_set[turn])
        t = lambda name, shape: mem.take(f"{tag}_{name}", shape)
        s = lambda name: mem.sem(f"{tag}_{name}")
        wi, wh, bs = t("wi", [128, KD * D]), t("wh", [128, KD * D]), t("b", [128, 2 * KD])
        wi_k, wh_k = (a.rearrange("p (k o) -> p k o", k=KD) for a in (wi, wh))
        bias = t("bias", [128, KD])
        xT = t("xT", [128, KD, B * L])
        ring = t("ring", [128, KD, B, 2 * WIN])
        HS = t("HS", [128, KD, B, L])
        loaded, bias_set, pre, copied, summed, turned, added = map(
            s, ("loaded", "bias_set", "pre", "copied", "summed", "turned", "added"))
        tanhed, ready = [s("tanhed0"), s("tanhed1")], [s("ready0"), s("ready1")]
        rows = feature_rows(tag + "f", mem, X, xT, norm=True)
        xT_g = xT.rearrange("p k (g r) -> p k g r", r=GT)
        xT_t = xT.rearrange("p k (b w j) -> p k b w j", b=B, j=2 * WIN)

        def bank(step, m):
            return PS[:, 2 * (step % 2) + m, 0:B]

        def sync(sp):
            for dst, name in ((wi, "wi"), (wh, "wh"), (bs, "b")):
                sp.dma_start(dst[:], ins[f"{tag}_{name}"]).then_inc(loaded, 16)

        def tensor(pe):
            pe.wait_ge(loaded, 48)
            rows["tensor"](pe)
            pe.wait_ge(rows["taken"], NG)
            with pe.Fori(0, NG // 2) as pair:
                for p in range(2):
                    g = 2 * pair + p
                    pe.wait_ge(summed, g + 1)
                    for m in range(KD):
                        for k in range(KD):
                            step = nc.tensor.matmul(PS[:, 4 + 2 * p + m], wi_k[:, k, m * 128:m * 128 + 128], xT_g[:, k, g],
                                                    start=k == 0, stop=k == KD - 1)
                    step.then_inc(pre, 1)
            pe.wait_ge(summed, NG + 2)

            def start(turn, j):
                for m in range(KD):
                    nc.tensor.matmul(bank(j, m), ident[:], xT_t[:, m, :, turn, j], start=True, stop=False)

            def join(turn, j):
                for k in range(KD):
                    pe.wait_ge(tanhed[k], turn * (2 * WIN) + j + 1)
                    for m in range(KD):
                        sums = nc.tensor.matmul(bank(j, m), wh_k[:, k, m * 128:m * 128 + 128], ring[:, k, :, (j - 1) % (2 * WIN)],
                                                start=False, stop=k == KD - 1)
                        if k == KD - 1:
                            sums.then_inc(ready[m], 1)

            start(0, 0)
            with pe.Fori(0, TURNS - 1) as turn:
                for j in range(2 * WIN):
                    join(turn, j)
                    start(*((turn, j + 1) if j + 1 < 2 * WIN else (turn + 1, 0)))
            for j in range(2 * WIN):
                join(TURNS - 1, j)
                if j + 1 < 2 * WIN:
                    start(TURNS - 1, j + 1)
            pe.wait_ge(copied, 2 * TURNS + 1)
            for b in range(B):
                if b % 2 == 0 and b >= 4:
                    pe.wait_ge(added, b // 2 - 1)
                for c in range(KD):
                    step = nc.tensor.transpose(PS[:, b // 2 % 2, (b % 2 * KD + c) * 128:(b % 2 * KD + c) * 128 + 128], HS[:, c, b], ident[:])
                if b % 2:
                    step.then_inc(turned, 1)

        def scalar(act):
            rows["scalar"](act)
            act.wait_ge(copied, 1)

            def window(turn, place):
                after(act, copied, 2 * turn + place)
                for j in range(WIN):
                    step = turn * (2 * WIN) + place * WIN + j
                    for m in range(KD):
                        act.wait_ge(ready[m], step + 1)
                        nc.scalar.activation(ring[:, m, :, place * WIN + j], bank(j, m), ACT.Tanh).then_inc(tanhed[m], 1)

            window(0, 0)
            window(0, 1)
            with act.Fori(0, TURNS - 1) as turn:
                window(turn + 1, 0)
                window(turn + 1, 1)

        def vector(dve):
            dve.wait_ge(loaded, 48)
            nc.vector.memset(ring[:], 0.0).then_inc(copied, 1)
            dve.wait_ge(copied, 1)
            dve.sem_inc(tanhed[0], 1)
            dve.sem_inc(tanhed[1], 1)
            nc.vector.tensor_tensor(bias[:], bs[:, 0:KD], bs[:, KD:2 * KD], ALU.add).then_inc(bias_set, 1)
            dve.sem_inc(summed, 2)
            rows["vector"](dve)
            dve.wait_ge(bias_set, 1)
            with dve.Fori(0, NG // 2) as pair:
                for p in range(2):
                    g = 2 * pair + p
                    dve.wait_ge(pre, g + 1)
                    for m in range(KD):
                        step = nc.vector.tensor_tensor(xT_g[:, m, g], PS[:, 4 + 2 * p + m], bias[:, m:m + 1].broadcast_to([128, GT]), ALU.add)
                    step.then_inc(summed, 1)
            HS_w = HS.rearrange("p k b (w j) -> p (k b) w j", j=WIN)
            with dve.Fori(0, TURNS) as turn:
                for place in range(2):
                    for m in range(KD):
                        dve.wait_ge(tanhed[m], (2 * turn + place + 1) * WIN + 1)
                    nc.vector.tensor_copy(HS_w[:, :, 2 * turn + place],
                                          ring.rearrange("p k b j -> p (k b) j")[:, :, place * WIN:place * WIN + WIN]).then_inc(copied, 1)
            x_seq = X.rearrange("p g s d -> p (g s) d")
            for b in range(0, B, 2):
                dve.wait_ge(turned, b // 2 + 1)
                nc.vector.tensor_tensor(x_seq[:, b:b + 2], x_seq[:, b:b + 2],
                                        PS[:, b // 2 % 2].rearrange("p (b d) -> p b d", b=2), ALU.add).then_inc(added, 1)
            dve.wait_ge(added, B // 2)

        def pool(pl):
            rows["pool"](pl)

        mem.end()
        return dict(sync=sync, tensor=tensor, scalar=scalar, vector=vector, pool=pool)

    def experts(tag, turn, src, gated, rows_by_expert, out_by_expert, listed):
        E = 8
        SHN = NG if gated else 0
        UNITS = units_of_list(NG)
        F, FC = 512, 4
        TILES = NG * GS
        mem = Stage(nc, sem_set[turn])
        t = lambda name, shape, dtype=F32: mem.take(f"{tag}_{name}", shape, dtype)
        s = lambda name: mem.sem(f"{tag}_{name}")
        UPS = (2 if gated else 1) * KD * F
        WN = UPS + FC * D
        w = t("w", [128, 2, WN])
        w_gate = w[:, :, 0:KD * F].rearrange("p r (k f) -> p r k f", k=KD)
        w_up = w[:, :, UPS - KD * F:UPS].rearrange("p r (k f) -> p r k f", k=KD)
        w_down = w[:, :, UPS:].rearrange("p r (f d) -> p r f d", f=FC)
        wr = t("wr", [128, KD * E])
        vec = t("v", [128, KD if gated else E])
        const = t("const", [128, 128 + E + NG + UNITS])
        before_me = const[:, 0:128]
        order = const[:, 128:128 + E]
        whole = const[:, 128 + E:128 + E + NG]
        unit_no = const[:, 128 + E + NG:]
        rows_full = src if gated else t("rows_full", [128, NG, GS, D])
        xT = t("xT", [128, KD, NG * GT])
        xT_g = xT.rearrange("p k (g r) -> p k g r", r=GT)
        big = t("big", [128, 2 * GS * 2 * D])
        lT = big[0:E, 0:NG * GT]
        lT_g = lT.rearrange("e (g r) -> e g r", r=GT)
        ones = t("ones", [128, 128])
        lg = t("lg", [128, TILES, E])
        tmp = t("tmp", [128, TILES, E])
        best = t("best", [128, 2, TILES, E])
        chosen, total, until, place, first_of = (t(n, [128, E, TILES]) for n in ("chosen", "total", "until", "place", "first_of"))
        filled, units_e, last_e, base_e = t("filled", [128, E, NG]), t("units_e", [128, E]), t("last_e", [128, E]), t("base_e", [128, E])
        ones_e = t("ones_e", [128, E])
        passed_e, expert_f, expert_i = t("passed_e", [128, UNITS, E]), t("expert_f", [128, UNITS]), t("expert_i", [128, UNITS], I32)
        top = t("top", [128, 5, TILES])
        slot_f = t("slot_f", [128, TILES, 2])
        slot = t("slot", [128, NG, GS, 2], I32)
        share = t("share", [128, NG, GS, 2])
        slot_now, share_now = t("slot_now", [128, 2, GS, 2], I32), t("share_now", [128, 2, GS, 2])
        staged_rows = t("staged_rows", [128, 2, GS, D])
        unit_rows = t("unit_rows", [128, 2, GS, D])
        unit_T = t("unit_T", [128, 2, KD, GT])
        mark = t("mark", [128, 1])
        act_b = t("act_b", [128, 2, GT])
        hid = t("hid", [128, 2, FC, GT])
        y_rows = t("y_rows", [128, 2, GS, D])
        y_got = big.rearrange("p (r k j d) -> p r k j d", r=2, k=GS, j=2)
        rows = feature_rows(tag + "f", mem, src, xT, norm=not gated, scale=vec if gated else None,
                            xn=staged_rows, keep_rows=None if gated else rows_full)
        GB = lambda c: PS[:, 2 * (c % 2)]
        UB = lambda c: PS[:, 2 * (c % 2) + 1]
        DB = PS[:, 4:6].rearrange("p b (s d) -> p (b s) d", s=2)
        TB = PS[:, 6:8]
        list_units = rows_by_expert.rearrange("(u r p) d -> p u r d", p=128, r=GS)
        out_units = out_by_expert.rearrange("(u r p) d -> p u r d", p=128, r=GS)

        loaded, w_gu, w_dn = s("loaded"), [s("w_gu0"), s("w_gu1")], [s("w_dn0"), s("w_dn1")]
        logit, logit_in, back, routed, exped, link_s, chose, ranked, placed = map(s, (
            "logit", "logit_in", "back", "routed", "exped", "link", "chose", "ranked", "placed"))
        full, silued, hidden, down, taken, turned, turned_in = map(s, (
            "full", "silued", "hidden", "down", "taken", "turned", "turned_in"))
        staged, in_list, row_in, y_out = s("staged"), [s("in_list0"), s("in_list1")], [s("row_in0"), s("row_in1")], [s("y_out0"), s("y_out1")]
        asked, got, share_set, halved, combined = s("asked"), [s("got0"), s("got1")], s("share_set"), s("halved"), s("combined")

        def router_tensor(pe):
            pe.wait_ge(rows["taken"], NG)
            wr_k = wr.rearrange("p (k e) -> p k e", k=KD)
            with pe.Fori(0, NG // 2) as pair:
                for p in range(2):
                    g = 2 * pair + p
                    pe.wait_ge(logit_in, g + 1)
                    for k in range(KD):
                        step = nc.tensor.matmul(PS[0:E, p], wr_k[:, k], xT_g[:, k, g], start=k == 0, stop=k == KD - 1)
                    step.then_inc(logit, 1)
            pe.wait_ge(logit_in, NG + 2)
            for n in range(TILES):
                step = nc.tensor.transpose(PS[:, 7, n * E:n * E + E], lT[:, n * L:n * L + L], ident[0:E, 0:E])
            step.then_inc(back, 1)

        def rank_tensor(pe):
            pe.wait_ge(chose, 1)
            nc.tensor.matmul(PS[:, 4, 0:E * TILES], before_me, chosen.rearrange("p e n -> p (e n)"), start=True, stop=True)
            nc.tensor.matmul(PS[:, 5, 0:E * TILES], ones[:], chosen.rearrange("p e n -> p (e n)"), start=True, stop=True).then_inc(ranked, 1)

        def router_vector(dve):
            nc.vector.memset(ones_e[:], 1.0).then_inc(link_s, 1)
            nc.vector.memset(first_of[:], 1.0).then_inc(link_s, 1)
            dve.wait_ge(link_s, 2)
            nc.vector.memset(first_of[:, :, 0:1], 0.0).then_inc(link_s, 1)
            with dve.Fori(0, NG // 2) as pair:
                for p in range(2):
                    dve.wait_ge(logit, 2 * pair + p + 1)
                    nc.vector.tensor_copy(lT_g[:, 2 * pair + p], PS[0:E, p]).then_inc(logit_in, 1)
            link = Chain(dve, link_s, 99, 0)
            link.k = 3
            V = nc.vector
            by_e = lambda a: a.unsqueeze(2).broadcast_to([128, TILES, E])
            from_p = PS[:, 7, 0:TILES * E].rearrange("p (n e) -> p n e", e=E)
            dve.wait_ge(back, 1)
            if gated:
                link(V.tensor_reduce(top[:, 0], from_p, AX.X, ALU.max))
                link(V.tensor_tensor(lg[:], from_p, by_e(top[:, 0]), ALU.subtract))
                dve.sem_inc(routed, 1)
                dve.wait_ge(exped, 1)
                link(V.tensor_reduce(top[:, 1], lg[:], AX.X, ALU.add))
                link(V.reciprocal(top[:, 1], top[:, 1]))
                link(V.tensor_tensor(lg[:], lg[:], by_e(top[:, 1]), ALU.mult))
            else:
                link(V.tensor_tensor(lg[:], from_p, vec[:].unsqueeze(1).broadcast_to([128, TILES, E]), ALU.add))
                dve.sem_inc(routed, 1)
                dve.wait_ge(exped, 1)
                link(V.tensor_scalar(lg[:], lg[:], 1.0, None, ALU.add))
                link(V.reciprocal(lg[:], lg[:]))
            rank = order.unsqueeze(1).broadcast_to([128, TILES, E])
            for j in range(2):
                link(V.tensor_reduce(top[:, 2 + j], lg[:], AX.X, ALU.max))
                link(V.tensor_tensor(tmp[:], lg[:], by_e(top[:, 2 + j]), ALU.is_equal))
                link(V.tensor_tensor(tmp[:], tmp[:], rank, ALU.mult))
                link(V.tensor_reduce(top[:, 4], tmp[:], AX.X, ALU.max))
                link(V.tensor_tensor(best[:, j], tmp[:], by_e(top[:, 4]), ALU.is_equal))
                if j == 0:
                    link(V.scalar_tensor_tensor(out=lg[:], in0=best[:, 0], scalar=-2.0, in1=lg[:], op0=ALU.mult, op1=ALU.add))
            link(V.tensor_tensor(chosen.rearrange("p e n -> p n e"), best[:, 0], best[:, 1], ALU.add))
            dve.sem_inc(chose, 1)
            if gated:
                link(V.tensor_tensor(top[:, 4], top[:, 3], top[:, 2], ALU.subtract))
                dve.sem_inc(routed, 1)
                dve.wait_ge(exped, 2)
                link(V.tensor_scalar(top[:, 0], top[:, 4], 1.0, None, ALU.add))
                link(V.reciprocal(top[:, 0], top[:, 0]))
                link(V.tensor_tensor(top[:, 1], top[:, 4], top[:, 0], ALU.mult))
            else:
                link(V.tensor_tensor(top[:, 4], top[:, 2], top[:, 3], ALU.add))
            if not gated:
                link(V.tensor_scalar(top[:, 4], top[:, 4], 1e-6, None, ALU.add))
                link(V.reciprocal(top[:, 4], top[:, 4]))
                for j in range(2):
                    step = V.tensor_tensor(top[:, j], top[:, 2 + j], top[:, 4], ALU.mult)
                link(step)
            share_t = share.rearrange("p g s j -> p (g s) j")
            for j in range(2):
                link(V.tensor_copy(share_t[:, :, j], top[:, j]))
            dve.wait_ge(ranked, 1)
            ranks = lambda b: PS[:, b, 0:E * TILES].rearrange("p (e n) -> p e n", e=E)
            flat_e = lambda a: a.rearrange("p e n -> p (e n)")
            link(V.tensor_copy(total[:], ranks(5)))
            link(V.tensor_tensor_scan(flat_e(until), flat_e(first_of), flat_e(total), 0.0, ALU.mult, ALU.add))
            link(V.tensor_tensor(filled[:], until[:, :, TILES - 1:TILES].broadcast_to([128, E, NG]),
                                 whole.unsqueeze(1).broadcast_to([128, E, NG]), ALU.is_gt))
            link(V.tensor_reduce(units_e[:], filled[:], AX.X, ALU.add))
            link(V.tensor_tensor_scan(last_e[:], ones_e[:], units_e[:], 0.0, ALU.mult, ALU.add))
            link(V.tensor_tensor(base_e[:], last_e[:], units_e[:], ALU.subtract))
            link(V.tensor_scalar(base_e[:], base_e[:], float(GT), None, ALU.mult))
            link(V.tensor_tensor(place[:], until[:], total[:], ALU.subtract))
            link(V.tensor_tensor(place[:], place[:], ranks(4), ALU.add))
            link(V.tensor_tensor(place[:], place[:], base_e[:].unsqueeze(2).broadcast_to([128, E, TILES]), ALU.add))
            for j in range(2):
                link(V.tensor_tensor(tmp[:], best[:, j], place.rearrange("p e n -> p n e"), ALU.mult))
                link(V.tensor_reduce(slot_f[:, :, j], tmp[:], AX.X, ALU.add))
            link(V.tensor_copy(slot.rearrange("p g s j -> p (g s) j"), slot_f[:]))
            link(V.tensor_tensor(passed_e[:], unit_no.unsqueeze(2).broadcast_to([128, UNITS, E]),
                                 last_e[:].unsqueeze(1).broadcast_to([128, UNITS, E]), ALU.is_ge))
            link(V.tensor_reduce(expert_f[:], passed_e[:], AX.X, ALU.add))
            link(V.tensor_scalar(expert_f[:], expert_f[:], float(E - 1), None, ALU.min))
            link(V.tensor_copy(expert_i[:], expert_f[:]))
            dve.sem_inc(placed, 1)

        def router_scalar(act):
            act.wait_ge(routed, 1)
            nc.scalar.activation(lg[:], lg[:], ACT.Exp, scale=1.0 if gated else -1.0).then_inc(exped, 1)
            if gated:
                act.wait_ge(routed, 2)
                nc.scalar.activation(top[:, 4], top[:, 4], ACT.Exp).then_inc(exped, 1)

        def to_list_pool(pl):
            if not gated:
                pl.wait_ge(rows["kept"], NG)
            pl.wait_ge(placed, 1)
            pl.wait_ge(listed, 16 * UNITS)

            def group(turn, p):
                g = 2 * turn + p
                after(pl, in_list[p], 16 * 2 * GS * turn)
                nc.gpsimd.tensor_copy(staged_rows[:, p], rows_full[:, g])
                nc.gpsimd.tensor_copy(slot_now[:, p], slot[:, g]).then_inc(staged, 1)
                pl.wait_ge(staged, g + 1)
                nc.gpsimd.tensor_tensor(mark[:], eps[:, 0:1], eps[:, 0:1], ALU.add)
                for k in range(GS):
                    for j in range(2):
                        nc.gpsimd.indirect_dma_start(
                            rows_by_expert, bass.IndirectOffsetOnAxis(slot_now[:, p, k, j:j + 1], 0),
                            staged_rows[:, p, k], None).then_inc(in_list[p], 16)

            group(0, 0)
            group(0, 1)
            with pl.Fori(0, NG // 2 - 1) as turn:
                group(turn + 1, 0)
                group(turn + 1, 1)

        def collect_pool(pl):
            for p in range(2):
                pl.wait_ge(y_out[p], 16 * ((UNITS + 1 - p) // 2 + 1))
            with pl.Fori(0, NG // 2) as pair:
                for p in range(2):
                    g = 2 * pair + p
                    pl.wait_ge(combined, g + 1)
                    nc.gpsimd.tensor_copy(slot_now[:, p], slot[:, g]).then_inc(asked, 1)
                    pl.wait_ge(asked, g + 1)
                    nc.gpsimd.tensor_tensor(mark[:], eps[:, 0:1], eps[:, 0:1], ALU.add)
                    for k in range(GS):
                        for j in range(2):
                            nc.gpsimd.indirect_dma_start(
                                y_got[:, p, k, j], None, out_by_expert,
                                bass.IndirectOffsetOnAxis(slot_now[:, p, k, j:j + 1], 0)).then_inc(got[p], 16)

        def collect_vector(dve):
            dve.sem_inc(combined, 2)
            with dve.Fori(0, NG // 2) as pair:
                for p in range(2):
                    g = 2 * pair + p
                    dve.wait_ge(combined, g + 2)
                    nc.vector.tensor_copy(share_now[:, p], share[:, g]).then_inc(share_set, 1)
                    dve.wait_ge(share_set, g + 1)
                    dve.wait_ge(got[p], 16 * 2 * GS * (pair + 1))
                    for j in range(2):
                        for k in range(GS):
                            step = nc.vector.scalar_tensor_tensor(
                                out=X[:, g, k], in0=y_got[:, p, k, j], scalar=share_now[:, p, k, j:j + 1], in1=X[:, g, k],
                                op0=ALU.mult, op1=ALU.add)
                        step.then_inc((halved, combined)[j], 1)
                        if j == 0:
                            dve.wait_ge(halved, g + 1)

        def output_tensor(pe, v, kind, at, p, r):
            for q in range(GS):
                if q == 0:
                    pe.wait_ge(hidden, v * FC + FC)
                    pe.wait_ge(taken, 2 * v + 1)
                if q == 2:
                    pe.wait_ge(taken, 2 * v + 2)
                if q == 0 and kind == "list":
                    wait_ring(pe, w_dn, at, r)
                for f in range(FC):
                    step = nc.tensor.matmul(DB[:, q], hid[:, p, f, q * L:q * L + L], w_down[:, r, f], start=f == 0, stop=f == FC - 1)
                if q % 2:
                    step.then_inc(down, 1)

        def wait_ring(pe, sems, j, r):
            extra = 1 if SHN and r == 0 else 0
            if isinstance(j, int):
                pe.wait_ge(sems[r], 16 * (j // 2 + 1 + extra))
            else:
                pe.wait_ge(sems[r], 8 * (j - (j_parity(r))) + 16 * (1 + extra))

        def j_parity(r):
            return 1 - r if SHN else r

        def ring_of(jp):
            return 1 - jp if SHN else jp

        def turn_rows(pe, j, jp):
            if isinstance(j, int):
                pe.wait_ge(row_in[jp], 16 * (j // 2 + 1))
            else:
                pe.wait_ge(row_in[jp], 8 * (j - jp) + 16)
            after(pe, turned_in, j)
            for c in range(KD):
                for k in range(GS):
                    step = nc.tensor.transpose(TB[:, c, k * L:k * L + L], unit_rows[:, jp, k, c * 128:c * 128 + 128], ident[:])
            step.then_inc(turned, 1)

        def unit_tensor(pe, u, kind, at, p, r, before, ahead):
            for f in range(FC):
                after(pe, hidden, u * FC + (f - 1))
                if f == 0 and kind == "list":
                    wait_ring(pe, w_gu, at, r)
                    pe.wait_ge(turned_in, at + 1)
                for b, wt in ((GB(f), w_gate), (UB(f), w_up))[:2 if gated else 1]:
                    for c in range(KD):
                        x = xT_g[:, c, at] if kind == "shared" else unit_T[:, p, c]
                        step = nc.tensor.matmul(b, wt[:, r, c, f * 128:f * 128 + 128], x, start=c == 0, stop=c == KD - 1)
                step.then_inc(full, 1)
                if f == 0 and before is not None:
                    output_tensor(pe, u - 1, *before)
                if f == 1 and ahead:
                    turn_rows(pe, at + 1, 1 - p)

        def take_rows(act, j, jp):
            act.wait_ge(turned, j + 1)
            for c in range(KD):
                step = nc.scalar.activation(unit_T[:, jp, c], TB[:, c], ACT.Copy, scale=vec[:, c:c + 1] if gated else 1.0)
            step.then_inc(turned_in, 1)

        def unit_scalar(act, u, kind, at, p, r, before, ahead):
            for f in range(FC):
                if gated:
                    after(act, hidden, u * FC + (f - 1))
                else:
                    after(act, down, 2 * u)
                act.wait_ge(full, u * FC + (f + 1))
                if gated:
                    nc.scalar.activation(act_b[:, f % 2], GB(f), ACT.Silu).then_inc(silued, 1)
                else:
                    nc.scalar.activation(hid[:, p, f], GB(f), ACT.Silu).then_inc(hidden, 1)
                if f == 1 and ahead:
                    take_rows(act, at + 1, 1 - p)

        def unit_vector(dve, u, kind, at, p, r, before, ahead):
            for f in range(FC):
                if gated:
                    if f == 0:
                        after(dve, down, 2 * u)
                    dve.wait_ge(silued, u * FC + (f + 1))
                    nc.vector.tensor_tensor(hid[:, p, f], act_b[:, f % 2], UB(f), ALU.mult).then_inc(hidden, 1)
                if f == 0 and before is not None:
                    output_vector(dve, u - 1, *before)

        def output_vector(dve, v, kind, at, p, r):
            if kind == "list":
                turns = 16 * (at // 2) if isinstance(at, int) else 8 * (at - p)
                dve.wait_ge(y_out[p], turns + 16)
            for h in range(2):
                dve.wait_ge(down, 2 * v + (h + 3))
                o = DB[:, 2 * h:2 * h + 2]
                if kind == "shared":
                    step = nc.vector.tensor_tensor(X[:, at, 2 * h:2 * h + 2], X[:, at, 2 * h:2 * h + 2], o, ALU.add)
                else:
                    step = nc.vector.tensor_copy(y_rows[:, p, 2 * h:2 * h + 2], o)
                step.then_inc(taken, 1)

        def run(eng, unit, output, first_rows):
            SHR = lambda g, gp: ("shared", g, gp, 0)
            LST = lambda j, jp: ("list", j, jp, ring_of(jp))
            if SHN:
                unit(eng, 0, *SHR(0, 0), None, False)
                with eng.Fori(0, NG // 2 - 1) as pair:
                    unit(eng, 2 * pair + 1, *SHR(2 * pair + 1, 1), SHR(2 * pair, 0), False)
                    unit(eng, 2 * pair + 2, *SHR(2 * pair + 2, 0), SHR(2 * pair + 1, 1), False)
                unit(eng, NG - 1, *SHR(NG - 1, 1), SHR(NG - 2, 0), False)
            first_rows(eng, 0, 0)
            unit(eng, SHN, *LST(0, 0), SHR(NG - 1, 1) if SHN else None, True)
            with eng.Fori(0, (UNITS - 3) // 2) as pair:
                j = 2 * pair + 1
                unit(eng, j + SHN, *LST(j, 1), LST(j - 1, 0), True)
                unit(eng, j + (SHN + 1), *LST(j + 1, 0), LST(j, 1), True)
            unit(eng, SHN + UNITS - 2, *LST(UNITS - 2, 1), LST(UNITS - 3, 0), True)
            unit(eng, SHN + UNITS - 1, *LST(UNITS - 1, 0), LST(UNITS - 2, 1), False)
            output(eng, SHN + UNITS - 1, *LST(UNITS - 1, 0))

        def load_rows(sp, j, jp):
            after(sp, turned, j - 1)
            sp.dma_start(unit_rows[:, jp], list_units[:, j]).then_inc(row_in[jp], 16)

        def load_weights(sp, j, r, expert, at_part):
            u = j + SHN
            if at_part == 0:
                after(sp, full, FC * (u - 1))
                sp.dma_start(w[:, r, 0:UPS], ins[f"{tag}_w"][expert][:, 0:UPS]).then_inc(w_gu[r], 16)
            else:
                sp.wait_ge(down, 2 * u)
                sp.dma_start(w[:, r, UPS:], ins[f"{tag}_w"][expert][:, UPS:]).then_inc(w_dn[r], 16)

        def store_out(sp, j, jp):
            sp.wait_ge(taken, 2 * (j + SHN) + 4)
            sp.dma_start(out_units[:, j], y_rows[:, jp]).then_inc(y_out[jp], 16)

        def expert_of(sp, j):
            return sp.value_load(expert_i[:].unsqueeze(2)[0:1, j], min_val=0, max_val=E - 1)

        def sync(sp):
            for dst, name in ((wr, "wr"), (vec, "v"), (const, "const")):
                sp.dma_start(dst[:], ins[f"{tag}_{name}"]).then_inc(loaded, 16)
            if SHN:
                sp.dma_start(w[:, 0, 0:UPS], ins[f"{tag}_w"][E][:, 0:UPS]).then_inc(w_gu[0], 16)
                sp.dma_start(w[:, 0, UPS:], ins[f"{tag}_w"][E][:, UPS:]).then_inc(w_dn[0], 16)
            sp.wait_ge(placed, 1)
            e = expert_of(sp, 0)
            for sems, lo, hi in ((w_gu, 0, UPS), (w_dn, UPS, WN)):
                sp.dma_start(w[:, ring_of(0), lo:hi], ins[f"{tag}_w"][e][:, lo:hi]).then_inc(sems[ring_of(0)], 16)
            for p in range(2):
                sp.wait_ge(in_list[p], 16 * 2 * GS * (NG // 2))
            load_rows(sp, 0, 0)

            def step(j, jp, store=True):
                load_rows(sp, j + 1, 1 - jp)
                e = expert_of(sp, j + 1)
                load_weights(sp, j + 1, ring_of(1 - jp), e, 0)
                load_weights(sp, j + 1, ring_of(1 - jp), e, 1)
                if store:
                    store_out(sp, j - 1, 1 - jp)

            step(0, 0, False)
            with sp.Fori(0, (UNITS - 3) // 2) as pair:
                step(2 * pair + 1, 1)
                step(2 * pair + 2, 0)
            step(UNITS - 2, 1)
            store_out(sp, UNITS - 2, 1)
            store_out(sp, UNITS - 1, 0)

        def tensor(pe):
            pe.wait_ge(loaded, 48)
            rows["tensor"](pe)
            router_tensor(pe)
            rank_tensor(pe)
            if SHN:
                pe.wait_ge(w_gu[0], 16)
                pe.wait_ge(w_dn[0], 16)
            run(pe, unit_tensor, output_tensor, turn_rows)

        def scalar(act):
            rows["scalar"](act)
            router_scalar(act)
            run(act, unit_scalar, lambda *a: None, take_rows)

        def vector(dve):
            dve.wait_ge(loaded, 48)
            nc.vector.memset(ones[:], 1.0)
            dve.sem_inc(logit_in, 2)
            dve.sem_inc(taken, 2)
            dve.sem_inc(down, 2)
            for p in range(2):
                dve.sem_inc(y_out[p], 16)
            rows["vector"](dve)
            router_vector(dve)
            run(dve, unit_vector, output_vector, lambda *a: None)
            dve.wait_ge(taken, 2 * (SHN + UNITS) + 2)
            collect_vector(dve)
            dve.wait_ge(combined, NG + 2)

        def pool(pl):
            rows["pool"](pl)
            to_list_pool(pl)
            collect_pool(pl)

        mem.end()
        return dict(sync=sync, tensor=tensor, scalar=scalar, vector=vector, pool=pool)

    h_mem = Stage(nc, ())
    H = h_mem.take("H", [128, NG, GS, D])
    z_mem = Stage(nc, ())
    zeros = z_mem.take("zeros", [128, GS, D])

    b_attn = attention("b", 1, ["ctx"], relu=True)
    c_attn = attention("c", 0, ["x"], rms=True, out_w=True)
    z_mem.end()
    experts0 = experts("d", 1, H, True, rows_by_expert, out_by_expert, listed)
    h_mem.end()
    recur = recurrence("r", 0)
    e_attn = attention("e", 1, ["x", "ctx"], out_w=True)
    experts1 = experts("f", 0, X, False, rows_by_expert, out_by_expert, listed)

    stages = [b_attn, c_attn, experts0, recur, e_attn, experts1]

    def pass_stage(eng, n):
        eng.drain().then_inc(passed[n], 1)
        eng.wait_ge(passed[n], 5)
        after(eng, cleared, n)
        eng.drain()

    block = ctx.enter_context(nc.Block())

    @block.sync
    def _(sp):
        sp.dma_start(ident[:], ins["ident"]).then_inc(setup, 16)
        for t, name in ((m_w_sb, "m_w"), (m_v_sb, "m_v"), (b_bc, "m_bbc"), (m_rows, "m_rows"), (selector, "m_sel")):
            sp.dma_start(t[:], ins[name]).then_inc(m_loaded, 16)
        for g in range(NG):
            sp.dma_start(X[:, g], ins["x"][g * GS:g * GS + GS].rearrange("s t d -> t s d")).then_inc(x_first[g] if g < 2 else x_rest, 16)
        for n, st in enumerate(stages):
            sp.sem_inc(passed[n], 1)
            sp.wait_ge(passed[n], 5)
            after(sp, cleared, n)
            sp.drain()
            st["sync"](sp)
            if n == 0:
                sp.wait_ge(zeroed, 1)
                with sp.Fori(0, UNITS) as u:
                    sp.dma_start(rows_by_expert.rearrange("(u r p) d -> p u r d", p=128, r=GS)[:, u], zeros[:]).then_inc(listed, 16)
        sp.sem_inc(passed[len(stages)], 1)
        sp.wait_ge(passed[len(stages)], 5)
        for g in range(NG):
            sp.dma_start(out[g * GS:g * GS + GS].rearrange("s t d -> t s d"), X[:, g]).then_inc(stored, 16)
        sp.wait_ge(stored, 16 * NG)

    @block.gpsimd
    def _(pool):
        nc.gpsimd.memset(eps[:], EPS)
        nc.gpsimd.memset(rms_eps[:], RMS_EPS)
        nc.gpsimd.memset(minus_one[:], -1.0)
        nc.gpsimd.memset(neg_half[:], -0.5).then_inc(setup, 1)
        mamba_setup_pool(pool)
        pool.wait_ge(setup, 17)
        mamba(pool, mamba_early_pool, mamba_late_pool, mamba_scan_pool, mamba_back_pool)
        for n, st in enumerate(stages):
            pass_stage(pool, n)
            pool.sem_clear(sem_set[n % 2])
            pool.drain().then_inc(cleared, 1)
            if n == 0:
                nc.gpsimd.memset(zeros[:], 0.0).then_inc(zeroed, 1)
            st["pool"](pool)
        pass_stage(pool, len(stages))

    @block.scalar
    def _(act):
        mamba_setup_scalar(act)
        act.wait_ge(m_half, 1)
        act.wait_ge(m_prep, 2)
        act.wait_ge(m_edge, 2)
        mamba(act, mamba_early_scalar, mamba_late_scalar, mamba_scan_scalar, mamba_back_scalar)
        for n, st in enumerate(stages):
            pass_stage(act, n)
            st["scalar"](act)
        pass_stage(act, len(stages))

    @block.vector
    def _(dve):
        mamba_setup_vector(dve)
        mamba(dve, mamba_early_vector, mamba_late_vector, mamba_scan_vector, mamba_back_vector)
        for n, st in enumerate(stages):
            pass_stage(dve, n)
            st["vector"](dve)
        pass_stage(dve, len(stages))

    @block.tensor
    def _(pe):
        pe.wait_ge(setup, 17)
        pe.wait_ge(m_loaded, 16 * 5)
        pe.wait_ge(m_skip, KD)
        mamba(pe, mamba_early_tensor, mamba_late_tensor, mamba_scan_tensor, mamba_back_tensor)
        for n, st in enumerate(stages):
            pass_stage(pe, n)
            st["tensor"](pe)
        pass_stage(pe, len(stages))

    ctx.close()


def kernel(**inputs):
    import ml_dtypes
    import concourse.bacc as bacc
    from concourse.bass_utils import run_bass_kernel_spmd as run

    a = {k: np.asarray(v) for k, v in inputs.items()}
    seqs_n = a["x"].shape[0]

    def rows_in(w):
        k = w.shape[0] // 128
        return w.reshape(k, 128, w.shape[1]).transpose(1, 0, 2).reshape(128, -1)

    def per_row(v):
        return v.reshape(v.shape[0] // 128, 128, -1).transpose(1, 0, 2).reshape(128, -1)

    def to_all(v):
        return np.broadcast_to(v.reshape(1, -1), (128, v.size))

    m = {k[8:]: v for k, v in a.items() if k.startswith("L0_attn_")}
    bc3 = np.concatenate([m["bc_w"].T] * 3, axis=1)
    selector = np.zeros((96, 32, 128), ml_dtypes.bfloat16)
    for n in range(32):
        selector[n::32, n] = 1
    arrays = {
        "x": a["x"],
        "ident": np.eye(128, dtype=np.float32),
        "m_w": np.concatenate([rows_in(m["in_proj_w"].T), rows_in(m["dt_w"].T), rows_in(m["out_w"].T), rows_in(bc3)], 1),
        "m_v": np.concatenate([per_row(m["in_proj_b"]), per_row(m["conv_w"][:, 0]), per_row(m["conv_b"]),
                               per_row(m["dt_b"]), per_row(m["A_log"]), per_row(m["D"])], 1),
        "m_bbc": np.concatenate([m["bc_b"]] * 3).reshape(96, 1),
        "m_rows": np.stack([to_all(m["out_b"]), to_all(m["ln_g"]), to_all(m["ln_b"])], 1),
        "m_sel": selector,
    }
    strip_mask = np.zeros((128, 8), np.float32)
    for e in range(8):
        strip_mask[np.arange(128) // 16 == e, e] = 16 ** -0.5
    groups = seqs_n // GS
    arrays |= {
        "ctxT": a["ctx_1024"].transpose(2, 0, 1).reshape(2, 128, groups, GS * 128).transpose(1, 0, 2, 3),
        "b_wq": rows_in(a["L0_xattn_Wq"].T), "b_wk0": rows_in(a["L0_xattn_Wk"].T), "b_wv0": rows_in(a["L0_xattn_Wv"].T),
        "b_mask": strip_mask,
    }
    f = {k[7:]: v for k, v in a.items() if k.startswith("L0_ffn_")}
    arrays |= {
        "c_wq": rows_in(f["wq"]), "c_wk0": rows_in(f["wk"]), "c_wv0": rows_in(f["wv"]), "c_wo": rows_in(f["wo"]),
        "c_norm": per_row(f["norm1_w"]), "c_mask": strip_mask,
    }
    e = {k[9:]: v for k, v in a.items() if k.startswith("L1_xattn_")}
    wq, wk, wv = np.split(e["Wqkv"], 3, axis=1)
    _, wka, wva = np.split(e["Wqkv_aux"], 3, axis=1)
    bq, bk, bv = np.split(e["bqkv"], 3)
    _, bka, bva = np.split(e["bqkv_aux"], 3)
    arrays |= {
        "e_wq": rows_in(wq), "e_wk0": rows_in(wk), "e_wv0": rows_in(wv), "e_wk1": rows_in(wka), "e_wv1": rows_in(wva),
        "e_wo": rows_in(e["Wo"]), "e_bq": per_row(bq), "e_bk0": per_row(bk), "e_bk1": per_row(bka),
        "e_bv0": to_all(bv), "e_bv1": to_all(bva), "e_bo": to_all(e["bo"]), "e_gate": to_all(e["g"]), "e_mask": strip_mask,
    }
    r = {k[8:]: v for k, v in a.items() if k.startswith("L1_attn_")}
    arrays |= {"r_wi": rows_in(r["Wi"].T), "r_wh": rows_in(r["Wh"].T),
               "r_b": np.concatenate([per_row(r["bi"]), per_row(r["bh"])], 1)}
    experts = lambda parts: np.stack([np.concatenate([rows_in(w[e]) for w in parts], 1) for e in range(8)])
    consts = np.concatenate([np.triu(np.ones((128, 128), np.float32), 1), to_all(np.arange(8, 0, -1, dtype=np.float32)),
                             to_all(np.arange(groups, dtype=np.float32) * GT),
                             to_all(np.arange(units_of_list(groups), dtype=np.float32))], 1)
    shared = np.concatenate([rows_in(f[n]) for n in ("sh_gate", "sh_up", "sh_down")], 1)
    n = {k[7:]: v for k, v in a.items() if k.startswith("L1_ffn_")}
    arrays |= {
        "d_w": np.concatenate([experts([f["e_gate"], f["e_up"], f["e_down"]]), shared[None]]), "d_wr": rows_in(f["router_w"]),
        "d_v": per_row(f["norm2_w"]), "d_const": consts,
        "f_w": experts([n["w1"].transpose(0, 2, 1), n["w2"].transpose(0, 2, 1)]), "f_wr": rows_in(n["gate_w"].T),
        "f_v": to_all(n["balance_bias"]), "f_const": consts,
    }
    nc = bacc.Bacc("TRN2", target_bir_lowering=False, num_devices=1)
    fed, ins = {}, {}
    for name, v in arrays.items():
        v = np.ascontiguousarray(v)
        fed[f"in_{name}"] = v
        ins[name] = nc.dram_tensor(f"in_{name}", v.shape, mybir.dt.from_np(v.dtype), kind="ExternalInput").ap()
    out = nc.dram_tensor("out_0", a["x"].shape, F32, kind="ExternalOutput").ap()
    decoder_kernel(nc, ins, out)
    r = run(nc, [fed], core_ids=[0])
    return r.results[0]["out_0"]
```

```python
import numpy as np

import concourse.bass as bass
from concourse import mybir
from contextlib import ExitStack

F32 = mybir.dt.float32
BF16 = mybir.dt.bfloat16
U32 = mybir.dt.uint32
I32 = mybir.dt.int32
ALU = mybir.AluOpType
ACT = mybir.ActivationFunctionType
AX = mybir.AxisListType


def after(eng, sem, count):
    if not isinstance(count, int) or count > 0:
        eng.wait_ge(sem, count)


def weave(main, side):
    due = next(side, None)
    for step in main:
        while due is not None and due <= step:
            due = next(side, None)
    while due is not None:
        due = next(side, None)


def alone(side):
    for _ in side:
        pass


def merged(*sides):
    heads = [next(s, None) for s in sides]
    while any(h is not None for h in heads):
        n = min((h, n) for n, h in enumerate(heads) if h is not None)[1]
        yield heads[n]
        heads[n] = next(sides[n], None)


class Chain:

    def __init__(self, eng, sem, per, turn):
        self.eng, self.sem, self.per, self.turn, self.k = eng, sem, per, turn, 0

    def __call__(self, step):
        self.k += 1
        assert self.k <= self.per
        step.then_inc(self.sem, 1)
        self.eng.wait_ge(self.sem, self.turn * self.per + self.k)

    def turn_over(self):
        assert self.k == self.per, (self.k, self.per)


class Stage:

    def __init__(self, nc, numbers):
        self.nc, self.stack, self.numbers, self.left = nc, ExitStack(), numbers, list(numbers)

    def take(self, name, shape, dtype=F32):
        return self.stack.enter_context(self.nc.sbuf_tensor(name, shape, dtype))

    def sem(self, name):
        return self.stack.enter_context(self.nc.semaphore(name, num=self.left.pop(0)))

    def gpsimd_sem(self, name):
        return self.stack.enter_context(self.nc.semaphore(name, num=self.left.pop()))

    def end(self):
        self.stack.close()


def flat(a):
    return a.rearrange("p a b -> p (a b)")


EPS, TINY = 1e-5, 1e-30
D, L, KD, NS = 256, 128, 2, 16
GS = 4
GT = GS * L
STAGES, SET = 6, 60


UR = 256


def units_of_list(groups):
    return (2 * groups * GT - 8) // UR + 8


NH, DH = 16, 16
RMS_EPS = 1e-6


def heads(a):
    return a.rearrange("p (h d) -> p h d", h=NH)


def seqs(a):
    return a.rearrange("p (s t) -> p s t", s=GS)


def decoder_kernel(nc, ins, out):
    NG = ins["x"].shape[0] // GS
    ctx = ExitStack()

    def sem(name):
        return ctx.enter_context(nc.semaphore(name))

    def keep(name, shape, dtype=F32):
        return ctx.enter_context(nc.sbuf_tensor(name, shape, dtype))

    X = keep("X", [128, NG, GS, D])
    ident = keep("ident", [128, 128])
    neg_half, eps = keep("neg_half", [128, 16]), keep("eps", [128, 16])
    rms_eps, minus_one = keep("rms_eps", [128, 16]), keep("minus_one", [128, 16])
    PS = ctx.enter_context(nc.psum_tensor("PS", [128, 8, 512], F32))
    x_first, x_rest = [sem("x_first0"), sem("x_first1")], sem("x_rest")
    setup, stored = sem("setup"), sem("stored")
    cleared, zeroed, listed = sem("cleared"), sem("zeroed"), sem("listed")
    UNITS = units_of_list(NG)
    rows_by_expert = nc.dram_tensor("rows_by_expert", (UNITS * UR, D), F32, kind="Internal").ap()
    out_by_expert = nc.dram_tensor("out_by_expert", (UNITS * UR, D), F32, kind="Internal").ap()
    passed = [sem(f"passed{n}") for n in range(STAGES)]
    own = passed[-1].num + 1
    sem_set = [range(own, own + SET), range(own + SET, own + 2 * SET)]

    mamba_mem = Stage(nc, sem_set[0])
    m_w_sb = mamba_mem.take("m_w", [128, 2240])
    w_in = m_w_sb[:, 0:1024].rearrange("p (k o) -> p k o", k=KD)
    w_dt = m_w_sb[:, 1024:1536].rearrange("p (k o) -> p k o", k=KD)
    w_out = m_w_sb[:, 1536:2048].rearrange("p (k o) -> p k o", k=KD)
    w_bc = m_w_sb[:, 2048:2240].rearrange("p (k o) -> p k o", k=KD)
    m_v_sb = mamba_mem.take("m_v", [128, 50])
    b_in, cw, cb = m_v_sb[:, 0:4], m_v_sb[:, 4:12], m_v_sb[:, 12:14]
    b_dt, a_log, d_skip = m_v_sb[:, 14:16], m_v_sb[:, 16:48], m_v_sb[:, 48:50]
    b_bc = mamba_mem.take("b_bc", [96, 1])
    m_rows = mamba_mem.take("m_rows", [128, 3, D])
    selector = mamba_mem.take("selector", [96, 2 * NS, 128], BF16)
    decay_rate = mamba_mem.take("decay_rate", [128, KD * NS])
    half_v = mamba_mem.take("half_v", [128, 14])
    hb_in, hcw, hcb = half_v[:, 0:4], half_v[:, 4:12], half_v[:, 12:14]

    RD, RU, RC, RB = 4, 4, 4, 4
    xn = mamba_mem.take("xn", [128, 2, GS, D])
    xnb = mamba_mem.take("xnb", [128, 2, GS, D])
    xnT = mamba_mem.take("xnT", [128, 2, KD, GT])
    xpad = mamba_mem.take("xpad", [128, KD, GS, L + 3])
    half_conv = mamba_mem.take("half_conv", [128, KD, GS, L])
    conv_tanh = mamba_mem.take("conv_tanh", [128, KD * GT])
    xconv = mamba_mem.take("xconv", [128, 2, KD, GT])
    half_gate = mamba_mem.take("half_gate", [128, KD, GT])
    gate_tanh = mamba_mem.take("gate_tanh", [128, KD, GT])
    gate = mamba_mem.take("gate", [128, 2, KD * GT])
    bc96 = mamba_mem.take("bc96", [96, GT])
    bc_rest = mamba_mem.take("bc_rest", [64, GT])
    bc16 = mamba_mem.take("bc16", [96, 2, GT], BF16)
    dt_pre = mamba_mem.take("dt_pre", [128, KD * GT])
    dt_e = mamba_mem.take("dt_e", [128, KD * GT])
    dt_u = mamba_mem.take("dt_u", [128, KD * GT])
    dt_l = mamba_mem.take("dt_l", [128, KD * GT])
    dt_c = mamba_mem.take("dt_c", [128, KD * GT])
    dt = mamba_mem.take("dt", [128, 2, KD, GT])
    dtx = mamba_mem.take("dtx", [128, 2, KD, GT])
    b_rep = mamba_mem.take("b_rep", [128, RB, GT])
    decay = mamba_mem.take("decay", [128, RD, GS, L])
    u_in = mamba_mem.take("u_in", [128, RU, GT])
    state = mamba_mem.take("state", [128, 2, GT])
    scaled = mamba_mem.take("scaled", [128, RC, GT])
    skip_w = mamba_mem.take("skip_w", [128, KD, 128])
    bc_mid = mamba_mem.take("bc_mid", [32, GT])
    y_gated = mamba_mem.take("y_gated", [128, KD, GT])
    z_row = mamba_mem.take("z_row", [128, GS, D])
    z_norm = mamba_mem.take("z_norm", [128, GS, D])
    spare = mamba_mem.take("spare", [128, 1])
    stat = mamba_mem.take("stat", [128, 2, GS, 6])
    mv = mamba_mem.take("mv", [128, 2, GS, 2])
    rst = mamba_mem.take("rst", [128, 2, 4, GS])

    FB, BB, CB, YB = PS[:, 0:2], PS[:, 2:4], PS[:, 4:6], PS[:, 6:8]
    m_loaded, m_prep, m_edge = mamba_mem.sem("m_loaded"), mamba_mem.sem("m_prep"), mamba_mem.sem("m_edge")
    m_half, m_skip = mamba_mem.sem("m_half"), mamba_mem.sem("m_skip")
    m_vec, m_vec3, m_pool = mamba_mem.sem("m_vec"), mamba_mem.sem("m_vec3"), mamba_mem.sem("m_pool")
    m_vec2, m_pool2 = mamba_mem.sem("m_vec2"), mamba_mem.sem("m_pool2")
    m_mv, m_nb, m_xn, m_tr, m_fev1, m_fev2, m_xnb = map(
        mamba_mem.sem, ("m_mv", "m_nb", "m_xn", "m_tr", "m_fev1", "m_fev2", "m_xnb"))
    m_ip, m_ipg, m_gate, m_conv, m_th, m_xc, m_bcp, m_bcs, m_br = map(
        mamba_mem.sem, ("m_ip", "m_ipg", "m_gate", "m_conv", "m_th", "m_xc", "m_bcp", "m_bcs", "m_br"))
    m_dtp, m_e, m_u1, m_ln, m_q, m_dt, m_dtx = map(
        mamba_mem.sem, ("m_dtp", "m_e", "m_u1", "m_ln", "m_q", "m_dt", "m_dtx"))
    m_bb, m_cb, m_brep, m_da, m_u, m_h, m_hc, m_y = map(
        mamba_mem.sem, ("m_bb", "m_cb", "m_brep", "m_da", "m_u", "m_h", "m_hc", "m_y"))
    m_abs, m_yg, m_op, m_z, m_mv2, m_nb2, m_zn, m_zb, m_x = map(
        mamba_mem.sem, ("m_abs", "m_yg", "m_op", "m_z", "m_mv2", "m_nb2", "m_zn", "m_zb", "m_x"))

    NU = KD * NS
    LA = 3
    EV1, EV2 = 3, 5

    def rstd_of(pool, turn, which, chain, counted, done):
        after(pool, counted, turn + 1)
        m, r = mv[:, which], rst[:, which]
        chain(nc.gpsimd.tensor_tensor(r[:, 0], m[:, :, 1], eps[:, 0:GS], ALU.add))
        chain(nc.gpsimd.tensor_tensor(r[:, 1], r[:, 0], neg_half[:, 0:GS], ALU.pow))
        chain(nc.gpsimd.tensor_tensor(r[:, 2], m[:, :, 0], r[:, 1], ALU.mult))
        nc.gpsimd.tensor_tensor(r[:, 3], r[:, 2], minus_one[:, 0:GS], ALU.mult).then_inc(done, 1)

    def mamba_setup_scalar(act):
        act.wait_ge(m_loaded, 16 * 5)
        nc.scalar.activation(decay_rate[:], a_log, ACT.Exp).then_inc(m_prep, 1)

    def mamba_setup_vector(dve):
        dve.sem_inc(m_z, 1)
        dve.wait_ge(m_loaded, 16 * 5)
        dve.wait_ge(setup, 17)
        for c in range(KD):
            nc.vector.tensor_scalar(skip_w[:, c], ident[:], d_skip[:, c:c + 1], None, ALU.mult).then_inc(m_skip, 1)
        dve.wait_ge(m_half, 1)
        dve.wait_ge(m_edge, 2)

    def mamba_setup_pool(pool):
        nc.gpsimd.memset(decay[:], 0.0).then_inc(m_edge, 1)
        nc.gpsimd.memset(xpad[:], 0.0).then_inc(m_edge, 1)
        pool.wait_ge(m_loaded, 16 * 5)
        nc.gpsimd.tensor_scalar(half_v[:], m_v_sb[:, 0:14], 0.5, None, ALU.mult).then_inc(m_half, 1)
        pool.wait_ge(m_prep, 1)
        nc.gpsimd.tensor_scalar(decay_rate[:], decay_rate[:], -1.0, None, ALU.mult).then_inc(m_prep, 1)

    def mamba_early_vector(dve, g, p):
        link = Chain(dve, m_vec, 1, g)
        yield 14
        if isinstance(g, int) and g < 2:
            dve.wait_ge(x_first[g], 16)
        else:
            dve.wait_ge(x_rest, 16 * (NG - 2))
        for s in range(GS):
            step = nc.vector.bn_stats(stat[:, 0, s], X[:, g, s])
        link(step)
        after(dve, m_nb, g)
        nc.vector.tensor_copy(spare[:], eps[:, 0:1])
        for s in range(GS):
            step = nc.vector.bn_aggr(mv[:, 0, s], stat[:, 0, s])
        step.then_inc(m_mv, 1)

    def mamba_early_pool(pool, g, p):
        yield 17
        rstd_of(pool, g, 0, Chain(pool, m_pool, 3, g), m_mv, m_nb)

    def mamba_early_scalar(act, g, p):
        yield 21
        after(act, m_nb, g + 1)
        after(act, m_xnb, g - 1)
        for s in range(GS):
            step = nc.scalar.activation(xn[:, p, s], X[:, g, s], ACT.Identity, bias=rst[:, 0, 3, s:s + 1],
                                        scale=rst[:, 0, 1, s:s + 1])
        step.then_inc(m_xn, 1)
        yield 30
        after(act, m_tr, g + 1)
        after(act, m_ipg, 2 * g - 2)
        nc.scalar.activation(flat(xnT[:, p]), flat(FB), ACT.Copy).then_inc(m_fev1, 1)
        yield 31
        for m in range(2):
            after(act, m_ip, 2 * g + m + 1)
            after(act, m_conv, KD * g - KD + m + 1 if not isinstance(g, int) or g else 0)
            nc.scalar.activation(xpad[:, m, :, 3:L + 3], seqs(FB[:, m]), ACT.Identity,
                                 bias=b_in[:, m:m + 1]).then_inc(m_fev1, 1)

    def mamba_early_tensor(pe, g, p):
        yield 22
        after(pe, m_xn, g + 1)
        after(pe, m_fev2, EV2 * g)
        for c in range(KD):
            for s in range(GS):
                step = nc.tensor.transpose(FB[:, c, s * L:s * L + L], xn[:, p, s, c * 128:c * 128 + 128], ident[:])
        step.then_inc(m_tr, 1)
        yield 26
        after(pe, m_fev1, EV1 * g + 1)
        for m in range(2):
            for c in range(KD):
                step = nc.tensor.matmul(FB[:, m], w_in[:, c, m * 128:m * 128 + 128], xnT[:, p, c],
                                        start=c == 0, stop=c == KD - 1)
            step.then_inc(m_ip, 1)

    def mamba_late_vector(dve, g, p):
        link = Chain(dve, m_vec3, 7, g)
        for c in range(KD):
            yield 2 + 2 * c
            after(dve, m_fev1, EV1 * g + 2 + c)
            after(dve, m_th, g)
            link(nc.vector.tensor_scalar(half_conv[:, c], xpad[:, c, :, 0:L], hcw[:, 4 * c:4 * c + 1],
                                         hcb[:, c:c + 1], ALU.mult, ALU.add))
            for j in range(1, 4):
                step = nc.vector.scalar_tensor_tensor(
                    out=half_conv[:, c], in0=xpad[:, c, :, j:j + L], scalar=hcw[:, 4 * c + j:4 * c + j + 1],
                    in1=half_conv[:, c], op0=ALU.mult, op1=ALU.add)
                if j < 3:
                    link(step)
            step.then_inc(m_conv, 1)
        yield 8
        after(dve, m_th, g + 1)
        after(dve, m_conv, KD * g + KD)
        nc.vector.scalar_tensor_tensor(out=flat(xconv[:, p]), in0=conv_tanh[:], scalar=1.0,
                                       in1=half_conv.rearrange("p c s t -> p (c s t)"),
                                       op0=ALU.add, op1=ALU.mult).then_inc(m_xc, 1)
        yield 21
        after(dve, m_e, g + 1)
        nc.vector.tensor_scalar(dt_u[:], dt_e[:], 1.0, None, ALU.add).then_inc(m_u1, 1)
        yield 18
        dve.wait_ge(m_u1, g + 1)
        nc.vector.scalar_tensor_tensor(out=dt_c[:], in0=dt_u[:], scalar=1.0, in1=dt_e[:],
                                       op0=ALU.subtract, op1=ALU.subtract).then_inc(m_q, 1)
        yield 24
        after(dve, m_fev2, EV2 * g + 5)
        link(nc.vector.scalar_tensor_tensor(out=gate[:, p], in0=flat(gate_tanh), scalar=1.0, in1=flat(half_gate),
                                            op0=ALU.add, op1=ALU.mult))
        yield 25
        after(dve, m_ln, g + 1)
        nc.vector.scalar_tensor_tensor(out=dt_l[:], in0=dt_pre[:], scalar=0.0, in1=dt_l[:],
                                       op0=ALU.max, op1=ALU.add).then_inc(m_q, 1)
        link.turn_over()

    def mamba_late_pool(pool, g, p):
        yield 10
        after(pool, m_xn, g + 1)
        after(pool, m_z, g)
        nc.gpsimd.tensor_tensor(xnb[:, p], xn[:, p], m_rows[:, 0:1].broadcast_to([128, GS, D]),
                                ALU.add).then_inc(m_xnb, 1)
        yield 16
        after(pool, m_bcs, 3 * g + 1)
        nc.gpsimd.tensor_tensor(bc_rest[:], bc96[0:64], bc16[0:64, p], ALU.subtract).then_inc(m_br, 1)
        yield 19
        after(pool, m_bcs, 3 * g + 2)
        nc.gpsimd.tensor_tensor(bc_mid[:], bc_rest[0:32], bc16[0:32, p], ALU.subtract).then_inc(m_br, 1)
        yield 27
        after(pool, m_q, 2 * g + 2)
        after(pool, m_h, NU * g - NU)
        nc.gpsimd.tensor_tensor(flat(dt[:, p]), dt_l[:], dt_c[:], ALU.subtract).then_inc(m_dt, 1)
        yield 30
        pool.wait_ge(m_dt, g + 1)
        nc.gpsimd.tensor_tensor(dtx[:, p], dt[:, p], xconv[:, p], ALU.mult).then_inc(m_dtx, 1)

    def mamba_late_scalar(act, g, p):
        yield 9
        after(act, m_conv, KD * g + KD)
        nc.scalar.activation(conv_tanh[:], half_conv.rearrange("p c s t -> p (c s t)"), ACT.Tanh).then_inc(m_th, 1)
        yield 13
        after(act, m_bcp, g + 1)
        after(act, m_br, 2 * g)
        after(act, m_cb, NS * g - NS)
        nc.scalar.activation(bc96[:], PS[0:96, 0], ACT.Identity, bias=b_bc[:])
        nc.scalar.activation(bc16[:, p], PS[0:96, 0], ACT.Identity, bias=b_bc[:]).then_inc(m_bcs, 1)
        act.wait_ge(m_bcs, 3 * g + 1)
        act.sem_inc(m_fev2, 1)
        for m in range(KD):
            yield 16 + 3 * m
            after(act, m_dtp, KD * g + m + 1)
            after(act, m_dt, g)
            nc.scalar.activation(dt_pre[:, m * GT:m * GT + GT], FB[:, 1 - m], ACT.Identity,
                                 bias=b_dt[:, m:m + 1]).then_inc(m_fev2, 1)
        yield 20
        after(act, m_br, 2 * g + 1)
        nc.scalar.activation(bc16[0:64, p], bc_rest[:], ACT.Copy).then_inc(m_bcs, 1)
        yield 21
        act.wait_ge(m_fev2, EV2 * g + 3)
        nc.scalar.activation(dt_e[:], dt_pre[:], ACT.Abs).then_inc(m_abs, 1)
        act.wait_ge(m_abs, g + 1)
        nc.scalar.activation(dt_e[:], dt_e[:], ACT.Exp, scale=-1.0).then_inc(m_e, 1)
        yield 22
        after(act, m_br, 2 * g + 2)
        nc.scalar.activation(bc16[0:32, p], bc_mid[:], ACT.Copy).then_inc(m_bcs, 1)
        for m in range(2):
            yield 18
            after(act, m_ipg, 2 * g + m + 1)
            after(act, m_vec3, 7 * g)
            nc.scalar.activation(half_gate[:, m], FB[:, 1 - m], ACT.Identity, bias=hb_in[:, 2 + m:3 + m], scale=0.5)
            nc.scalar.activation(gate_tanh[:, m], FB[:, 1 - m], ACT.Tanh, bias=hb_in[:, 2 + m:3 + m],
                                 scale=0.5).then_inc(m_fev2, 1)
        yield 25
        after(act, m_u1, g + 1)
        nc.scalar.activation(dt_l[:], dt_u[:], ACT.Ln).then_inc(m_ln, 1)

    def mamba_late_tensor(pe, g, p):
        yield 7
        after(pe, m_xc, g + 1)
        after(pe, m_z, g)
        after(pe, m_fev1, EV1 * g + 3)
        for c in range(KD):
            step = nc.tensor.matmul(PS[0:96, 0], w_bc[:, c], xconv[:, p, c], start=c == 0, stop=c == KD - 1)
        step.then_inc(m_bcp, 1)
        for m in range(KD):
            yield 9 + 3 * m
            after(pe, m_fev2, EV2 * g + m)
            for c in range(KD):
                step = nc.tensor.matmul(FB[:, 1 - m], w_dt[:, c, m * 128:m * 128 + 128], xconv[:, p, c],
                                        start=c == 0, stop=c == KD - 1)
            step.then_inc(m_dtp, 1)
        for m in range(2):
            yield 16 + m
            after(pe, m_fev2, EV2 * g + 2 + m)
            for c in range(KD):
                step = nc.tensor.matmul(FB[:, 1 - m], w_in[:, c, 256 + m * 128:384 + m * 128], xnT[:, p, c],
                                        start=c == 0, stop=c == KD - 1)
            step.then_inc(m_ipg, 1)

    def mamba_scan_tensor(pe, g, p):
        def rep_b(n):
            if n >= NS:
                after(pe, m_bcs, 3 * g + 6)
            after(pe, m_brep, NS * g + n - 1)
            nc.tensor.matmul(BB[:, n % 2], selector[:, n % NS], bc16[:, p if n < NS else 1 - p], start=True, stop=True).then_inc(m_bb, 1)

        def rep_c(n):
            after(pe, m_hc, KD * (NS * g + n - 1))
            nc.tensor.matmul(CB[:, n % 2], selector[:, NS + n % NS], bc16[:, p if n < NS else 1 - p], start=True, stop=True).then_inc(m_cb, 1)

        last = isinstance(g, int) and g == NG - 1
        if isinstance(g, int) and g == 0:
            after(pe, m_bcs, 3)
            for n in range(LA):
                rep_b(n)
                if n < 2:
                    rep_c(n)
        after(pe, m_yg, g)
        for c in range(KD):
            nc.tensor.matmul(YB[:, c], skip_w[:, c], xconv[:, p, c], start=True, stop=False)
        for n in range(NS):
            if n + LA < NS or not last:
                rep_b(n + LA)
            for c in range(KD):
                unit = NU * g + KD * n + c
                after(pe, m_hc, unit + 1)
                nc.tensor.matmul(YB[:, c], ident[:], scaled[:, (KD * n + c) % RC], start=False,
                                 stop=n == NS - 1).then_inc(m_y, 1)
                if c == KD - 1 and (n + 2 < NS or not last):
                    rep_c(n + 2)
                yield KD * n + c

    def mamba_scan_scalar(act, g, p):
        def copy_b(n):
            after(act, m_bb, NS * g + n + 1)
            after(act, m_u, KD * (NS * g + n - RB + 1))
            nc.scalar.activation(b_rep[:, n % RB], BB[:, n % 2], ACT.Copy).then_inc(m_brep, 1)

        after(act, m_dt, g + 1)
        for n in range(NS):
            copy_b(n)
            for c in range(KD):
                k = KD * n + c
                after(act, m_h, NU * g + k - RD + 1)
                nc.scalar.activation(decay[:, k % RD, :, 1:L], seqs(dt[:, p, c])[:, :, 1:L], ACT.Exp,
                                     scale=decay_rate[:, c * NS + n:c * NS + n + 1]).then_inc(m_da, 1)
                yield k

    def mamba_scan_pool(pool, g, p):
        after(pool, m_dtx, g + 1)
        for n in range(NS):
            after(pool, m_brep, NS * g + n + 1)
            for c in range(KD):
                k = KD * n + c
                after(pool, m_h, NU * g + k - RU + 1)
                nc.gpsimd.tensor_tensor(u_in[:, k % RU], dtx[:, p, c], b_rep[:, n % RB],
                                        ALU.mult).then_inc(m_u, 1)
                yield k

    def mamba_scan_vector(dve, g, p):
        def scale_by_c(k):
            n = k // KD
            after(dve, m_h, NU * g + k + 1)
            after(dve, m_cb, NS * g + n + 1)
            after(dve, m_y, NU * g + k - RC + 1)
            nc.vector.tensor_tensor(scaled[:, k % RC], state[:, k % 2], CB[:, n % 2], ALU.mult).then_inc(m_hc, 1)

        for k in range(NU):
            after(dve, m_da, NU * g + k + 1)
            after(dve, m_u, NU * g + k + 1)
            after(dve, m_hc, NU * g + k - 1)
            nc.vector.tensor_tensor_scan(state[:, k % 2], decay[:, k % RD].rearrange("p s t -> p (s t)"), u_in[:, k % RU],
                                         0.0, ALU.mult, ALU.add).then_inc(m_h, 1)
            if k:
                scale_by_c(k - 1)
            yield k
        scale_by_c(NU - 1)

    def mamba_back_vector(dve, g, p):
        link = Chain(dve, m_vec2, 1, g)
        yield 1
        after(dve, m_op, g)
        after(dve, m_y, NU * g + NU)
        nc.vector.tensor_tensor(flat(y_gated), flat(YB), gate[:, p], ALU.mult).then_inc(m_yg, 1)
        yield 6
        after(dve, m_op, g + 1)
        after(dve, m_zn, g)
        nc.vector.tensor_tensor(flat(z_row), flat(FB), flat(xnb[:, p]), ALU.add).then_inc(m_z, 1)
        dve.wait_ge(m_z, g + 2)
        for s in range(GS):
            step = nc.vector.bn_stats(stat[:, 1, s], z_row[:, s])
        link(step)
        after(dve, m_nb2, g)
        nc.vector.tensor_copy(spare[:], eps[:, 0:1])
        for s in range(GS):
            step = nc.vector.bn_aggr(mv[:, 1, s], stat[:, 1, s])
        step.then_inc(m_mv2, 1)
        yield 16
        after(dve, m_zb, g + 1)
        nc.vector.tensor_tensor(X[:, g], X[:, g], z_norm[:], ALU.add).then_inc(m_x, 1)

    def mamba_back_tensor(pe, g, p):
        yield 1
        after(pe, m_yg, g + 1)
        after(pe, m_fev1, EV1 * (g + 3) if not isinstance(g, int) else EV1 * min(g + 3, NG))
        after(pe, m_fev2, EV2 * (g + 2) if not isinstance(g, int) else EV2 * min(g + 2, NG))
        after(pe, m_z, g + 1)
        for s in range(GS):
            for c in range(KD):
                step = nc.tensor.matmul(flat(FB)[:, s * D:s * D + D], y_gated[:, c, s * L:s * L + L],
                                        w_out[:, c], start=c == 0, stop=c == KD - 1)
        step.then_inc(m_op, 1)

    def mamba_back_scalar(act, g, p):
        yield 12
        after(act, m_nb2, g + 1)
        after(act, m_x, g)
        for s in range(GS):
            step = nc.scalar.activation(z_norm[:, s], z_row[:, s], ACT.Identity, bias=rst[:, 1, 3, s:s + 1],
                                        scale=rst[:, 1, 1, s:s + 1])
        step.then_inc(m_zn, 1)

    def mamba_back_pool(pool, g, p):
        yield 11
        link = Chain(pool, m_pool2, 4, g)
        rstd_of(pool, g, 1, link, m_mv2, m_nb2)
        yield 13
        after(pool, m_zn, g + 1)
        link(nc.gpsimd.tensor_tensor(z_norm[:], z_norm[:], m_rows[:, 1:2].broadcast_to([128, GS, D]), ALU.mult))
        yield 11
        nc.gpsimd.tensor_tensor(z_norm[:], z_norm[:], m_rows[:, 2:3].broadcast_to([128, GS, D]),
                                ALU.add).then_inc(m_zb, 1)
        link.turn_over()

    def mamba(eng, early, late, scan, back):
        def turn(g, p):
            sides = []
            if not isinstance(g, int) or g > 0:
                sides.append(back(eng, g - 1, 1 - p))
            if not isinstance(g, int) or g + 1 < NG:
                sides.append(late(eng, g + 1, 1 - p))
            if not isinstance(g, int) or g + 2 < NG:
                sides.append(early(eng, g + 2, p))
            weave(scan(eng, g, p), merged(*sides))

        alone(early(eng, 0, 0))
        alone(late(eng, 0, 0))
        alone(early(eng, 1, 1))
        turn(0, 0)
        turn(1, 1)
        with eng.Fori(0, (NG - 4) // 2) as pair:
            turn(2 * pair + 2, 0)
            turn(2 * pair + 3, 1)
        turn(NG - 2, 0)
        turn(NG - 1, 1)
        alone(back(eng, NG - 1, 1))
    mamba_mem.end()

    SH = NH // KD
    WHEN = {
        "b": ([3, 4, 6, 9, 11, 12, 15, 18], [5.0, 5, 7.9, 10.1, 12.0, 14.9, 15.8, 19.1],
              [], [], 2),
        "c": ([11, 12, 12, 12, 14, 15, 16, 18], [11.2, 12.8, 12.9, 13.9, 14.3, 16.9, 17.0, 19.9],
              [3, 6, 8, 9], [3.4, 6.1], 10),
        "e": ([5, 8, 11, 14, 18, 21, 24, 27, 32, 35, 37, 41], [5.9, 8.8, 13.9, 15.8, 18.9, 21.1, 24.1, 27.1, 34.8, 36.9, 37.9, 43.6],
              [6, 9, 11, 17], [6.9, 10.9], 4),
    }

    def attention(tag, turn, sets, relu=False, rms=None, out_w=None):
        A = len(sets)
        UNITS = GS * A * KD
        mem = Stage(nc, sem_set[turn])
        t = lambda name, shape, dtype=F32: mem.take(f"{tag}_{name}", shape, dtype)
        s = lambda name: mem.sem(f"{tag}_{name}")
        wide = {"wq": KD * D}
        for a in range(A):
            wide |= {f"wk{a}": KD * D, f"wv{a}": KD * D}
        if out_w:
            wide["wo"] = KD * D
        w = {name: t(name, [128, n]) for name, n in wide.items()}
        halves = {name: a.rearrange("p (k o) -> p k o", k=KD) for name, a in w.items()}
        vecs = {"mask": [128, SH]}
        if rms:
            vecs["norm"] = [128, KD]
        if not relu and not rms:
            vecs |= {"bq": [128, KD], "bo": [128, D], "gate": [128, NH], "gate_f": [128, KD]}
            for a in range(A):
                vecs |= {f"bk{a}": [128, KD], f"bv{a}": [128, KD]}
        biased = "bq" in vecs
        v = {name: t(name, shape) for name, shape in vecs.items()}
        q_all = t("q_all", [128, KD, GT])
        share = t("share", [128, A, NH])
        share_f, bv_mix = (t(n, [128, A, KD]) for n in ("share_f", "bv_mix"))
        bv_wide = t("bv_wide", [128, KD, 128]) if biased else None
        xn = t("xn", [128, 2, GS, D])
        hn = q_all[:].rearrange("p k t -> p (k t)").rearrange("p (s d) -> p s d", s=GS) if rms else None
        xT = t("xT", [128, KD, GT])
        cT = t("cT", [128, 2, KD, GT]) if "ctx" in sets else None
        q = t("q", [128, 2, SH, KD, GT])
        kT = t("kT", [128, 2, A, KD, GT])
        va = t("va", [128, 2, A, GS, NH, DH + 1])
        pr = t("pr", [128, 2, 8, L])
        pT = t("pT", [128, 2, 8, L])
        mx = t("mx", [128, 2, 8])
        rec = t("rec", [128, SH])
        part = t("part", [128, SH, DH])
        ctx_rows = t("ctx_rows", [128, 2, GS, D])
        oT = t("oT", [128, KD, GT]) if out_w else None
        st, mvs, rs = t("st", [128, GS, 6]), t("mvs", [128, GS, 2]), t("rs", [128, 8, GS])
        spare = t("spare", [128, 1])
        x1 = t("x1", [128, 2, 2, D]) if rms else None
        st2, mvs2, rs2 = t("st2", [128, 2, 2, 6]), t("mvs2", [128, 2, 2, 2]), t("rs2", [128, 2, 2])
        scores_of = lambda i: PS[:, 2 * (i % 2):2 * (i % 2) + 2].rearrange("p b (h k) -> p (b h) k", h=4)
        TR = PS[:, 4:6].rearrange("p b (h q) -> p (b h) q", h=4)
        CT = PS[:, 6, 0:2 * L]
        RW = PS[:, 6, 2 * L:4 * L].rearrange("p (h d) -> p h d", d=32)
        cx = t("cx", [128, 2, L])
        FB = PS[:, 7]

        def front_bank(g, j):
            return PS[:, (7, 0, 1, 2)[j % 4]] if is_first(g) else FB

        loaded, ready, ctx_in, ones_set = s("loaded"), s("ready"), [s("ctx_in0"), s("ctx_in1")], s("ones_set")
        mean, scaled_by, normed, vec, pool_c = s("mean"), s("scaled_by"), s("normed"), s("vec"), s("pool_c")
        masked, lifted, rows_back = s("masked"), s("lifted"), s("rows_back")
        full, empty = s("full"), s("empty")
        scored, shifted, maxed, exped, turned, taken, valued, rowed, recip, parted, back_in, x_done = map(s, (
            "scored", "shifted", "maxed", "exped", "turned", "taken", "valued", "rowed", "recip", "parted",
            "back_in", "x_done"))
        x1_in, x1_mean, x1_scale = s("x1_in"), s("x1_mean"), s("x1_scale")
        n_loads = len(wide) + len(vecs)

        front_parts = [("tr", 0), ("tr", 1), ("q", 0), ("q", 1)]
        for a in range(A):
            front_parts += [("k", a, 0), ("k", a, 1), ("v", a, 0), ("v", a, 1)]
        back_parts = [("tb", 0), ("tb", 1), ("o", 0), ("o", 1)] if out_w else []
        NF, NB = len(front_parts), len(back_parts)
        STEPS = 3 * UNITS
        front_at, front_taken, back_at, back_taken, norm_at = WHEN[tag]
        in_turn = sorted([("back", j) for j in range(NB)] + [("front", j) for j in range(NF)],
                         key=lambda x: ((back_at if x[0] == "back" else front_at)[x[1]], x))

        def product(kind, g, j):
            if kind == "front":
                if isinstance(g, int) and g < 2:
                    return g * NF + j
                return 2 * NF + (g - 2) * (NF + NB) + in_turn.index((kind, j))
            if isinstance(g, int) and g >= NG - 2:
                return 2 * NF + (NG - 2) * (NF + NB) + (g - NG + 2) * NB + j
            return 2 * NF + g * (NF + NB) + in_turn.index((kind, j))

        def setup_load(sp):
            for name, dst in {**w, **v}.items():
                sp.dma_start(dst[:], ins[f"{tag}_{name}"]).then_inc(loaded, 16)

        def load_ctx(sp, g, p):
            after(sp, scored, UNITS * (g - 1))
            sp.dma_start(cT[:, p], ins["ctxT"][:, :, g]).then_inc(ctx_in[p], 16)

        def setup_vector(dve):
            dve.wait_ge(loaded, 16 * n_loads)
            nc.vector.memset(PS[:, 6], 0.0)
            nc.vector.memset(va[:], 1.0).then_inc(ones_set, 1)
            if biased:
                dve.wait_ge(recip, 2)
                for sh in (share, share_f):
                    nc.vector.tensor_scalar(sh[:, 0], sh[:, 1], -0.5, 0.5, ALU.mult, ALU.add).then_inc(ready, 1)
                dve.wait_ge(ready, 2)
                for sh in (share, share_f):
                    nc.vector.tensor_scalar(sh[:, 1], sh[:, 1], 0.5, 0.5, ALU.mult, ALU.add).then_inc(ready, 1)
                dve.wait_ge(ready, 4)
                for a in range(A):
                    nc.vector.tensor_tensor(bv_mix[:, a], v[f"bv{a}"][:], share_f[:, a], ALU.mult).then_inc(ready, 1)
                dve.wait_ge(ready, 4 + A)
                nc.vector.tensor_tensor(bv_mix[:, 0], bv_mix[:, 0], bv_mix[:, 1], ALU.add).then_inc(ready, 1)
                dve.wait_ge(ready, 5 + A)
                for c in range(KD):
                    nc.vector.tensor_copy(bv_wide[:, c], bv_mix[:, 0, c:c + 1].broadcast_to([128, 128])).then_inc(ready, 1)
                dve.wait_ge(x_done, 1)
                nc.vector.tensor_tensor(v["bo"][:], v["bo"][:], FB[:, 0:D], ALU.add).then_inc(ready, 1)
                dve.wait_ge(ready, 8 + A)

        def setup_tensor(pe):
            if biased:
                pe.wait_ge(ready, 7 + A)
                for c in range(KD):
                    step = nc.tensor.matmul(FB[:, 0:D], bv_wide[:, c], halves["wo"][:, c], start=c == 0, stop=c == KD - 1)
                step.then_inc(x_done, 1)
                pe.wait_ge(ready, 8 + A)

        def setup_scalar(act):
            act.wait_ge(loaded, 16 * n_loads)
            if biased:
                nc.scalar.activation(share[:, 1], v["gate"][:], ACT.Tanh, scale=0.5).then_inc(recip, 1)
                nc.scalar.activation(share_f[:, 1], v["gate_f"][:], ACT.Tanh, scale=0.5).then_inc(recip, 1)
            if biased:
                act.wait_ge(ready, 4)
            act.wait_ge(ones_set, 1)

        recip0 = 2 if biased else 0

        def behind(n):
            return n if n % 3 else n + 1

        def front_vector(dve, g, p):
            yield 1
            for k in range(GS):
                step = nc.vector.bn_stats(st[:, k], X[:, g, k])
            step.then_inc(vec, 1)
            after(dve, scaled_by, g)
            dve.wait_ge(vec, g + 1)
            nc.vector.tensor_copy(spare[:], eps[:, 0:1])
            for k in range(GS):
                step = nc.vector.bn_aggr(mvs[:, k], st[:, k])
            step.then_inc(mean, 1)

            if is_first(g):
                mask_queries(dve, nc.vector, g, p, front_parts.index(("q", 1)))

        def mask_queries(eng, engine, g, p, j):
            c = front_parts[j][1]
            eng.wait_ge(empty, product("front", g, j) + 1)
            for e in range(SH):
                step = engine.tensor_tensor(q[:, p, e, c], q_all[:, c], v["mask"][:, e:e + 1].broadcast_to([128, GT]), ALU.mult)
            step.then_inc(masked, 1)

        def front_pool(pool, g, p):
            yield 2
            link = Chain(pool, pool_c, 9 if rms else 3, g)
            after(pool, mean, g + 1)
            m = mvs
            link(nc.gpsimd.tensor_tensor(rs[:, 0], m[:, :, 1], eps[:, 0:GS], ALU.add))
            link(nc.gpsimd.tensor_tensor(rs[:, 1], rs[:, 0], neg_half[:, 0:GS], ALU.pow))
            link(nc.gpsimd.tensor_tensor(rs[:, 2], m[:, :, 0], rs[:, 1], ALU.mult))
            step = nc.gpsimd.tensor_tensor(rs[:, 3], rs[:, 2], minus_one[:, 0:GS], ALU.mult)
            if rms:
                link(step)
                link(nc.gpsimd.tensor_tensor(rs[:, 4], rs[:, 1], rs[:, 1], ALU.mult))
                link(nc.gpsimd.tensor_tensor(rs[:, 5], rs[:, 4], m[:, :, 1], ALU.mult))
                link(nc.gpsimd.tensor_tensor(rs[:, 6], rs[:, 5], rms_eps[:, 0:GS], ALU.add))
                link(nc.gpsimd.tensor_tensor(rs[:, 7], rs[:, 6], neg_half[:, 0:GS], ALU.pow))
                link(nc.gpsimd.tensor_tensor(rs[:, 4], rs[:, 7], rs[:, 1], ALU.mult))
                step = nc.gpsimd.tensor_tensor(rs[:, 5], rs[:, 7], rs[:, 3], ALU.mult)
            step.then_inc(scaled_by, 1)
            link.turn_over()
            for j, part in enumerate(front_parts):
                if part[0] == "q" and not (is_first(g) and part[1] == 1):
                    yield front_at[j] + 2
                    mask_queries(pool, nc.gpsimd, g, p, j)

        def front_scalar(act, g, p):
            yield norm_at
            after(act, scaled_by, g + 1)
            if rms:
                after(act, masked, KD * g)
                after(act, back_in, 2 * (g - 1) if not isinstance(g, int) or g > 1 else 0)
            after(act, full, product("front", g - 1, 1) + 1 if not isinstance(g, int) or g else 0)
            for k in range(GS):
                step = nc.scalar.activation(xn[:, p, k], X[:, g, k], ACT.Identity, bias=rs[:, 3, k:k + 1],
                                            scale=rs[:, 1, k:k + 1])
            if rms:
                for k in range(GS):
                    step = nc.scalar.activation(hn[:, k], X[:, g, k], ACT.Identity, bias=rs[:, 5, k:k + 1],
                                                scale=rs[:, 4, k:k + 1])
            step.then_inc(normed, 1)
            for j, part in enumerate(front_parts):
                yield front_taken[j]
                n = product("front", g, j)
                bank = front_bank(g, j)
                act.wait_ge(full, n + 1)
                if part[0] == "tr":
                    c = part[1]
                    step = nc.scalar.activation(xT[:, c], bank, ACT.Copy, scale=v["norm"][:, c:c + 1] if rms else 1.0)
                elif part[0] == "q":
                    c = part[1]
                    after(act, masked, KD * g)
                    if biased:
                        step = nc.scalar.activation(q_all[:, c], bank, ACT.Identity, bias=v["bq"][:, c:c + 1])
                    else:
                        step = nc.scalar.activation(q_all[:, c], bank, ACT.Relu if relu else ACT.Copy)
                elif part[0] == "k":
                    a, c = part[1:]
                    if biased:
                        step = nc.scalar.activation(kT[:, p, a, c], bank, ACT.Identity, bias=v[f"bk{a}"][:, c:c + 1])
                    else:
                        step = nc.scalar.activation(kT[:, p, a, c], bank, ACT.Relu if relu else ACT.Copy)
                else:
                    a, h = part[1:]
                    for k in range(2):
                        step = nc.scalar.activation(va[:, p, a, 2 * h + k, :, 0:DH], heads(bank[:, k * D:k * D + D]),
                                                    ACT.Relu if relu else ACT.Copy)
                step.then_inc(empty, 1)

        def front_tensor(pe, g, p):
            for j, part in enumerate(front_parts):
                yield front_at[j]
                n = product("front", g, j)
                bank = front_bank(g, j)
                if is_first(g):
                    after(pe, empty, max(n - 3, min(n, 2)))
                else:
                    after(pe, empty, n)
                if part[0] == "tr":
                    c = part[1]
                    after(pe, normed, g + 1)
                    for k in range(GS):
                        step = nc.tensor.transpose(bank[:, k * L:k * L + L], (hn[:, k] if rms else xn[:, p, k])[:, c * 128:c * 128 + 128],
                                                   ident[:])
                elif part[0] in "qk":
                    a, c = (0, part[1]) if part[0] == "q" else part[1:]
                    src = xT if part[0] == "q" or sets[a] == "x" else cT[:, p]
                    wt = halves["wq" if part[0] == "q" else f"wk{a}"]
                    if src is not xT:
                        wait_ctx(pe, g, p)
                    for h in range(KD):
                        step = nc.tensor.matmul(bank, wt[:, h, c * 128:c * 128 + 128], src[:, h], start=h == 0, stop=h == KD - 1)
                else:
                    a, h = part[1:]
                    src = xT if sets[a] == "x" else cT[:, p]
                    for k in range(2):
                        row = (2 * h + k) * L
                        for i in range(KD):
                            step = nc.tensor.matmul(bank[:, k * D:k * D + D], src[:, i, row:row + L], halves[f"wv{a}"][:, i],
                                                    start=i == 0, stop=i == KD - 1)
                step.then_inc(full, 1)

        def wait_ctx(pe, g, p):
            if isinstance(g, int):
                pe.wait_ge(ctx_in[p], 16 * (g // 2 + 1))
            else:
                pe.wait_ge(ctx_in[p], 8 * (g - p) + 16)

        def head_at(i, n):
            return SH * unit(i)[2] + n

        def unit(i):
            k, rest = divmod(i, A * KD)
            return (k, *divmod(rest, KD))

        def is_first(g):
            return isinstance(g, int) and g == 0

        def is_last(g):
            return isinstance(g, int) and g == NG - 1

        def units_tensor(pe, g, p):
            def scores(g, p, i):
                k, a, c = unit(i)
                u = UNITS * g + i
                if i == 0:
                    after(pe, masked, KD * (g + 1))
                    after(pe, empty, product("front", g, NF - 1) + 1)
                after(pe, shifted, u - 1)
                for e in range(SH):
                    step = nc.tensor.matmul(scores_of(i)[:, e], q[:, p, e, c, k * L:k * L + L],
                                            kT[:, p, a, c, k * L:k * L + L], start=True, stop=True)
                step.then_inc(scored, 1)

            def transposes(i):
                u = UNITS * g + i
                after(pe, exped, u + 1)
                after(pe, taken, u)
                for h in range(SH):
                    step = nc.tensor.transpose(TR[:, h], pr[:, i % 2, h], ident[:])
                step.then_inc(turned, 1)

            def values(g, p, i):
                k, a, c = unit(i)
                u = UNITS * g + i
                after(pe, taken, u + 1)
                after(pe, rowed, u)
                for h in range(SH):
                    at, half = h % 4, h // 4
                    step = nc.tensor.matmul(CT[32 * at:32 * at + DH + 1, half * L:half * L + L], va[:, p, a, k, head_at(i, h)],
                                            pT[:, i % 2, h], start=True, stop=True, tile_position=(0, 32 * at))
                step.then_inc(valued, 1)

            def turn_back(g, i):
                u = UNITS * g + i
                after(pe, lifted, u + 1)
                for half in range(2):
                    step = nc.tensor.transpose(RW[:, 4 * half:4 * half + 4].rearrange("p h d -> p (h d)"), cx[:, half], ident[:])
                step.then_inc(rows_back, 1)

            if is_first(g):
                scores(g, p, 0)
            for i in range(UNITS):
                if i + 1 < UNITS:
                    scores(g, p, i + 1)
                elif not is_last(g):
                    scores(g + 1, 1 - p, 0)
                if i >= 2:
                    turn_back(g, i - 2)
                elif not is_first(g):
                    turn_back(g - 1, UNITS - 2 + i)
                yield 3 * i
                transposes(i)
                yield 3 * i + 1
                if i:
                    values(g, p, i - 1)
                elif not is_first(g):
                    values(g - 1, 1 - p, UNITS - 1)
                yield 3 * i + 2
            if is_last(g):
                turn_back(g, UNITS - 2)
                values(g, p, UNITS - 1)
                turn_back(g, UNITS - 1)

        def units_vector(dve, g, p):
            def rows(g, p, i):
                k, a, c = unit(i)
                u = UNITS * g + i
                after(dve, rows_back, u + 1)
                if i == 0 and out_w:
                    after(dve, full, product("back", g - 2, 1) + 1 if not isinstance(g, int) or g > 1 else 0)
                nc.vector.reciprocal(rec[:], RW[:, :, DH]).then_inc(recip, 1)
                if biased:
                    dve.wait_ge(recip, recip0 + 2 * u + 1)
                    nc.vector.tensor_tensor(rec[:], rec[:], share[:, a, SH * c:SH * c + SH], ALU.mult).then_inc(recip, 1)
                    dve.wait_ge(recip, recip0 + 2 * u + 2)
                else:
                    dve.wait_ge(recip, u + 1)
                dst = heads(ctx_rows[:, p, k])[:, SH * c:SH * c + SH]
                wide_rec = rec[:].unsqueeze(2).broadcast_to([128, SH, DH])
                if a == 0:
                    nc.vector.tensor_tensor(dst, RW[:, :, 0:DH], wide_rec, ALU.mult).then_inc(rowed, 1)
                else:
                    nc.vector.tensor_tensor(part[:], RW[:, :, 0:DH], wide_rec, ALU.mult).then_inc(rowed, 1)
                    dve.wait_ge(rowed, u + 1)
                    nc.vector.tensor_tensor(dst, dst, part[:], ALU.add).then_inc(parted, 1)
                if not out_w and c == KD - 1:
                    dve.wait_ge(rowed, u + 1)
                    nc.vector.tensor_tensor(X[:, g, k], X[:, g, k], ctx_rows[:, p, k], ALU.add).then_inc(x_done, 1)

            for i in range(UNITS):
                u = UNITS * g + i
                dve.wait_ge(scored, u + 1)
                nc.vector.tensor_reduce(mx[:, i % 2], scores_of(i), AX.X, ALU.max).then_inc(maxed, 1)
                yield 3 * i
                dve.wait_ge(maxed, u + 1)
                after(dve, turned, u - 1)
                nc.vector.tensor_tensor(pr[:, i % 2], scores_of(i), mx[:, i % 2].unsqueeze(2).broadcast_to([128, SH, L]),
                                        ALU.subtract).then_inc(shifted, 1)
                yield 3 * i + 1
                if i >= 2:
                    rows(g, p, i - 2)
                elif not is_first(g):
                    rows(g - 1, 1 - p, UNITS - 2 + i)
                yield 3 * i + 2
            if is_last(g):
                rows(g, p, UNITS - 2)
                rows(g, p, UNITS - 1)

        def units_scalar(act, g, p):
            def take(g, i):
                u = UNITS * g + i
                after(act, turned, u + 1)
                after(act, valued, u - 1)
                nc.scalar.activation(pT[:, i % 2].rearrange("p h q -> p (h q)"), flat(PS[:, 4:6]), ACT.Copy).then_inc(taken, 1)

            def lift(g, i):
                u = UNITS * g + i
                after(act, valued, u + 1)
                after(act, rows_back, u)
                nc.scalar.activation(cx[:].rearrange("p h q -> p (h q)"), CT, ACT.Copy).then_inc(lifted, 1)

            for i in range(UNITS):
                if i >= 2:
                    lift(g, i - 2)
                elif not is_first(g):
                    lift(g - 1, UNITS - 2 + i)
                act.wait_ge(shifted, UNITS * g + i + 1)
                nc.scalar.activation(pr[:, i % 2], pr[:, i % 2], ACT.Exp).then_inc(exped, 1)
                yield 3 * i
                if i:
                    take(g, i - 1)
                elif not is_first(g):
                    take(g - 1, UNITS - 1)
                yield 3 * i + 1
                yield 3 * i + 2
            if is_last(g):
                lift(g, UNITS - 2)
                take(g, UNITS - 1)
                lift(g, UNITS - 1)

        def units_pool(pool, g, p):
            for i in range(STEPS):
                yield i

        def back_tensor(pe, g, p):
            for j, part in enumerate(back_parts):
                yield back_at[j]
                n = product("back", g, j)
                after(pe, empty, n)
                if part[0] == "tb":
                    c = part[1]
                    after(pe, rowed, UNITS * (g + 1))
                    if A > 1:
                        after(pe, parted, UNITS // A * (g + 1))
                    for k in range(GS):
                        step = nc.tensor.transpose(FB[:, k * L:k * L + L], ctx_rows[:, p, k, c * 128:c * 128 + 128], ident[:])
                else:
                    for k in range(2):
                        row = (2 * part[1] + k) * L
                        for c in range(KD):
                            step = nc.tensor.matmul(FB[:, k * D:k * D + D], oT[:, c, row:row + L], halves["wo"][:, c],
                                                    start=c == 0, stop=c == KD - 1)
                step.then_inc(full, 1)

        def back_scalar(act, g, p):
            for j, part in enumerate(back_parts):
                if part[0] == "tb":
                    yield back_taken[j]
                    act.wait_ge(full, product("back", g, j) + 1)
                    nc.scalar.activation(oT[:, part[1]], FB, ACT.Copy).then_inc(empty, 1)

        def back_vector(dve, g, p):
            for j, part in enumerate(back_parts):
                if part[0] == "o":
                    yield behind(back_at[j] + 1)
                    h = part[1]
                    turn = 2 * g + h
                    dve.wait_ge(full, product("back", g, j) + 1)
                    o = FB.rearrange("p (k d) -> p k d", k=2)
                    if rms:
                        after(dve, x1_scale, 2 * g)
                        nc.vector.tensor_tensor(x1[:, h], o, xn[:, p, 2 * h:2 * h + 2], ALU.add).then_inc(empty, 1)
                        dve.wait_ge(empty, product("back", g, j) + 1)
                        nc.vector.tensor_tensor(X[:, g, 2 * h:2 * h + 2], X[:, g, 2 * h:2 * h + 2], x1[:, h], ALU.add).then_inc(back_in, 1)
                        for k in range(2):
                            step = nc.vector.bn_stats(st2[:, h, k], x1[:, h, k])
                        step.then_inc(x1_in, 1)
                        dve.wait_ge(x1_in, turn + 1)
                        nc.vector.tensor_copy(spare[:], eps[:, 0:1])
                        for k in range(2):
                            step = nc.vector.bn_aggr(mvs2[:, h, k], st2[:, h, k])
                        step.then_inc(x1_mean, 1)
                    else:
                        after(dve, back_in, turn)
                        nc.vector.tensor_tensor(o2[:], o, v["bo"][:].unsqueeze(1).broadcast_to([128, 2, D]), ALU.add).then_inc(empty, 1)
                        dve.wait_ge(empty, product("back", g, j) + 1)
                        nc.vector.tensor_tensor(X[:, g, 2 * h:2 * h + 2], X[:, g, 2 * h:2 * h + 2], o2[:], ALU.add).then_inc(back_in, 1)

        o2 = t("o2", [128, 2, D]) if biased else None

        def back_pool(pool, g, p):
            if not rms:
                return
            for h in range(2):
                yield back_at[2 + h] + 3
                turn = 2 * g + h
                link = Chain(pool, s_x1c, 4, turn)
                pool.wait_ge(x1_mean, turn + 1)
                link(nc.gpsimd.tensor_tensor(rs2[:, 0], mvs2[:, h, :, 0], mvs2[:, h, :, 0], ALU.mult))
                link(nc.gpsimd.tensor_tensor(rs2[:, 0], rs2[:, 0], mvs2[:, h, :, 1], ALU.add))
                link(nc.gpsimd.tensor_tensor(rs2[:, 0], rs2[:, 0], rms_eps[:, 0:2], ALU.add))
                link(nc.gpsimd.tensor_tensor(rs2[:, 1], rs2[:, 0], neg_half[:, 0:2], ALU.pow))
                nc.gpsimd.tensor_tensor(H[:, g, 2 * h:2 * h + 2], x1[:, h],
                                        rs2[:, 1].unsqueeze(2).broadcast_to([128, 2, D]), ALU.mult).then_inc(x1_scale, 1)
                link.turn_over()

        s_x1c = s("x1c")

        def run(eng, front, units, back):
            def turn(g, p):
                sides = []
                if not isinstance(g, int) or g > 0:
                    sides.append(back(eng, g - 1, 1 - p))
                if not isinstance(g, int) or g + 1 < NG:
                    sides.append(front(eng, g + 1, 1 - p))
                weave(units(eng, g, p), merged(*sides))

            alone(front(eng, 0, 0))
            turn(0, 0)
            with eng.Fori(0, (NG - 2) // 2) as pair:
                turn(2 * pair + 1, 1)
                turn(2 * pair + 2, 0)
            turn(NG - 1, 1)
            alone(back(eng, NG - 1, 1))

        def none(eng, g, p):
            return
            yield

        def sync(sp):
            setup_load(sp)
            if cT is not None:
                load_ctx(sp, 0, 0)
                load_ctx(sp, 1, 1)
                with sp.Fori(0, (NG - 2) // 2) as pair:
                    load_ctx(sp, 2 * pair + 2, 0)
                    load_ctx(sp, 2 * pair + 3, 1)

        def tensor(pe):
            pe.wait_ge(loaded, 16 * n_loads)
            setup_tensor(pe)
            run(pe, front_tensor, units_tensor, back_tensor if out_w else none)

        def scalar(act):
            setup_scalar(act)
            run(act, front_scalar, units_scalar, back_scalar if out_w else none)

        def vector(dve):
            setup_vector(dve)
            run(dve, front_vector, units_vector, back_vector if out_w else none)

        def pool(pl):
            run(pl, front_pool, units_pool, back_pool if out_w else none)

        mem.end()
        return dict(x_done=x_done, back_in=back_in, sync=sync, tensor=tensor, scalar=scalar, vector=vector, pool=pool)

    def feature_rows(tag, mem, src, dst, then, norm=False, scale=None, xn=None, keep_rows=None):
        t = lambda name, shape: mem.take(f"{tag}_{name}", shape)
        s = lambda name: mem.sem(f"{tag}_{name}")
        xn = t("xn", [128, 2, GS, D]) if xn is None else xn
        st, mvs, rs = t("st", [128, 2, GS, 6]), t("mvs", [128, 2, GS, 2]), t("rs", [128, 2, 4, GS])
        spare = t("spare", [128, 1])
        vec, mean, chain, scaled_by, normed, turned, taken, kept = map(s, (
            "vec", "mean", "chain", "scaled_by", "normed", "turned", "taken", "kept"))
        TB = lambda p: PS[:, 2 * p:2 * p + 2]
        dst_g = dst.rearrange("p k (g r) -> p k g r", r=GT)

        def vector(dve):
            def take(g, p):
                dve.wait_ge(turned, g + 1)
                for c in range(KD):
                    if scale is None:
                        step = nc.vector.tensor_copy(dst_g[:, c, g], TB(p)[:, c])
                    else:
                        step = nc.vector.tensor_tensor(dst_g[:, c, g], TB(p)[:, c], scale[:, c:c + 1].broadcast_to([128, GT]), ALU.mult)
                step.then_inc(taken, 1)

            def stats(g, p):
                if not norm:
                    return
                for k in range(GS):
                    step = nc.vector.bn_stats(st[:, p, k], src[:, g, k])
                step.then_inc(vec, 1)
                dve.wait_ge(vec, g + 1)
                nc.vector.tensor_copy(spare[:], eps[:, 0:1])
                for k in range(GS):
                    step = nc.vector.bn_aggr(mvs[:, p, k], st[:, p, k])
                step.then_inc(mean, 1)

            stats(0, 0)
            stats(1, 1)
            take(0, 0)
            with dve.Fori(0, NG // 2 - 1) as pair:
                for g, p in ((2 * pair + 1, 1), (2 * pair + 2, 0)):
                    stats(g + 1, 1 - p)
                    take(g, p)
                    then[1](dve, g - 1, 1 - p)
            take(NG - 1, 1)
            then[1](dve, NG - 2, 0)
            then[1](dve, NG - 1, 1)

        def pool(pl):
            if not norm:
                return

            def rstd(g, p):
                link = Chain(pl, chain, 3, g)
                if keep_rows is not None:
                    after(pl, kept, g - 1)
                pl.wait_ge(mean, g + 1)
                link(nc.gpsimd.tensor_tensor(rs[:, p, 0], mvs[:, p, :, 1], eps[:, 0:GS], ALU.add))
                link(nc.gpsimd.tensor_tensor(rs[:, p, 1], rs[:, p, 0], neg_half[:, 0:GS], ALU.pow))
                link(nc.gpsimd.tensor_tensor(rs[:, p, 2], mvs[:, p, :, 0], rs[:, p, 1], ALU.mult))
                nc.gpsimd.tensor_tensor(rs[:, p, 3], rs[:, p, 2], minus_one[:, 0:GS], ALU.mult).then_inc(scaled_by, 1)

            rstd(0, 0)
            rstd(1, 1)
            with pl.Fori(0, NG // 2 - 1) as pair:
                for p in range(2):
                    rstd(2 * pair + p + 2, p)

        def scalar(act):
            def rows_of(g, p):
                for to, done in [(xn[:, p], normed)] + ([(keep_rows[:, g], kept)] if keep_rows is not None else []):
                    for k in range(GS):
                        if norm:
                            step = nc.scalar.activation(to[:, k], src[:, g, k], ACT.Identity, bias=rs[:, p, 3, k:k + 1],
                                                        scale=rs[:, p, 1, k:k + 1])
                        else:
                            step = nc.scalar.activation(to[:, k], src[:, g, k], ACT.Copy)
                    step.then_inc(done, 1)

            for g in range(2):
                if norm:
                    act.wait_ge(scaled_by, g + 1)
                rows_of(g, g)
            with act.Fori(0, NG // 2 - 1) as pair:
                for p in range(2):
                    g = 2 * pair + p + 2
                    if norm:
                        act.wait_ge(scaled_by, g + 1)
                    act.wait_ge(normed, g)
                    act.wait_ge(turned, g - 1)
                    nc.scalar.activation(spare_s[:], eps[:, 0:1], ACT.Copy)
                    rows_of(g, p)

        spare_s = t("spare_s", [128, 1])

        def tensor(pe):
            def turn(g, p):
                pe.wait_ge(normed, g + 1)
                after(pe, taken, g - 1)
                for c in range(KD):
                    for k in range(GS):
                        step = nc.tensor.transpose(TB(p)[:, c, k * L:k * L + L], xn[:, p, k, c * 128:c * 128 + 128], ident[:])
                step.then_inc(turned, 1)

            def go_on(g, p):
                pe.wait_ge(taken, g + 1)
                then[0](pe, g, p)

            turn(0, 0)
            turn(1, 1)
            with pe.Fori(0, NG // 2 - 1) as pair:
                for p in range(2):
                    go_on(2 * pair + p, p)
                    turn(2 * pair + p + 2, p)
            go_on(NG - 2, 0)
            go_on(NG - 1, 1)

        return dict(vector=vector, pool=pool, scalar=scalar, tensor=tensor, kept=kept)

    def recurrence(tag, turn):
        WIN = 8
        B = NG * GS
        TURNS = L // (2 * WIN)
        mem = Stage(nc, sem_set[turn])
        t = lambda name, shape: mem.take(f"{tag}_{name}", shape)
        s = lambda name: mem.sem(f"{tag}_{name}")
        wi, wh, bs = t("wi", [128, KD * D]), t("wh", [128, KD * D]), t("b", [128, 2 * KD])
        wi_k, wh_k = (a.rearrange("p (k o) -> p k o", k=KD) for a in (wi, wh))
        bias = t("bias", [128, KD])
        xT = t("xT", [128, KD, B * L])
        ring = t("ring", [128, KD, B, 2 * WIN])
        HS = t("HS", [128, KD, B, L])
        sums = t("sums", [128, 2, KD, B])
        loaded, bias_set, pre, copied, summed, turned, added = map(
            s, ("loaded", "bias_set", "pre", "copied", "summed", "turned", "added"))
        tanhed, ready, joined = ([s(f"{n}{m}") for m in range(KD)] for n in ("tanhed", "ready", "joined"))
        xT_g = xT.rearrange("p k (g r) -> p k g r", r=GT)
        xT_t = xT.rearrange("p k (b w j) -> p k b w j", b=B, j=2 * WIN)

        def bank(step, m):
            return PS[:, 2 * (step % 2) + m, 0:B]

        def inputs_tensor(pe, g, p):
            pe.wait_ge(summed, g + 1)
            for m in range(KD):
                for k in range(KD):
                    step = nc.tensor.matmul(PS[:, 4 + 2 * p + m], wi_k[:, k, m * 128:m * 128 + 128], xT_g[:, k, g],
                                            start=k == 0, stop=k == KD - 1)
            step.then_inc(pre, 1)

        def inputs_vector(dve, g, p):
            dve.wait_ge(pre, g + 1)
            for m in range(KD):
                step = nc.vector.tensor_tensor(xT_g[:, m, g], PS[:, 4 + 2 * p + m], bias[:, m:m + 1].broadcast_to([128, GT]), ALU.add)
            step.then_inc(summed, 1)

        rows = feature_rows(tag + "f", mem, X, xT, (inputs_tensor, inputs_vector), norm=True)

        def sync(sp):
            for dst, name in ((wi, "wi"), (wh, "wh"), (bs, "b")):
                sp.dma_start(dst[:], ins[f"{tag}_{name}"]).then_inc(loaded, 16)

        def tensor(pe):
            pe.wait_ge(loaded, 48)
            rows["tensor"](pe)
            pe.wait_ge(summed, NG + 2)

            def step(turn, j):
                for k in range(KD):
                    pe.wait_ge(tanhed[k], turn * (2 * WIN) + j + 1)
                    for m in range(KD):
                        product = nc.tensor.matmul(bank(j, m), wh_k[:, k, m * 128:m * 128 + 128], ring[:, k, :, (j - 1) % (2 * WIN)],
                                                start=k == 0, stop=k == KD - 1)
                        if k == KD - 1:
                            product.then_inc(ready[m], 1)

            with pe.Fori(0, TURNS) as turn:
                for j in range(2 * WIN):
                    step(turn, j)
            pe.wait_ge(copied, 2 * TURNS + 1)
            for b in range(B):
                if b % 2 == 0 and b >= 4:
                    pe.wait_ge(added, b // 2 - 1)
                for c in range(KD):
                    step = nc.tensor.transpose(PS[:, b // 2 % 2, (b % 2 * KD + c) * 128:(b % 2 * KD + c) * 128 + 128], HS[:, c, b], ident[:])
                if b % 2:
                    step.then_inc(turned, 1)

        def scalar(act):
            rows["scalar"](act)
            act.wait_ge(copied, 1)

            def window(turn, place):
                after(act, copied, 2 * turn + place)
                for j in range(WIN):
                    step = turn * (2 * WIN) + place * WIN + j
                    for m in range(KD):
                        act.wait_ge(joined[m], step + 1)
                        nc.scalar.activation(ring[:, m, :, place * WIN + j], sums[:, j % 2, m], ACT.Tanh).then_inc(tanhed[m], 1)

            window(0, 0)
            window(0, 1)
            with act.Fori(0, TURNS - 1) as turn:
                window(turn + 1, 0)
                window(turn + 1, 1)

        def vector(dve):
            dve.wait_ge(loaded, 48)
            nc.vector.memset(ring[:], 0.0).then_inc(copied, 1)
            dve.wait_ge(copied, 1)
            dve.sem_inc(tanhed[0], 1)
            dve.sem_inc(tanhed[1], 1)
            nc.vector.tensor_tensor(bias[:], bs[:, 0:KD], bs[:, KD:2 * KD], ALU.add).then_inc(bias_set, 1)
            dve.sem_inc(summed, 2)
            dve.wait_ge(bias_set, 1)
            rows["vector"](dve)
            HS_w = HS.rearrange("p k b (w j) -> p (k b) w j", j=WIN)

            def window(turn, place, keep):
                for j in range(WIN):
                    at = turn * (2 * WIN) + place * WIN + j
                    for m in range(KD):
                        dve.wait_ge(ready[m], at + 1)
                        nc.vector.tensor_tensor(sums[:, j % 2, m], bank(j, m), xT_t[:, m, :, turn, place * WIN + j],
                                                ALU.add).then_inc(joined[m], 1)
                    if j == 1 and keep is not None:
                        keep_states(*keep)

            def keep_states(turn, place):
                for m in range(KD):
                    dve.wait_ge(tanhed[m], (2 * turn + place + 1) * WIN + 1)
                nc.vector.tensor_copy(HS_w[:, :, 2 * turn + place],
                                      ring.rearrange("p k b j -> p (k b) j")[:, :, place * WIN:place * WIN + WIN]).then_inc(copied, 1)

            window(0, 0, None)
            window(0, 1, (0, 0))
            with dve.Fori(0, TURNS - 1) as turn:
                window(turn + 1, 0, (turn, 1))
                window(turn + 1, 1, (turn + 1, 0))
            keep_states(TURNS - 1, 1)
            x_seq = X.rearrange("p g s d -> p (g s) d")
            for b in range(0, B, 2):
                dve.wait_ge(turned, b // 2 + 1)
                nc.vector.tensor_tensor(x_seq[:, b:b + 2], x_seq[:, b:b + 2],
                                        PS[:, b // 2 % 2].rearrange("p (b d) -> p b d", b=2), ALU.add).then_inc(added, 1)
            dve.wait_ge(added, B // 2)

        def pool(pl):
            rows["pool"](pl)

        mem.end()
        return dict(sync=sync, tensor=tensor, scalar=scalar, vector=vector, pool=pool)

    def experts(tag, turn, src, gated, rows_by_expert, out_by_expert, listed, result=None):
        E = 8
        SHN = NG // 2 if gated else 0
        UNITS = units_of_list(NG)
        UT = UR // 128
        F, FC = 512, 4
        FILLS = NG * GT // UR
        TILES = NG * GS
        mem = Stage(nc, sem_set[turn])
        t = lambda name, shape, dtype=F32: mem.take(f"{tag}_{name}", shape, dtype)
        s = lambda name: mem.sem(f"{tag}_{name}")
        UPS = (2 if gated else 1) * KD * F
        WN = UPS + FC * D
        w = t("w", [128, 2, WN])
        w_gate = w[:, :, 0:KD * F].rearrange("p r (k f) -> p r k f", k=KD)
        w_up = w[:, :, UPS - KD * F:UPS].rearrange("p r (k f) -> p r k f", k=KD)
        w_down = w[:, :, UPS:].rearrange("p r (f d) -> p r f d", f=FC)
        wr = t("wr", [128, KD * E])
        vec = t("v", [128, KD if gated else E])
        const = t("const", [128, 128 + E + FILLS + UNITS])
        before_me = const[:, 0:128]
        order = const[:, 128:128 + E]
        whole = const[:, 128 + E:128 + E + FILLS]
        unit_no = const[:, 128 + E + FILLS:]
        rows_full = src if gated else t("rows_full", [128, NG, GS, D])
        xT = t("xT", [128, KD, NG * GT])
        xT_g = xT.rearrange("p k (g r) -> p k g r", r=GT)
        big = t("big", [128, 2 * GS * 2 * D])
        lT = big[0:E, 0:NG * GT]
        lT_g = lT.rearrange("e (g r) -> e g r", r=GT)
        ones = t("ones", [128, 128])
        lg = t("lg", [128, TILES, E])
        tmp = t("tmp", [128, TILES, E])
        best = t("best", [128, 2, TILES, E])
        chosen, total, until, place, first_of = (t(n, [128, E, TILES]) for n in ("chosen", "total", "until", "place", "first_of"))
        filled, units_e, last_e, base_e = t("filled", [128, E, FILLS]), t("units_e", [128, E]), t("last_e", [128, E]), t("base_e", [128, E])
        ones_e = t("ones_e", [128, E])
        passed_e, expert_f, expert_i = t("passed_e", [128, UNITS, E]), t("expert_f", [128, UNITS]), t("expert_i", [128, UNITS], I32)
        top = t("top", [128, 5, TILES])
        slot_f = t("slot_f", [128, TILES, 2])
        slot = t("slot", [128, NG, GS, 2], I32)
        share = t("share", [128, NG, GS, 2])
        slot_now, share_now = t("slot_now", [128, 2, GS, 2], I32), t("share_now", [128, 2, GS, 2])
        staged_rows = t("staged_rows", [128, 2, GS, D])
        unit_rows = t("unit_rows", [128, 2, UT, D])
        unit_T = t("unit_T", [128, 2, KD, UR])
        mark = t("mark", [128, 1])
        act_b = t("act_b", [128, 2, GT])
        hid = t("hid", [128, 2, FC, GT])
        y_rows = t("y_rows", [128, 2, UT, D])
        y_got = big.rearrange("p (r k j d) -> p r k j d", r=2, k=GS, j=2)
        width = {"shared": GT, "list": UR}
        GB = lambda c, kind: PS[:, 2 * (c % 2), 0:width[kind]]
        UB = lambda c, kind: PS[:, 2 * (c % 2) + 1, 0:width[kind]]
        DB = lambda h, kind: PS[:, 4 + h, 0:width[kind] // 2 // 128 * D].rearrange("p (s d) -> p s d", d=D)
        TB = PS[:, 6:8, 0:UR]
        list_units = rows_by_expert.rearrange("(u r p) d -> p u r d", p=128, r=UT)
        out_units = out_by_expert.rearrange("(u r p) d -> p u r d", p=128, r=UT)

        loaded, w_gu, w_dn = s("loaded"), [s("w_gu0"), s("w_gu1")], [s("w_dn0"), s("w_dn1")]
        logit, logit_in, back, routed, exped, link_s, chose, ranked, placed = map(s, (
            "logit", "logit_in", "back", "routed", "exped", "link", "chose", "ranked", "placed"))
        full, silued, hidden, down, taken, turned, turned_in = map(s, (
            "full", "silued", "hidden", "down", "taken", "turned", "turned_in"))
        staged, in_list, row_in, y_out = s("staged"), [mem.gpsimd_sem(f"{tag}_in_list0"), mem.gpsimd_sem(f"{tag}_in_list1")], [s("row_in0"), s("row_in1")], [s("y_out0"), s("y_out1")]
        asked, got, share_set, halved, combined = s("asked"), [mem.gpsimd_sem(f"{tag}_got0"), mem.gpsimd_sem(f"{tag}_got1")], s("share_set"), s("halved"), s("combined")
        marked = s("marked")

        def logits_tensor(pe, g, p):
            pe.wait_ge(logit_in, g + 1)
            wr_k = wr.rearrange("p (k e) -> p k e", k=KD)
            for k in range(KD):
                step = nc.tensor.matmul(PS[0:E, 4 + p], wr_k[:, k], xT_g[:, k, g], start=k == 0, stop=k == KD - 1)
            step.then_inc(logit, 1)

        def logits_vector(dve, g, p):
            dve.wait_ge(logit, g + 1)
            nc.vector.tensor_copy(lT_g[:, g], PS[0:E, 4 + p]).then_inc(logit_in, 1)

        rows = feature_rows(tag + "f", mem, src, xT, (logits_tensor, logits_vector), norm=not gated, scale=vec if gated else None,
                            xn=staged_rows, keep_rows=None if gated else rows_full)

        def router_tensor(pe):
            pe.wait_ge(logit_in, NG + 2)
            for n in range(TILES):
                step = nc.tensor.transpose(PS[:, 7, n * E:n * E + E], lT[:, n * L:n * L + L], ident[0:E, 0:E])
            step.then_inc(back, 1)

        def rank_tensor(pe):
            pe.wait_ge(chose, 1)
            nc.tensor.matmul(PS[:, 4, 0:E * TILES], before_me, chosen.rearrange("p e n -> p (e n)"), start=True, stop=True)
            nc.tensor.matmul(PS[:, 5, 0:E * TILES], ones[:], chosen.rearrange("p e n -> p (e n)"), start=True, stop=True).then_inc(ranked, 1)

        def router_vector(dve):
            nc.vector.memset(ones_e[:], 1.0).then_inc(link_s, 1)
            nc.vector.memset(first_of[:], 1.0).then_inc(link_s, 1)
            dve.wait_ge(link_s, 2)
            nc.vector.memset(first_of[:, :, 0:1], 0.0).then_inc(link_s, 1)
            link = Chain(dve, link_s, 99, 0)
            link.k = 3
            V = nc.vector
            by_e = lambda a: a.unsqueeze(2).broadcast_to([128, TILES, E])
            from_p = PS[:, 7, 0:TILES * E].rearrange("p (n e) -> p n e", e=E)
            dve.wait_ge(back, 1)
            if gated:
                link(V.tensor_reduce(top[:, 0], from_p, AX.X, ALU.max))
                link(V.tensor_tensor(lg[:], from_p, by_e(top[:, 0]), ALU.subtract))
                dve.sem_inc(routed, 1)
                dve.wait_ge(exped, 1)
                link(V.tensor_reduce(top[:, 1], lg[:], AX.X, ALU.add))
                link(V.reciprocal(top[:, 1], top[:, 1]))
                link(V.tensor_tensor(lg[:], lg[:], by_e(top[:, 1]), ALU.mult))
            else:
                link(V.tensor_tensor(lg[:], from_p, vec[:].unsqueeze(1).broadcast_to([128, TILES, E]), ALU.add))
                dve.sem_inc(routed, 1)
                dve.wait_ge(exped, 1)
                link(V.tensor_scalar(lg[:], lg[:], 1.0, None, ALU.add))
                link(V.reciprocal(lg[:], lg[:]))
            rank = order.unsqueeze(1).broadcast_to([128, TILES, E])
            for j in range(2):
                link(V.tensor_reduce(top[:, 2 + j], lg[:], AX.X, ALU.max))
                link(V.tensor_tensor(tmp[:], lg[:], by_e(top[:, 2 + j]), ALU.is_equal))
                link(V.tensor_tensor(tmp[:], tmp[:], rank, ALU.mult))
                link(V.tensor_reduce(top[:, 4], tmp[:], AX.X, ALU.max))
                link(V.tensor_tensor(best[:, j], tmp[:], by_e(top[:, 4]), ALU.is_equal))
                if j == 0:
                    link(V.scalar_tensor_tensor(out=lg[:], in0=best[:, 0], scalar=-2.0, in1=lg[:], op0=ALU.mult, op1=ALU.add))
            link(V.tensor_tensor(chosen.rearrange("p e n -> p n e"), best[:, 0], best[:, 1], ALU.add))
            dve.sem_inc(chose, 1)
            if gated:
                link(V.tensor_tensor(top[:, 4], top[:, 3], top[:, 2], ALU.subtract))
                dve.sem_inc(routed, 1)
                dve.wait_ge(exped, 2)
                link(V.tensor_scalar(top[:, 0], top[:, 4], 1.0, None, ALU.add))
                link(V.reciprocal(top[:, 0], top[:, 0]))
                link(V.tensor_tensor(top[:, 1], top[:, 4], top[:, 0], ALU.mult))
            else:
                link(V.tensor_tensor(top[:, 4], top[:, 2], top[:, 3], ALU.add))
            if not gated:
                link(V.tensor_scalar(top[:, 4], top[:, 4], 1e-6, None, ALU.add))
                link(V.reciprocal(top[:, 4], top[:, 4]))
                for j in range(2):
                    step = V.tensor_tensor(top[:, j], top[:, 2 + j], top[:, 4], ALU.mult)
                link(step)
            share_t = share.rearrange("p g s j -> p (g s) j")
            for j in range(2):
                link(V.tensor_copy(share_t[:, :, j], top[:, j]))
            dve.wait_ge(ranked, 1)
            ranks = lambda b: PS[:, b, 0:E * TILES].rearrange("p (e n) -> p e n", e=E)
            flat_e = lambda a: a.rearrange("p e n -> p (e n)")
            link(V.tensor_copy(total[:], ranks(5)))
            link(V.tensor_tensor_scan(flat_e(until), flat_e(first_of), flat_e(total), 0.0, ALU.mult, ALU.add))
            link(V.tensor_tensor(filled[:], until[:, :, TILES - 1:TILES].broadcast_to([128, E, FILLS]),
                                 whole.unsqueeze(1).broadcast_to([128, E, FILLS]), ALU.is_gt))
            link(V.tensor_reduce(units_e[:], filled[:], AX.X, ALU.add))
            link(V.tensor_tensor_scan(last_e[:], ones_e[:], units_e[:], 0.0, ALU.mult, ALU.add))
            link(V.tensor_tensor(base_e[:], last_e[:], units_e[:], ALU.subtract))
            link(V.tensor_scalar(base_e[:], base_e[:], float(UR), None, ALU.mult))
            link(V.tensor_tensor(place[:], until[:], total[:], ALU.subtract))
            link(V.tensor_tensor(place[:], place[:], ranks(4), ALU.add))
            link(V.tensor_tensor(place[:], place[:], base_e[:].unsqueeze(2).broadcast_to([128, E, TILES]), ALU.add))
            for j in range(2):
                link(V.tensor_tensor(tmp[:], best[:, j], place.rearrange("p e n -> p n e"), ALU.mult))
                link(V.tensor_reduce(slot_f[:, :, j], tmp[:], AX.X, ALU.add))
            link(V.tensor_copy(slot.rearrange("p g s j -> p (g s) j"), slot_f[:]))
            link(V.tensor_tensor(passed_e[:], unit_no.unsqueeze(2).broadcast_to([128, UNITS, E]),
                                 last_e[:].unsqueeze(1).broadcast_to([128, UNITS, E]), ALU.is_ge))
            link(V.tensor_reduce(expert_f[:], passed_e[:], AX.X, ALU.add))
            link(V.tensor_scalar(expert_f[:], expert_f[:], float(E - 1), None, ALU.min))
            link(V.tensor_copy(expert_i[:], expert_f[:]))
            dve.sem_inc(placed, 1)

        def router_scalar(act):
            act.wait_ge(routed, 1)
            nc.scalar.activation(lg[:], lg[:], ACT.Exp, scale=1.0 if gated else -1.0).then_inc(exped, 1)
            if gated:
                act.wait_ge(routed, 2)
                nc.scalar.activation(top[:, 4], top[:, 4], ACT.Exp).then_inc(exped, 1)

        def stage_group(dve, turn, p):
            g = 2 * turn + p
            after(dve, in_list[p], 16 * 2 * GS * turn)
            nc.vector.tensor_copy(staged_rows[:, p], rows_full[:, g])
            nc.vector.tensor_copy(slot_now[:, p], slot[:, g]).then_inc(staged, 1)

        def stage_vector(dve):
            dve.wait_ge(placed, 1)
            if not gated:
                dve.wait_ge(rows["kept"], NG)
            stage_group(dve, 0, 0)
            if not gated:
                stage_group(dve, 0, 1)
                with dve.Fori(0, NG // 2 - 1) as turn:
                    stage_group(dve, turn + 1, 0)
                    stage_group(dve, turn + 1, 1)

        def to_list_pool(pl):
            pl.wait_ge(listed, 16 * UNITS)

            def group(turn, p):
                g = 2 * turn + p
                after(pl, marked, g)
                pl.wait_ge(staged, g + 1)
                nc.gpsimd.tensor_tensor(mark[:], eps[:, 0:1], eps[:, 0:1], ALU.add).then_inc(marked, 1)
                for k in range(GS):
                    for j in range(2):
                        nc.gpsimd.indirect_dma_start(
                            rows_by_expert, bass.IndirectOffsetOnAxis(slot_now[:, p, k, j:j + 1], 0),
                            staged_rows[:, p, k], None).then_inc(in_list[p], 16)

            group(0, 0)
            group(0, 1)
            with pl.Fori(0, NG // 2 - 1) as turn:
                group(turn + 1, 0)
                group(turn + 1, 1)

        def collect_pool(pl):
            for p in range(2):
                pl.wait_ge(y_out[p], 16 * ((UNITS + 1 - p) // 2 + 1))
            with pl.Fori(0, NG // 2) as pair:
                for p in range(2):
                    g = 2 * pair + p
                    pl.wait_ge(combined, g + 1)
                    nc.gpsimd.tensor_copy(slot_now[:, p], slot[:, g]).then_inc(asked, 1)
                    pl.wait_ge(asked, g + 1)
                    nc.gpsimd.tensor_tensor(mark[:], eps[:, 0:1], eps[:, 0:1], ALU.add)
                    for k in range(GS):
                        for j in range(2):
                            nc.gpsimd.indirect_dma_start(
                                y_got[:, p, k, j], None, out_by_expert,
                                bass.IndirectOffsetOnAxis(slot_now[:, p, k, j:j + 1], 0)).then_inc(got[p], 16)

        def collect_group(dve, turn, p):
            g = 2 * turn + p
            if SHN:
                dve.wait_ge(taken, 2 * (g + 2 + (UNITS if g >= SHN else 0)))
            dve.wait_ge(combined, g + 2)
            nc.vector.tensor_copy(share_now[:, p], share[:, g]).then_inc(share_set, 1)
            dve.wait_ge(share_set, g + 1)
            dve.wait_ge(got[p], 16 * 2 * GS * (turn + 1))
            for j in range(2):
                for k in range(GS):
                    step = nc.vector.scalar_tensor_tensor(
                        out=X[:, g, k], in0=y_got[:, p, k, j], scalar=share_now[:, p, k, j:j + 1], in1=X[:, g, k],
                        op0=ALU.mult, op1=ALU.add)
                step.then_inc((halved, combined)[j], 1)
                if j == 0:
                    dve.wait_ge(halved, g + 1)

        def collect_vector(dve):
            if gated:
                for g in range(2 * (NG - SHN - 1), NG):
                    collect_group(dve, g // 2, g % 2)
            else:
                with dve.Fori(0, NG // 2) as turn:
                    collect_group(dve, turn, 0)
                    collect_group(dve, turn, 1)

        def output_tensor(pe, v, kind, at, p, r):
            if kind == "list":
                wait_ring(pe, w_dn, at, r)
            pe.wait_ge(hidden, v * FC + FC)
            for h in range(2):
                pe.wait_ge(taken, 2 * v + h + 1)
                out_h = DB(h, kind)
                tiles = width[kind] // 2 // 128
                for q in range(tiles):
                    row = (h * tiles + q) * 128
                    for f in range(FC):
                        step = nc.tensor.matmul(out_h[:, q], hid[:, p, f, row:row + 128], w_down[:, r, f], start=f == 0, stop=f == FC - 1)
                step.then_inc(down, 1)

        def wait_ring(pe, sems, j, r):
            extra = 1 if SHN and r == 0 else 0
            if isinstance(j, int):
                pe.wait_ge(sems[r], 16 * (j // 2 + 1 + extra))
            else:
                pe.wait_ge(sems[r], 8 * (j - (j_parity(r))) + 16 * (1 + extra))

        def j_parity(r):
            return 1 - r if SHN else r

        def ring_of(jp):
            return 1 - jp if SHN else jp

        def turn_rows(pe, j, jp):
            if isinstance(j, int):
                pe.wait_ge(row_in[jp], 16 * (j // 2 + 1))
            else:
                pe.wait_ge(row_in[jp], 8 * (j - jp) + 16)
            after(pe, turned_in, j)
            for c in range(KD):
                for k in range(UT):
                    step = nc.tensor.transpose(TB[:, c, k * L:k * L + L], unit_rows[:, jp, k, c * 128:c * 128 + 128], ident[:])
            step.then_inc(turned, 1)

        def unit_tensor(pe, u, kind, at, p, r, before, ahead, again=None):
            if again == 0:
                for sems in (w_gu, w_dn):
                    pe.wait_ge(sems[0], 16 * (UNITS // 2 + 2))
            for f in range(FC):
                after(pe, hidden, u * FC + (f - 1))
                if f == 0 and kind == "list":
                    wait_ring(pe, w_gu, at, r)
                    pe.wait_ge(turned_in, at + 1)
                for b, wt in ((GB(f, kind), w_gate), (UB(f, kind), w_up))[:2 if gated else 1]:
                    for c in range(KD):
                        x = xT_g[:, c, at] if kind == "shared" else unit_T[:, p, c]
                        step = nc.tensor.matmul(b, wt[:, r, c, f * 128:f * 128 + 128], x, start=c == 0, stop=c == KD - 1)
                step.then_inc(full, 1)
                if f == 0 and before is not None:
                    output_tensor(pe, u - 1, *before)
                if f == 1 and ahead == "list":
                    turn_rows(pe, at + 1, 1 - p)

        def take_rows(act, j, jp):
            act.wait_ge(turned, j + 1)
            for c in range(KD):
                step = nc.scalar.activation(unit_T[:, jp, c], TB[:, c], ACT.Copy, scale=vec[:, c:c + 1] if gated else 1.0)
            step.then_inc(turned_in, 1)

        def unit_scalar(act, u, kind, at, p, r, before, ahead, again=None):
            for f in range(FC):
                if gated:
                    after(act, hidden, u * FC + (f - 1))
                else:
                    after(act, down, 2 * u)
                act.wait_ge(full, u * FC + (f + 1))
                if gated:
                    nc.scalar.activation(act_b[:, f % 2, 0:width[kind]], GB(f, kind), ACT.Silu).then_inc(silued, 1)
                else:
                    nc.scalar.activation(hid[:, p, f, 0:width[kind]], GB(f, kind), ACT.Silu).then_inc(hidden, 1)
                if f == 1 and ahead == "list":
                    take_rows(act, at + 1, 1 - p)

        def unit_vector(dve, u, kind, at, p, r, before, ahead, again=None):
            for f in range(FC):
                if gated:
                    if f == 0:
                        after(dve, down, 2 * u)
                    dve.wait_ge(silued, u * FC + (f + 1))
                    nc.vector.tensor_tensor(hid[:, p, f, 0:width[kind]], act_b[:, f % 2, 0:width[kind]], UB(f, kind), ALU.mult).then_inc(hidden, 1)
                if f == 0 and before is not None:
                    output_vector(dve, u - 1, *before)
                if kind == "shared" and again is None and (f == 1 or f == 3 and ahead):
                    stage_group(dve, u + f // 2, 1 - f // 2)
                if again and f % 2 == 0:
                    collect_group(dve, again - 1, f // 2)

        def output_vector(dve, v, kind, at, p, r):
            if kind == "list":
                turns = 16 * (at // 2) if isinstance(at, int) else 8 * (at - p)
                dve.wait_ge(y_out[p], turns + 16)
            for h in range(2):
                dve.wait_ge(down, 2 * v + (h + 3))
                o = DB(h, kind)
                if kind == "shared":
                    step = nc.vector.tensor_tensor(X[:, at, 2 * h:2 * h + 2], X[:, at, 2 * h:2 * h + 2], o, ALU.add)
                else:
                    step = nc.vector.tensor_copy(y_rows[:, p, h:h + 1], o)
                step.then_inc(taken, 1)

        def run(eng, unit, output, first_rows):
            SHR = lambda g, gp: ("shared", g, gp, 0)
            LST = lambda j, jp: ("list", j, jp, ring_of(jp))
            if SHN:
                unit(eng, 0, *SHR(0, 0), None, "shared")
                with eng.Fori(0, SHN // 2 - 1) as pair:
                    unit(eng, 2 * pair + 1, *SHR(2 * pair + 1, 1), SHR(2 * pair, 0), "shared")
                    unit(eng, 2 * pair + 2, *SHR(2 * pair + 2, 0), SHR(2 * pair + 1, 1), "shared")
                unit(eng, SHN - 1, *SHR(SHN - 1, 1), SHR(SHN - 2, 0), None)
            first_rows(eng, 0, 0)
            unit(eng, SHN, *LST(0, 0), SHR(SHN - 1, 1) if SHN else None, "list")
            with eng.Fori(0, (UNITS - 3) // 2) as pair:
                j = 2 * pair + 1
                unit(eng, j + SHN, *LST(j, 1), LST(j - 1, 0), "list")
                unit(eng, j + (SHN + 1), *LST(j + 1, 0), LST(j, 1), "list")
            unit(eng, SHN + UNITS - 2, *LST(UNITS - 2, 1), LST(UNITS - 3, 0), "list")
            unit(eng, SHN + UNITS - 1, *LST(UNITS - 1, 0), LST(UNITS - 2, 1), None)
            before = LST(UNITS - 1, 0)
            for g in range(SHN, NG if SHN else 0):
                now = SHR(g, 1 - g % 2)
                unit(eng, UNITS + g, *now, before, None, again=g - SHN)
                before = now
            output(eng, (UNITS + NG if SHN else UNITS) - 1, *before)

        def load_rows(sp, j, jp):
            after(sp, turned, j - 1)
            sp.dma_start(unit_rows[:, jp], list_units[:, j]).then_inc(row_in[jp], 16)

        def load_weights(sp, j, r, expert, at_part):
            u = j + SHN
            if at_part == 0:
                after(sp, full, FC * (u - 1))
                sp.dma_start(w[:, r, 0:UPS], ins[f"{tag}_w"][expert][:, 0:UPS]).then_inc(w_gu[r], 16)
            else:
                sp.wait_ge(down, 2 * u)
                sp.dma_start(w[:, r, UPS:], ins[f"{tag}_w"][expert][:, UPS:]).then_inc(w_dn[r], 16)

        def store_out(sp, j, jp):
            sp.wait_ge(taken, 2 * (j + SHN) + 4)
            sp.dma_start(out_units[:, j], y_rows[:, jp]).then_inc(y_out[jp], 16)

        def expert_of(sp, j):
            return sp.value_load(expert_i[:].unsqueeze(2)[0:1, j], min_val=0, max_val=E - 1)

        def sync(sp):
            for dst, name in ((wr, "wr"), (vec, "v"), (const, "const")):
                sp.dma_start(dst[:], ins[f"{tag}_{name}"]).then_inc(loaded, 16)
            if SHN:
                sp.dma_start(w[:, 0, 0:UPS], ins[f"{tag}_w"][E][:, 0:UPS]).then_inc(w_gu[0], 16)
                sp.dma_start(w[:, 0, UPS:], ins[f"{tag}_w"][E][:, UPS:]).then_inc(w_dn[0], 16)
            sp.wait_ge(placed, 1)
            e = expert_of(sp, 0)
            for sems, lo, hi in ((w_gu, 0, UPS), (w_dn, UPS, WN)):
                sp.dma_start(w[:, ring_of(0), lo:hi], ins[f"{tag}_w"][e][:, lo:hi]).then_inc(sems[ring_of(0)], 16)
            for p in range(2):
                sp.wait_ge(in_list[p], 16 * 2 * GS * (NG // 2))
            load_rows(sp, 0, 0)

            def step(j, jp, store=True):
                load_rows(sp, j + 1, 1 - jp)
                e = expert_of(sp, j + 1)
                load_weights(sp, j + 1, ring_of(1 - jp), e, 0)
                load_weights(sp, j + 1, ring_of(1 - jp), e, 1)
                if store:
                    store_out(sp, j - 1, 1 - jp)

            step(0, 0, False)
            with sp.Fori(0, (UNITS - 3) // 2) as pair:
                step(2 * pair + 1, 1)
                step(2 * pair + 2, 0)
            step(UNITS - 2, 1)
            if SHN:
                load_weights(sp, UNITS, 0, E, 0)
                load_weights(sp, UNITS, 0, E, 1)
            store_out(sp, UNITS - 2, 1)
            store_out(sp, UNITS - 1, 0)
            if result is not None:
                for g in range(NG):
                    sp.wait_ge(combined, g + 3)
                    sp.dma_start(result[g * GS:g * GS + GS].rearrange("s t d -> t s d"), X[:, g]).then_inc(stored, 16)
                sp.wait_ge(stored, 16 * NG)

        def tensor(pe):
            pe.wait_ge(loaded, 48)
            rows["tensor"](pe)
            router_tensor(pe)
            rank_tensor(pe)
            if SHN:
                pe.wait_ge(w_gu[0], 16)
                pe.wait_ge(w_dn[0], 16)
            run(pe, unit_tensor, output_tensor, turn_rows)

        def scalar(act):
            rows["scalar"](act)
            router_scalar(act)
            run(act, unit_scalar, lambda *a: None, take_rows)

        def vector(dve):
            dve.wait_ge(loaded, 48)
            nc.vector.memset(ones[:], 1.0)
            dve.sem_inc(logit_in, 2)
            dve.sem_inc(taken, 2)
            dve.sem_inc(down, 2)
            dve.sem_inc(combined, 2)
            for p in range(2):
                dve.sem_inc(y_out[p], 16)
            rows["vector"](dve)
            router_vector(dve)
            stage_vector(dve)
            run(dve, unit_vector, output_vector, lambda *a: None)
            if not gated:
                dve.wait_ge(taken, 2 * UNITS + 2)
            collect_vector(dve)
            dve.wait_ge(combined, NG + 2)

        def pool(pl):
            rows["pool"](pl)
            to_list_pool(pl)
            collect_pool(pl)

        mem.end()
        return dict(sync=sync, tensor=tensor, scalar=scalar, vector=vector, pool=pool)

    h_mem = Stage(nc, ())
    H = h_mem.take("H", [128, NG, GS, D])
    z_mem = Stage(nc, ())
    zeros = z_mem.take("zeros", [128, UR // 128, D])

    b_attn = attention("b", 1, ["ctx"], relu=True)
    c_attn = attention("c", 0, ["x"], rms=True, out_w=True)
    z_mem.end()
    experts0 = experts("d", 1, H, True, rows_by_expert, out_by_expert, listed)
    h_mem.end()
    recur = recurrence("r", 0)
    e_attn = attention("e", 1, ["x", "ctx"], out_w=True)
    experts1 = experts("f", 0, X, False, rows_by_expert, out_by_expert, listed, out)

    stages = [b_attn, c_attn, experts0, recur, e_attn, experts1]

    def pass_stage(eng, n):
        eng.drain().then_inc(passed[n], 1)
        eng.wait_ge(passed[n], 5)
        after(eng, cleared, n)
        eng.drain()

    block = ctx.enter_context(nc.Block())

    @block.sync
    def _(sp):
        sp.dma_start(ident[:], ins["ident"]).then_inc(setup, 16)
        for t, name in ((m_w_sb, "m_w"), (m_v_sb, "m_v"), (b_bc, "m_bbc"), (m_rows, "m_rows"), (selector, "m_sel")):
            sp.dma_start(t[:], ins[name]).then_inc(m_loaded, 16)
        for g in range(NG):
            sp.dma_start(X[:, g], ins["x"][g * GS:g * GS + GS].rearrange("s t d -> t s d")).then_inc(x_first[g] if g < 2 else x_rest, 16)
        for n, st in enumerate(stages):
            sp.sem_inc(passed[n], 1)
            sp.wait_ge(passed[n], 5)
            after(sp, cleared, n)
            sp.drain()
            st["sync"](sp)
            if n == 0:
                sp.wait_ge(zeroed, 1)
                with sp.Fori(0, UNITS) as u:
                    sp.dma_start(rows_by_expert.rearrange("(u r p) d -> p u r d", p=128, r=UR // 128)[:, u], zeros[:]).then_inc(listed, 16)

    @block.gpsimd
    def _(pool):
        nc.gpsimd.memset(eps[:], EPS)
        nc.gpsimd.memset(rms_eps[:], RMS_EPS)
        nc.gpsimd.memset(minus_one[:], -1.0)
        nc.gpsimd.memset(neg_half[:], -0.5).then_inc(setup, 1)
        mamba_setup_pool(pool)
        pool.wait_ge(setup, 17)
        mamba(pool, mamba_early_pool, mamba_late_pool, mamba_scan_pool, mamba_back_pool)
        for n, st in enumerate(stages):
            pass_stage(pool, n)
            pool.sem_clear(sem_set[n % 2])
            pool.drain().then_inc(cleared, 1)
            if n == 0:
                nc.gpsimd.memset(zeros[:], 0.0).then_inc(zeroed, 1)
            st["pool"](pool)

    @block.scalar
    def _(act):
        mamba_setup_scalar(act)
        act.wait_ge(m_half, 1)
        act.wait_ge(m_prep, 2)
        act.wait_ge(m_edge, 2)
        mamba(act, mamba_early_scalar, mamba_late_scalar, mamba_scan_scalar, mamba_back_scalar)
        for n, st in enumerate(stages):
            pass_stage(act, n)
            st["scalar"](act)

    @block.vector
    def _(dve):
        mamba_setup_vector(dve)
        mamba(dve, mamba_early_vector, mamba_late_vector, mamba_scan_vector, mamba_back_vector)
        for n, st in enumerate(stages):
            pass_stage(dve, n)
            st["vector"](dve)

    @block.tensor
    def _(pe):
        pe.wait_ge(setup, 17)
        pe.wait_ge(m_loaded, 16 * 5)
        pe.wait_ge(m_skip, KD)
        mamba(pe, mamba_early_tensor, mamba_late_tensor, mamba_scan_tensor, mamba_back_tensor)
        for n, st in enumerate(stages):
            pass_stage(pe, n)
            st["tensor"](pe)

    ctx.close()


def kernel(**inputs):
    import ml_dtypes
    import concourse.bacc as bacc
    from concourse.bass_utils import run_bass_kernel_spmd as run

    a = {k: np.asarray(v) for k, v in inputs.items()}
    seqs_n = a["x"].shape[0]

    def rows_in(w):
        k = w.shape[0] // 128
        return w.reshape(k, 128, w.shape[1]).transpose(1, 0, 2).reshape(128, -1)

    def per_row(v):
        return v.reshape(v.shape[0] // 128, 128, -1).transpose(1, 0, 2).reshape(128, -1)

    def to_all(v):
        return np.broadcast_to(v.reshape(1, -1), (128, v.size))

    m = {k[8:]: v for k, v in a.items() if k.startswith("L0_attn_")}
    bc3 = np.concatenate([m["bc_w"].T] * 3, axis=1)
    selector = np.zeros((96, 32, 128), ml_dtypes.bfloat16)
    for n in range(32):
        selector[n::32, n] = 1
    arrays = {
        "x": a["x"],
        "ident": np.eye(128, dtype=np.float32),
        "m_w": np.concatenate([rows_in(m["in_proj_w"].T), rows_in(m["dt_w"].T), rows_in(m["out_w"].T), rows_in(bc3)], 1),
        "m_v": np.concatenate([per_row(m["in_proj_b"]), per_row(m["conv_w"][:, 0]), per_row(m["conv_b"]),
                               per_row(m["dt_b"]), per_row(m["A_log"]), per_row(m["D"])], 1),
        "m_bbc": np.concatenate([m["bc_b"]] * 3).reshape(96, 1),
        "m_rows": np.stack([to_all(m["out_b"]), to_all(m["ln_g"]), to_all(m["ln_b"])], 1),
        "m_sel": selector,
    }
    strip_mask = np.zeros((128, 8), np.float32)
    for e in range(8):
        strip_mask[np.arange(128) // 16 == e, e] = 16 ** -0.5
    groups = seqs_n // GS
    arrays |= {
        "ctxT": a["ctx_1024"].transpose(2, 0, 1).reshape(2, 128, groups, GS * 128).transpose(1, 0, 2, 3),
        "b_wq": rows_in(a["L0_xattn_Wq"].T), "b_wk0": rows_in(a["L0_xattn_Wk"].T), "b_wv0": rows_in(a["L0_xattn_Wv"].T),
        "b_mask": strip_mask,
    }
    f = {k[7:]: v for k, v in a.items() if k.startswith("L0_ffn_")}
    arrays |= {
        "c_wq": rows_in(f["wq"]), "c_wk0": rows_in(f["wk"]), "c_wv0": rows_in(f["wv"]), "c_wo": rows_in(f["wo"]),
        "c_norm": per_row(f["norm1_w"]), "c_mask": strip_mask,
    }
    e = {k[9:]: v for k, v in a.items() if k.startswith("L1_xattn_")}
    wq, wk, wv = np.split(e["Wqkv"], 3, axis=1)
    _, wka, wva = np.split(e["Wqkv_aux"], 3, axis=1)
    bq, bk, bv = np.split(e["bqkv"], 3)
    _, bka, bva = np.split(e["bqkv_aux"], 3)
    arrays |= {
        "e_wq": rows_in(wq), "e_wk0": rows_in(wk), "e_wv0": rows_in(wv), "e_wk1": rows_in(wka), "e_wv1": rows_in(wva),
        "e_wo": rows_in(e["Wo"]), "e_bq": per_row(bq), "e_bk0": per_row(bk), "e_bk1": per_row(bka),
        "e_bv0": per_row(bv), "e_bv1": per_row(bva), "e_gate_f": per_row(np.repeat(e["g"], 16)), "e_bo": to_all(e["bo"]), "e_gate": to_all(e["g"]), "e_mask": strip_mask,
    }
    r = {k[8:]: v for k, v in a.items() if k.startswith("L1_attn_")}
    arrays |= {"r_wi": rows_in(r["Wi"].T), "r_wh": rows_in(r["Wh"].T),
               "r_b": np.concatenate([per_row(r["bi"]), per_row(r["bh"])], 1)}
    experts = lambda parts: np.stack([np.concatenate([rows_in(w[e]) for w in parts], 1) for e in range(8)])
    consts = np.concatenate([np.triu(np.ones((128, 128), np.float32), 1), to_all(np.arange(8, 0, -1, dtype=np.float32)),
                             to_all(np.arange(groups * GT // UR, dtype=np.float32) * UR),
                             to_all(np.arange(units_of_list(groups), dtype=np.float32))], 1)
    shared = np.concatenate([rows_in(f[n]) for n in ("sh_gate", "sh_up", "sh_down")], 1)
    n = {k[7:]: v for k, v in a.items() if k.startswith("L1_ffn_")}
    arrays |= {
        "d_w": np.concatenate([experts([f["e_gate"], f["e_up"], f["e_down"]]), shared[None]]), "d_wr": rows_in(f["router_w"]),
        "d_v": per_row(f["norm2_w"]), "d_const": consts,
        "f_w": experts([n["w1"].transpose(0, 2, 1), n["w2"].transpose(0, 2, 1)]), "f_wr": rows_in(n["gate_w"].T),
        "f_v": to_all(n["balance_bias"]), "f_const": consts,
    }
    nc = bacc.Bacc("TRN2", target_bir_lowering=False, num_devices=1)
    fed, ins = {}, {}
    for name, v in arrays.items():
        v = np.ascontiguousarray(v)
        fed[f"in_{name}"] = v
        ins[name] = nc.dram_tensor(f"in_{name}", v.shape, mybir.dt.from_np(v.dtype), kind="ExternalInput").ap()
    out = nc.dram_tensor("out_0", a["x"].shape, F32, kind="ExternalOutput").ap()
    decoder_kernel(nc, ins, out)
    r = run(nc, [fed], core_ids=[0])
    return r.results[0]["out_0"]
```
